# Optimizing a Trainium2 kernel written in Bass

```python
import numpy as np
import jax
import jax.numpy as jnp

def _softmax(x, axis=-1):
    return jax.nn.softmax(x, axis=axis)

def _gelu(x):
    return jax.nn.gelu(x, approximate=True)

def _silu(x):
    return jax.nn.silu(x)

def _sigmoid(x):
    return jax.nn.sigmoid(x)

def _layernorm(x, axis=-1, eps=1e-05):
    m = jnp.mean(x, axis=axis, keepdims=True)
    v = jnp.var(x, axis=axis, keepdims=True)
    return (x - m) / jnp.sqrt(v + eps)

def _scatter_add(tgt, idx, src, axis=0):
    return tgt.at[idx].add(src)

def _segment_sum(src, seg, n):
    return jax.ops.segment_sum(src, seg, n)
kernel_name = 'mk_decoder_preln_d1_seqx_r8_6ad89b'

def setup_inputs(seed: int=0):
    np.random.seed(seed)
    _w = jnp.asarray

    def _rec_inputs():
        import jax
        import jax.numpy as jnp
        _rk = jax.random.key(seed)
        x = 0.000341 + 1 * jax.random.normal(jax.random.fold_in(_rk, 1), (16, 128, 256), jnp.float32)
        _lenS = 128 - jax.random.randint(jax.random.fold_in(_rk, 7), (16,), 0, max(1, 128 // 4) + 1, jnp.int32)
        _lenS2 = 128 - jax.random.randint(jax.random.fold_in(_rk, 8), (16,), 0, max(1, 128 // 4) + 1, jnp.int32)
        _ctx_2048P = jax.random.normal(jax.random.fold_in(_rk, 11), (16, 16, 256), jnp.float32)
        _ctx_2048c = jax.random.dirichlet(jax.random.fold_in(_rk, 511), 0.3 * jnp.ones((16,), jnp.float32), (16, 128))
        _ctx_2048t = jnp.einsum('bsk,bkd->bsd', _ctx_2048c, _ctx_2048P)
        _ctx_2048t = _ctx_2048t * jax.lax.rsqrt(jnp.mean(jnp.square(_ctx_2048t)) + 1e-12) * 0.953939
        ctx_2048 = -1.47943e-05 + 1.00017 * (_ctx_2048t + 0.3 * jax.random.normal(jax.random.fold_in(_rk, 611), (16, 128, 256), jnp.float32))
        return (x, ctx_2048)
    x, ctx_2048 = _rec_inputs()

    def _L0_attn_setup():
        import jax, jax.numpy as jnp
        import numpy as np
        HID = 256
        NH = 32
        QLR = 192
        KVLR = 64
        DR = 64
        DN = 128
        DV = 128
        DQK = DN + DR
        EPS = 1e-06
        ROPE_BASE = 10000.0

        def rms_norm(x, w):
            return x * jax.lax.rsqrt(jnp.mean(x * x, axis=-1, keepdims=True) + EPS) * w

        def apply_rope(x, pos):
            d = x.shape[-1]
            inv_freq = 1.0 / ROPE_BASE ** (jnp.arange(0, d, 2, dtype=jnp.float32) / d)
            freqs = pos[:, None].astype(jnp.float32) * inv_freq
            cos = jnp.cos(freqs)[None, :, None, :]
            sin = jnp.sin(freqs)[None, :, None, :]
            x1, x2 = (x[..., :d // 2], x[..., d // 2:])
            return jnp.concatenate([x1 * cos - x2 * sin, x1 * sin + x2 * cos], axis=-1)
        key = jax.random.key(seed)
        ks = jax.random.split(key, 8)
        s = 0.02
        return {'hidden_states': jax.random.normal(ks[0], (1, 256, HID), jnp.float32), 'q_a_w': jax.random.normal(ks[1], (HID, QLR), jnp.float32) * s, 'q_a_ln_w': jnp.ones((QLR,), jnp.float32), 'q_b_w': jax.random.normal(ks[2], (QLR, NH * DQK), jnp.float32) * s, 'kv_a_w': jax.random.normal(ks[3], (HID, KVLR + DR), jnp.float32) * s, 'kv_a_ln_w': jnp.ones((KVLR,), jnp.float32), 'kv_b_w': jax.random.normal(ks[4], (KVLR, NH * (DN + DV)), jnp.float32) * s, 'o_w': jax.random.normal(ks[5], (NH * DV, HID), jnp.float32) * s}
    _L0_attn_all = _L0_attn_setup()
    _L0_attn_in = {k: v for k, v in _L0_attn_all.items() if k in ('q_a_w', 'q_a_ln_w', 'q_b_w', 'kv_a_w', 'kv_a_ln_w', 'kv_b_w', 'o_w')}
    del _L0_attn_all

    def _L0_xattn_setup():
        import jax, jax.numpy as jnp
        import numpy as np

        def _wkv(time_decay, time_first, k, v):
            w = -jnp.exp(time_decay)
            u = time_first
            B, T, C = k.shape
            aa = jnp.zeros((B, C), dtype=k.dtype)
            bb = jnp.zeros((B, C), dtype=k.dtype)
            pp = jnp.full((B, C), -1e+38, dtype=k.dtype)

            def step(carry, kv_t):
                aa, bb, pp = carry
                kt, vt = kv_t
                ww = u + kt
                q = jnp.maximum(pp, ww)
                e1 = jnp.exp(pp - q)
                e2 = jnp.exp(ww - q)
                y_t = (e1 * aa + e2 * vt) / (e1 * bb + e2)
                ww2 = pp + w
                q2 = jnp.maximum(ww2, kt)
                e1b = jnp.exp(ww2 - q2)
                e2b = jnp.exp(kt - q2)
                new_carry = (e1b * aa + e2b * vt, e1b * bb + e2b, q2)
                return (new_carry, y_t)
            ks = jnp.transpose(k, (1, 0, 2))
            vs = jnp.transpose(v, (1, 0, 2))
            _, ys = jax.lax.scan(step, (aa, bb, pp), (ks, vs))
            return jnp.transpose(ys, (1, 0, 2))
        key = jax.random.key(seed)
        k1, k2, k3, k4 = jax.random.split(key, 4)
        B, T, C = (8, 128, 256)
        return {'batch_size': B, 'seq_len': T, 'embedding_dim': C, 'time_decay': jax.random.normal(k1, (C,), dtype=jnp.float32), 'time_first': jax.random.normal(k2, (C,), dtype=jnp.float32), 'k': jax.random.normal(k3, (B, T, C), dtype=jnp.float32), 'v': jax.random.normal(k4, (B, T, C), dtype=jnp.float32)}
    _L0_xattn_all = _L0_xattn_setup()
    _L0_xattn_in = {k: v for k, v in _L0_xattn_all.items() if k in ('time_decay', 'time_first')}
    del _L0_xattn_all

    def _L0_ffn_setup():
        import jax, jax.numpy as jnp
        import numpy as np
        B, S, H = (2, 128, 256)
        E, K = (8, 2)
        F = 176
        FS = 704
        NORM_TOPK = False

        def _swiglu(x, wg, wu, wd):
            return jax.nn.silu(x @ wg) * (x @ wu) @ wd
        key = jax.random.key(seed)
        ks = jax.random.split(key, 9)
        s = 0.02
        return {'hidden_states': jax.random.normal(ks[0], (B, S, H), dtype=jnp.float32), 'Wr': jax.random.normal(ks[1], (H, E), dtype=jnp.float32) * s, 'Wg': jax.random.normal(ks[2], (E, H, F), dtype=jnp.float32) * s, 'Wu': jax.random.normal(ks[3], (E, H, F), dtype=jnp.float32) * s, 'Wd': jax.random.normal(ks[4], (E, F, H), dtype=jnp.float32) * s, 'Sg': jax.random.normal(ks[5], (H, FS), dtype=jnp.float32) * s, 'Su': jax.random.normal(ks[6], (H, FS), dtype=jnp.float32) * s, 'Sd': jax.random.normal(ks[7], (FS, H), dtype=jnp.float32) * s, 'Wsg': jax.random.normal(ks[8], (H, 1), dtype=jnp.float32) * s}
    _L0_ffn_all = _L0_ffn_setup()
    _L0_ffn_in = {k: v for k, v in _L0_ffn_all.items() if k in ('Wr', 'Wg', 'Wu', 'Wd', 'Sg', 'Su', 'Sd', 'Wsg')}
    del _L0_ffn_all
    return {'x': x, 'ctx_2048': ctx_2048, 'L0_attn_q_a_w': _L0_attn_in['q_a_w'], 'L0_attn_q_a_ln_w': _L0_attn_in['q_a_ln_w'], 'L0_attn_q_b_w': _L0_attn_in['q_b_w'], 'L0_attn_kv_a_w': _L0_attn_in['kv_a_w'], 'L0_attn_kv_a_ln_w': _L0_attn_in['kv_a_ln_w'], 'L0_attn_kv_b_w': _L0_attn_in['kv_b_w'], 'L0_attn_o_w': _L0_attn_in['o_w'], 'L0_xattn_time_decay': _L0_xattn_in['time_decay'], 'L0_xattn_time_first': _L0_xattn_in['time_first'], 'L0_ffn_Wr': _L0_ffn_in['Wr'], 'L0_ffn_Wg': _L0_ffn_in['Wg'], 'L0_ffn_Wu': _L0_ffn_in['Wu'], 'L0_ffn_Wd': _L0_ffn_in['Wd'], 'L0_ffn_Sg': _L0_ffn_in['Sg'], 'L0_ffn_Su': _L0_ffn_in['Su'], 'L0_ffn_Sd': _L0_ffn_in['Sd'], 'L0_ffn_Wsg': _L0_ffn_in['Wsg']}

def reference(x, ctx_2048, L0_attn_q_a_w, L0_attn_q_a_ln_w, L0_attn_q_b_w, L0_attn_kv_a_w, L0_attn_kv_a_ln_w, L0_attn_kv_b_w, L0_attn_o_w, L0_xattn_time_decay, L0_xattn_time_first, L0_ffn_Wr, L0_ffn_Wg, L0_ffn_Wu, L0_ffn_Wd, L0_ffn_Sg, L0_ffn_Su, L0_ffn_Sd, L0_ffn_Wsg):
    import jax
    import jax.numpy as jnp

    def _L0_attn_ref(hidden_states, q_a_w, q_a_ln_w, q_b_w, kv_a_w, kv_a_ln_w, kv_b_w, o_w):
        import jax, jax.numpy as jnp
        import numpy as np
        HID = 256
        NH = 32
        QLR = 192
        KVLR = 64
        DR = 64
        DN = 128
        DV = 128
        DQK = DN + DR
        EPS = 1e-06
        ROPE_BASE = 10000.0

        def rms_norm(x, w):
            return x * jax.lax.rsqrt(jnp.mean(x * x, axis=-1, keepdims=True) + EPS) * w

        def apply_rope(x, pos):
            d = x.shape[-1]
            inv_freq = 1.0 / ROPE_BASE ** (jnp.arange(0, d, 2, dtype=jnp.float32) / d)
            freqs = pos[:, None].astype(jnp.float32) * inv_freq
            cos = jnp.cos(freqs)[None, :, None, :]
            sin = jnp.sin(freqs)[None, :, None, :]
            x1, x2 = (x[..., :d // 2], x[..., d // 2:])
            return jnp.concatenate([x1 * cos - x2 * sin, x1 * sin + x2 * cos], axis=-1)
        B, S, _ = hidden_states.shape
        q = rms_norm(hidden_states @ q_a_w, q_a_ln_w) @ q_b_w
        q = q.reshape(B, S, NH, DQK)
        q_pass, q_rot = (q[..., :DN], q[..., DN:])
        ckv = hidden_states @ kv_a_w
        c_kv, k_rot = (ckv[..., :KVLR], ckv[..., KVLR:])
        kv = rms_norm(c_kv, kv_a_ln_w) @ kv_b_w
        kv = kv.reshape(B, S, NH, DN + DV)
        k_pass, v = (kv[..., :DN], kv[..., DN:])
        pos = jnp.arange(S)
        q_rot = apply_rope(q_rot, pos)
        k_rot = apply_rope(k_rot[:, :, None, :], pos)[:, :, 0, :]
        scale = DQK ** (-0.5)
        scores = (jnp.einsum('bqhd,bkhd->bhqk', q_pass, k_pass) + jnp.einsum('bqhd,bkd->bhqk', q_rot, k_rot)) * scale
        causal = jnp.tril(jnp.ones((S, S), dtype=bool))
        scores = jnp.where(causal[None, None], scores, jnp.finfo(scores.dtype).min)
        p = jax.nn.softmax(scores, axis=-1)
        out = jnp.einsum('bhqk,bkhd->bqhd', p, v).reshape(B, S, NH * DV)
        return out @ o_w

    def _L0_xattn_ref(batch_size, seq_len, embedding_dim, time_decay, time_first, k, v):
        import jax, jax.numpy as jnp
        import numpy as np

        def _wkv(time_decay, time_first, k, v):
            w = -jnp.exp(time_decay)
            u = time_first
            B, T, C = k.shape
            aa = jnp.zeros((B, C), dtype=k.dtype)
            bb = jnp.zeros((B, C), dtype=k.dtype)
            pp = jnp.full((B, C), -1e+38, dtype=k.dtype)

            def step(carry, kv_t):
                aa, bb, pp = carry
                kt, vt = kv_t
                ww = u + kt
                q = jnp.maximum(pp, ww)
                e1 = jnp.exp(pp - q)
                e2 = jnp.exp(ww - q)
                y_t = (e1 * aa + e2 * vt) / (e1 * bb + e2)
                ww2 = pp + w
                q2 = jnp.maximum(ww2, kt)
                e1b = jnp.exp(ww2 - q2)
                e2b = jnp.exp(kt - q2)
                new_carry = (e1b * aa + e2b * vt, e1b * bb + e2b, q2)
                return (new_carry, y_t)
            ks = jnp.transpose(k, (1, 0, 2))
            vs = jnp.transpose(v, (1, 0, 2))
            _, ys = jax.lax.scan(step, (aa, bb, pp), (ks, vs))
            return jnp.transpose(ys, (1, 0, 2))
        assert seq_len <= 128
        return _wkv(time_decay, time_first, k, v)

    def _L0_ffn_ref(hidden_states, Wr, Wg, Wu, Wd, Sg, Su, Sd, Wsg):
        import jax, jax.numpy as jnp
        import numpy as np
        B, S, H = (2, 128, 256)
        E, K = (8, 2)
        F = 176
        FS = 704
        NORM_TOPK = False

        def _swiglu(x, wg, wu, wd):
            return jax.nn.silu(x @ wg) * (x @ wu) @ wd
        b, s, h = hidden_states.shape
        x = hidden_states.reshape(-1, h)
        router_logits = x @ Wr
        probs = jax.nn.softmax(router_logits.astype(jnp.float32), axis=-1)
        routing_weights, selected = jax.lax.top_k(probs, K)
        if NORM_TOPK:
            routing_weights = routing_weights / routing_weights.sum(-1, keepdims=True)
        routing_weights = routing_weights.astype(x.dtype)
        C = jnp.einsum('tk,tke->te', routing_weights, jax.nn.one_hot(selected, E, dtype=x.dtype))
        expert_out = jax.vmap(lambda wg, wu, wd: _swiglu(x, wg, wu, wd))(Wg, Wu, Wd)
        moe_out = jnp.einsum('te,eth->th', C, expert_out)
        shared = _swiglu(x, Sg, Su, Sd)
        shared = jax.nn.sigmoid(x @ Wsg) * shared
        out = (moe_out + shared).reshape(b, s, h)
        return out
    x = x + _L0_attn_ref(_layernorm(x, axis=-1), L0_attn_q_a_w, L0_attn_q_a_ln_w, L0_attn_q_b_w, L0_attn_kv_a_w, L0_attn_kv_a_ln_w, L0_attn_kv_b_w, L0_attn_o_w)
    x = x + _L0_xattn_ref(16, 128, 256, L0_xattn_time_decay, L0_xattn_time_first, _layernorm(x, axis=-1), ctx_2048)
    x = x + _L0_ffn_ref(_layernorm(x, axis=-1), L0_ffn_Wr, L0_ffn_Wg, L0_ffn_Wu, L0_ffn_Wd, L0_ffn_Sg, L0_ffn_Su, L0_ffn_Sd, L0_ffn_Wsg)
    return x

_drawn_inputs = setup_inputs


def setup_inputs(seed=0):
    import zlib

    import numpy as np

    out = dict(_drawn_inputs(seed))
    spreads = {'L0_attn_q_a_ln_w': (1.0, 0.6), 'L0_attn_kv_a_ln_w': (1.0, 0.6)}
    factors = {'L0_attn_q_a_w': 8.0,
     'L0_attn_q_b_w': 8.0,
     'L0_ffn_Wr': 8.0,
     'L0_ffn_Wg': 8.0,
     'L0_ffn_Wu': 8.0,
     'L0_ffn_Wd': 8.0,
     'L0_ffn_Sg': 5.137,
     'L0_ffn_Su': 5.086,
     'L0_ffn_Sd': 5.099,
     'L0_ffn_Wsg': 8.0}
    for name, (base, spread) in spreads.items():
        noise = np.random.default_rng([zlib.crc32(name.encode()), seed]).standard_normal(out[name].shape)
        drawn = base * np.exp(spread * noise) if base else spread * noise
        out[name] = jnp.asarray(drawn.astype(out[name].dtype))
    for name, factor in factors.items():
        out[name] = (out[name] * factor).astype(out[name].dtype)
    return out
```

```python
import concourse.bass as bass
from concourse import mybir
from contextlib import ExitStack, contextmanager
import numpy as np

F32 = mybir.dt.float32
F32R = mybir.dt.float32r
BF16 = mybir.dt.bfloat16
ALU = mybir.AluOpType
ACT = mybir.ActivationFunctionType
AX = mybir.AxisListType

B, S, D = 16, 128, 256
TOK = B * S
KT = D // 128
CH = 512
NCH = TOK // CH
BC = CH // S
NH, QLR, KVLR, DR, DN, DV = 32, 192, 64, 64, 128, 128
QR2 = QLR - 128
HG = 4
NG = NH // HG
NP = HG // 2
QUADS = NCH * BC
SCALE = float(DN + DR) ** -0.5
E, TOPK, FE, FS = 8, 2, 176, 704
FF = E * FE + FS
FT = -(-FF // 128)
NR = E + 1
NEG = -1e38
SEG = S + 1
LN_EPS, RMS_EPS = 1e-5, 1e-6
WT = 256
WB = WT // S
NW = TOK // WT
WAVES = CH // WT
SEGS = KT * WB
PARTS = 17
LINKS = 21
MCOL = 128 + 2 * QR2 + KVLR + 2 * DR
VCOL = KVLR + D
LEAD = 6
MW_SLOTS = (6, 7, 8, 10)
WO_SLOTS = (2, 3)
PIECE = 2 * FF // 4
PIECES = ([("gu", k, a, PIECE, 128) for k in range(KT) for a in range(0, 2 * FF, PIECE)]
          + [("d", 0, a, 4, 128) for a in range(0, FT - 1, 4)] + [("d", 0, FT - 1, 1, FF - 128 * (FT - 1))])


def fw(f):
    return min(128, FF - 128 * f)


class Linked:

    def __init__(self, eng, sem):
        self.eng, self.sem, self.base, self.made = eng, sem, 0, 0

    def start(self, base):
        self.base, self.made = base, 0

    def link(self, result):
        result.then_inc(self.sem, 1)
        self.made += 1
        self.eng.wait_ge(self.sem, self.base + self.made)


def decoder_program(nc, xT_d, ctx_d, td_d, tf_d, qaw_d, qaln_d, kvw_d, kvln_d, head_d, wr_d,
                    wgu_d, wd_d, rope_d, mask_d, ident_d, low_d, sel_d, out_d):
    stack = ExitStack()
    with stack:
        def sem(name):
            return stack.enter_context(nc.semaphore(name))

        def sb(ctx, name, shape, dt=F32):
            return ctx.enter_context(nc.sbuf_tensor(name, shape, dt))

        x = sb(stack, "x", [128, KT, TOK])
        ident = sb(stack, "ident", [128, 128])
        mean_w = sb(stack, "mean_w", [128, 128])
        power = sb(stack, "power", [128, WB])
        td = sb(stack, "td", [128, KT])
        tf = sb(stack, "tf", [128, KT])
        wr = sb(stack, "wr", [128, KT, NR])
        low = sb(stack, "low", [128, E, E])
        ps = stack.enter_context(nc.psum_tensor("ps", [128, 8, CH], F32))
        xw = sb(stack, "xw", [128, KT, WT])
        sqw = sb(stack, "sqw", [128, KT, WT])
        stat = sb(stack, "stat", [128, WB])
        rinv = sb(stack, "rinv", [128, WB])
        v = sb(stack, "v", [128, SEGS, S])
        wdec = sb(stack, "wdec", [128, SEGS, SEG])
        kp, pp, e1b, e2b, g, aa, bb = (sb(stack, n, [128, SEGS, SEG]) for n in
                                       ("kp", "pp", "e1b", "e2b", "g", "aa", "bb"))
        qq, e1, e2 = (sb(stack, n, [128, SEGS, S]) for n in ("qq", "e1", "e2"))
        lg = sb(stack, "lg", [128, WB, NR])
        pr = sb(stack, "pr", [128, WB, E])
        rt = sb(stack, "rt", [128, 2, WB])
        gt, eq = (sb(stack, n, [128, WB, E, E]) for n in ("gt", "eq"))
        rank = sb(stack, "rank", [128, WB, E])
        cw = sb(stack, "cw", [128, WB, NR])
        cwp = sb(stack, "cwp", [128, WB, 2 * NR], F32R)

        att = ExitStack()
        maskf = sb(att, "maskf", [128, S])
        maskb = sb(att, "maskb", [128, S], BF16)
        identb = sb(att, "identb", [128, 128], BF16)
        meanq_w = sb(att, "meanq_w", [128, 128])
        meankv_w = sb(att, "meankv_w", [KVLR, KVLR])
        eps = sb(att, "eps", [128, 2])
        rope = sb(att, "rope", [128, 4, S])
        qaw = sb(att, "qaw", [128, KT, 128 + 2 * QR2])
        kvw = sb(att, "kvw", [128, KT, 256])
        lnw = sb(att, "lnw", [128, 3])
        qn1h = sb(att, "qn1h", [128, TOK], F32R)
        qn1l = sb(att, "qn1l", [128, TOK], F32R)
        qn2 = sb(att, "qn2", [128, TOK], F32R)
        ka = sb(att, "ka", [128, TOK])
        ckv = sb(att, "ckv", [128, B, KVLR + 1])
        xc = sb(att, "xc", [128, KT, TOK])
        sq = sb(att, "sq", [128, KT, TOK])
        sd = sb(att, "sd", [128, TOK])
        rs = sb(att, "rs", [128, CH])
        pt1 = sb(att, "pt1", [128, CH])
        raw_m = sb(att, "raw_m", [128, HG, MCOL])
        raw_v = sb(att, "raw_v", [128, HG, VCOL])
        mwh = sb(att, "mwh", [128, HG, 2, 128], F32R)
        mwl = sb(att, "mwl", [128, HG, 2, 128], F32R)
        woh = sb(att, "woh", [128, NP, D], F32R)
        wol = sb(att, "wol", [128, NP, D], F32R)
        qa = sb(att, "qa", [128, 2, HG, CH])
        qs = sb(att, "qs", [128, CH])
        qu = sb(att, "qu", [128, CH])
        nmax = sb(att, "nmax", [128, 2, HG])
        p = sb(att, "p", [128, 2, HG, S])
        pT = sb(att, "pT", [128, HG, S])
        rsum = sb(att, "rsum", [128, HG])
        o = sb(att, "o", [128, HG, KVLR])
        oTh = sb(att, "oTh", [128, 2, NP, CH], F32R)
        oTl = sb(att, "oTl", [128, 2, NP, CH], F32R)
        att.close()

        ffn = ExitStack()
        wguh = sb(ffn, "wguh", [128, KT, 2 * FF], F32R)
        wgul = sb(ffn, "wgul", [128, KT, 2 * FF], F32R)
        wdh = sb(ffn, "wdh", [128, FT, D], F32R)
        wdl = sb(ffn, "wdl", [128, FT, D], F32R)
        sel = sb(ffn, "sel", [2 * NR, FT * 128], F32R)
        hh = sb(ffn, "hh", [128, KT, 2 * CH], F32R)
        hl = sb(ffn, "hl", [128, KT, 2 * CH], F32R)
        cT = sb(ffn, "cT", [2 * NR, 2 * CH], F32R)
        staging = ExitStack()
        stage = sb(staging, "stage", [128, 2, PIECE])
        selraw = sb(staging, "selraw", [2 * NR, FT * 128])
        staging.close()
        act_s = sb(ffn, "act_s", [128, 2, CH])
        act_t = sb(ffn, "act_t", [128, 2, CH])
        acth = sb(ffn, "acth", [128, 3, CH], F32R)
        actl = sb(ffn, "actl", [128, 3, CH], F32R)
        ffn.close()

        x_in = [sem(f"x_in{t}") for t in range(NCH)]
        w_in, const_in, raw_m_in, raw_v_in, v_in, sel_in, out_done = (sem(n) for n in (
            "w_in", "const_in", "raw_m_in", "raw_v_in", "v_in", "sel_in", "out_done"))
        stage_in = [sem("stage_in0"), sem("stage_in1")]
        const_set = sem("const_set")
        cast_set = sem("cast_set")
        pmean_done, pxc_done, psq_done, pvar_done, psd_done, pxn_done = (sem(n) for n in (
            "pmean_done", "pxc_done", "psq_done", "pvar_done", "psd_done", "pxn_done"))
        qproj_done, qsq_done, qsum_done, qsd_done, qn_done = (sem(n) for n in (
            "qproj_done", "qsq_done", "qsum_done", "qsd_done", "qn_done"))
        kvproj_done, kvsq_done, kvsum_done, kvsd_done, ckn_done, ckvT_done, ckv_set, keys_done = (
            sem(n) for n in ("kvproj_done", "kvsq_done", "kvsum_done", "kvsd_done", "ckn_done",
                             "ckvT_done", "ckv_set", "keys_done"))
        prep_chain = sem("prep_chain")
        mw_done, mwh_set, mwl_set, rot_set, wo_done, woh_set, wol_set = (sem(n) for n in (
            "mw_done", "mwh_set", "mwl_set", "rot_set", "wo_done", "woh_set", "wol_set"))
        qp_done, qs_set, qu_set, qcos_set, q_set = (sem(n) for n in (
            "qp_done", "qs_set", "qu_set", "qcos_set", "q_set"))
        s_done, max_done, p_done, pT_done, pT_set, pv_done, o_done, oT_done, oTh_set, oTl_set = (
            sem(n) for n in ("s_done", "max_done", "p_done", "pT_done", "pT_set", "pv_done",
                             "o_done", "oT_done", "oTh_set", "oTl_set"))
        rsum_set, y_done, y_added = sem("rsum_set"), sem("y_done"), sem("y_added")
        piece_h, piece_l, sel_set = sem("piece_h"), sem("piece_l"), sem("sel_set")
        decay_exp, wkv_ready = sem("decay_exp"), sem("wkv_ready")
        mean_done, xc_done, sq_done, var_done, stat_set, rinv_set, r_done, xn_done = (sem(n) for n in (
            "mean_done", "xc_done", "sq_done", "var_done", "stat_set", "rinv_set", "r_done", "xn_done"))
        d1_set, d2_set, d3_set, d4_set, e1b_set, e2b_set, e1_set, e2_set, g_set, e2v_set, wkv_done = (
            sem(n) for n in ("d1_set", "d2_set", "d3_set", "d4_set", "e1b_set", "e2b_set",
                             "e1_set", "e2_set", "g_set", "e2v_set", "wkv_done"))
        hh_set, hl_set, logit_done, lmax_set, lexp_set, cw_set, cT_done, cT_set = (sem(n) for n in (
            "hh_set", "hl_set", "logit_done", "lmax_set", "lexp_set", "cw_set", "cT_done", "cT_set"))
        primed = gate_done, up_done, silu_done, mix_done, prod_done, acth_set, actl_set, down_done, z_added = [
            sem(n) for n in ("gate_done", "up_done", "silu_done", "mix_done", "prod_done",
                             "acth_set", "actl_set", "down_done", "z_added")]
        primed_set = sem("primed_set")
        wave_chain = sem("wave_chain")

        S_BANK, PT_BANK, PV_BANK, OT_BANK, Q_BANK, Y_BANK = 0, 2, 3, 4, 5, 6
        WO_BANK, MW_BANK = Y_BANK, Y_BANK + 1
        G_BANK, U_BANK, C_BANK, Z_BANK, W_BANK = 0, 2, 4, 5, 7

        def bank(i):
            return ps[:, i, :]

        def toks(t):
            return bass.ds(t * CH, CH)

        def f32(ap):
            return ap.bitcast(F32)

        def over_b(ap):
            return ap.unsqueeze(1).to_broadcast([ap.shape[0], BC, S])

        def by_b(ap):
            return ap.rearrange("p (b s) -> p b s", s=S)

        def wtoks(w):
            return bass.ds(w * WT, WT)

        def held(w):
            return bass.ds((w % (2 * WAVES)) * WT, WT)

        def over_k(ap):
            return ap.unsqueeze(1).to_broadcast([ap.shape[0], KT, ap.shape[-1]])

        def now(eng, s, value):
            if not (isinstance(value, int) and value <= 0):
                eng.wait_ge(s, value)

        def over_groups(eng, body):
            body(0, True, False)
            with eng.Fori(1, NG - 1) as gi:
                body(gi, False, False)
            body(NG - 1, False, True)

        def wave_part(c, step):
            return WAVES * (c + 1) + step // PARTS, step % PARTS

        def over_chunks(eng, body):
            with eng.Fori(0, NCH - 1) as c:
                body(c, True)
            body(NCH - 1, False)

        def rotated(j):
            return raw_m[:, j, MCOL - 2 * DR:].rearrange("p (a c) -> p a c", a=2)

        def piece(n):
            kind, k, a, w, rows = PIECES[n]
            if kind == "gu":
                return stage[:, n % 2, 0:w], wguh[:, k, a:a + w], wgul[:, k, a:a + w]
            return (stage[0:rows, n % 2, 0:w * D], *(t[0:rows, a:a + w, :].rearrange("p f n -> p (f n)")
                                                     for t in (wdh, wdl)))

        block = stack.enter_context(nc.Block())

        @block.sync
        def _(sp):
            for t in range(NCH):
                sp.dma_start(x[:, :, toks(t)], xT_d[:, :, toks(t)]).then_inc(x_in[t], 16)
            for dst, src in ((qaw[:, :, :], qaw_d), (kvw[:, :, :], kvw_d), (lnw[:, 0:2], qaln_d),
                             (lnw[0:KVLR, 2:3], kvln_d), (rope[:, :, :], rope_d)):
                sp.dma_start(dst, src).then_inc(w_in, 16)
            for dst, src in ((ident[:, :], ident_d), (maskf[:, :], mask_d), (td[:, :], td_d),
                             (tf[:, :], tf_d), (wr[:, :, :], wr_d),
                             (low[:, :, :], low_d)):
                sp.dma_start(dst, src).then_inc(const_in, 16)

            def load_m(gi):
                sp.dma_start(raw_m[:, :, :].rearrange("p a b -> p (a b)"),
                             head_d[bass.ds(gi, 1), :, 0:HG * MCOL].rearrange("a p n -> (a p) n")
                             ).then_inc(raw_m_in, 16)

            def load_v(gi):
                sp.dma_start(raw_v[:, :, :].rearrange("p a b -> p (a b)"),
                             head_d[bass.ds(gi, 1), :, HG * MCOL:].rearrange("a p n -> (a p) n")
                             ).then_inc(raw_v_in, 16)

            load_m(0)
            load_v(0)
            with sp.Fori(1, NG) as gi:
                sp.wait_ge(mw_done, gi * HG)
                sp.wait_ge(rot_set, gi * HG)
                load_m(gi)
                sp.wait_ge(wo_done, gi * NP)
                load_v(gi)

            def load_v_wave(w):
                sp.dma_start(v[:, :, :].rearrange("p (k b) s -> p k (b s)", k=KT), ctx_d[:, :, wtoks(w)]
                             ).then_inc(v_in, 16)

            load_v_wave(0)
            sp.wait_ge(y_added, KT * NG * NCH)
            sp.dma_start(selraw[:, :], sel_d).then_inc(sel_in, 16)
            for n in range(len(PIECES)):
                if n >= 2:
                    sp.wait_ge(piece_l, n - 1)
                kind, k, a, w, rows = PIECES[n]
                if kind == "gu":
                    src, dst = wgu_d[128 * k:128 * k + 128, a:a + w], stage[:, n % 2, 0:w]
                else:
                    src = wd_d[128 * a:128 * a + rows * w, :].rearrange("(f p) n -> p f n", p=rows)
                    dst = stage[0:rows, n % 2, 0:w * D].rearrange("p (f n) -> p f n", n=D)
                sp.dma_start(dst, src).then_inc(stage_in[n % 2], 16)
            for w in range(1, WAVES):
                sp.wait_ge(wkv_done, w)
                load_v_wave(w)
            with sp.Fori(0, NCH - 1) as c:
                for i in range(WAVES):
                    w = WAVES * (c + 1) + i
                    sp.wait_ge(wkv_done, w)
                    load_v_wave(w)
                sp.wait_ge(z_added, KT * (c + 1) + 1)
                sp.dma_start(out_d[:, :, toks(c)], x[:, :, toks(c)]).then_inc(out_done, 16)
            sp.wait_ge(z_added, KT * NCH + 1)
            sp.dma_start(out_d[:, :, toks(NCH - 1)], x[:, :, toks(NCH - 1)]).then_inc(out_done, 16)
            sp.wait_ge(out_done, 16 * NCH)

        @block.gpsimd
        def _(pool):
            for s in primed:
                pool.sem_inc(s, 1)
            pool.memset(mean_w[:, :], 1.0 / D)
            pool.memset(power[:, :], -0.5)
            pool.memset(meanq_w[:, :], 1.0 / QLR)
            pool.memset(meankv_w[:, :], 1.0 / KVLR)
            pool.memset(eps[:, 0:1], LN_EPS)
            pool.memset(eps[:, 1:2], RMS_EPS)
            pool.memset(qs[:, :], 0.0)
            pool.memset(ckv[:, :, :], 1.0).then_inc(const_set, 1)

            def rot_parts(head, j):
                pool.wait_ge(mwh_set, head + 1)
                pool.tensor_tensor(mwl[:, j, :, KVLR:], rotated(j), f32(mwh[:, j, :, KVLR:]), ALU.subtract
                                   ).then_inc(rot_set, 1)

            def times_sine(job):
                pool.wait_ge(qs_set, job + 1)
                now(pool, q_set, job)
                pool.tensor_tensor(by_b(qu[:, :]), by_b(qs[:, :]), over_b(rope[:, 1, :]), ALU.mult
                                   ).then_inc(qu_set, 1)

            for j in range(HG):
                rot_parts(j, j)
            for job in range(LEAD):
                times_sine(job)

            def pool_group(gi, first, last):
                for k in range(QUADS):
                    if k + LEAD < QUADS or not last:
                        times_sine(QUADS * gi + k + LEAD)
                    if k in MW_SLOTS and not last:
                        j = MW_SLOTS.index(k)
                        rot_parts(HG * gi + HG + j, j)

            over_groups(pool, pool_group)

            def inverse_deviation(w, i):
                pool.wait_ge(stat_set, 2 * w + i + 1)
                pool.tensor_tensor(rinv[:, :], stat[:, :], power[:, :], ALU.pow).then_inc(rinv_set, 1)

            def pool_part(w, part):
                if part in (1, 12):
                    inverse_deviation(w, part // 12)
                elif part == 4:
                    pool.wait_ge(v_in, 16 * (w + 1))
                    pool.wait_ge(e2b_set, w + 1)
                    pool.tensor_tensor(g[:, :, 1:], e2b[:, :, 1:], v[:, :, :], ALU.mult).then_inc(g_set, 1)
                elif part == 6:
                    pool.wait_ge(e2_set, w + 1)
                    pool.wait_ge(g_set, w + 1)
                    pool.tensor_tensor(v[:, :, :], e2[:, :, :], v[:, :, :], ALU.mult).then_inc(e2v_set, 1)

            def low_piece(n):
                raw, hi, lo = piece(n)
                pool.wait_ge(piece_h, n + 1)
                pool.tensor_tensor(lo, raw, f32(hi), ALU.subtract).then_inc(piece_l, 1)

            for w in range(WAVES):
                for part in range(PARTS):
                    pool_part(w, part)
                    if w * PARTS + part < len(PIECES):
                        low_piece(w * PARTS + part)

            def pool_chunk(c, waves):
                for f in range(FT):
                    w, n = fw(f), FT * c + f + 1
                    if waves:
                        pool_part(*wave_part(c, 2 * f))
                    pool.wait_ge(acth_set, n + 1)
                    pool.tensor_tensor(actl[0:w, f % 3, :], act_t[0:w, f % 2, :], f32(acth[0:w, f % 3, :]),
                                       ALU.subtract).then_inc(actl_set, 1)
                    if waves:
                        pool_part(*wave_part(c, 2 * f + 1))

            over_chunks(pool, pool_chunk)

        @block.vector
        def _(dve):
            linked = Linked(dve, prep_chain)
            link = linked.link

            dve.wait_ge(decay_exp, 1)
            link(dve.tensor_scalar(td[:, :], td[:, :], -1.0, None, ALU.mult))
            link(dve.memset(wdec[:, :, :], 0.0))
            for k in range(KT):
                real = wdec[:, WB * k:WB * (k + 1), 1:]
                dve.tensor_scalar(real, real, td[:, k:k + 1], None, ALU.add)
            dve.memset(wdec[:, :, 0:1], NEG)
            dve.memset(kp[:, :, 0:1], NEG)
            dve.memset(e1b[:, :, 0:1], 0.0)
            dve.memset(e2b[:, :, 0:1], 0.0)
            link(dve.memset(g[:, :, 0:1], 0.0))
            dve.sem_inc(wkv_ready, 1)

            for t in range(NCH):
                dve.wait_ge(pmean_done, t + 1)
                dve.tensor_tensor(xc[:, :, toks(t)], x[:, :, toks(t)], over_k(bank(t)), ALU.subtract
                                  ).then_inc(pxc_done, 1)
            for t in range(NCH):
                dve.wait_ge(psd_done, t + 1)
                now(dve, pxn_done, t)
                link(dve.reciprocal(rs[:, :], sd[:, toks(t)]))
                dve.tensor_tensor(xc[:, :, toks(t)], xc[:, :, toks(t)], over_k(rs[:, :]), ALU.mult
                                  ).then_inc(pxn_done, 1)

            dve.wait_ge(w_in, 16 * 5)
            for t in range(NCH):
                b0 = 4 * (t % 2)
                dve.wait_ge(qsd_done, t + 1)
                dve.wait_ge(pxn_done, NCH)
                link(dve.reciprocal(rs[:, :], sd[:, toks(t)]))
                link(dve.scalar_tensor_tensor(pt1[:, :], bank(b0), lnw[:, 0:1], rs[:, :], ALU.mult, ALU.mult))
                link(dve.tensor_copy(qn1h[:, toks(t)], pt1[:, :]))
                link(dve.tensor_tensor(qn1l[:, toks(t)], pt1[:, :], f32(qn1h[:, toks(t)]), ALU.subtract))
                link(dve.scalar_tensor_tensor(pt1[:, :], bank(b0 + 1), lnw[:, 1:2], rs[:, :], ALU.mult, ALU.mult))
                link(dve.tensor_copy(qn2[:, toks(t)], pt1[:, :]))
                link(dve.tensor_tensor(qn2[QR2:, toks(t)], pt1[QR2:, :], f32(qn2[QR2:, toks(t)]), ALU.subtract
                                       ))
                dve.sem_inc(qn_done, 1)

            for t in range(NCH):
                b0 = 4 * (t % 2)
                lat, rot, swp = bank(b0)[0:KVLR, :], bank(b0)[KVLR:, :], bank(b0 + 1)[KVLR:, :]
                dve.wait_ge(kvsd_done, t + 1)
                link(dve.reciprocal(rs[0:KVLR, :], sd[0:KVLR, toks(t)]))
                if t:
                    dve.wait_ge(ckvT_done, t)
                link(dve.scalar_tensor_tensor(xc[0:KVLR, 0, toks(t)], lat, lnw[0:KVLR, 2:3], rs[0:KVLR, :],
                                              ALU.mult, ALU.mult))
                dve.sem_inc(ckn_done, 1)
                dve.tensor_scalar(ka[0:KVLR, toks(t)], xc[0:KVLR, 0, toks(t)], SCALE, None, ALU.mult)
                link(dve.tensor_tensor(by_b(pt1[KVLR:, :]), by_b(rot), over_b(rope[KVLR:, 2, :]), ALU.mult))
                link(dve.tensor_tensor(by_b(rs[KVLR:, :]), by_b(swp), over_b(rope[KVLR:, 3, :]), ALU.mult))
                link(dve.tensor_tensor(ka[KVLR:, toks(t)], pt1[KVLR:, :], rs[KVLR:, :], ALU.add))
                dve.sem_inc(keys_done, 1)
                dve.wait_ge(ckvT_done, t + 1)
                dve.tensor_copy(ckv[:, BC * t:BC * (t + 1), 0:KVLR],
                                bank(b0 + 3)[:, 0:BC * KVLR].rearrange("p (b c) -> p b c", c=KVLR)
                                ).then_inc(ckv_set, 1)

            def mw_low(head, j):
                dve.wait_ge(mwh_set, head + 1)
                dve.tensor_tensor(mwl[:, j, :, 0:KVLR],
                                  bank(MW_BANK)[:, 0:2 * KVLR].rearrange("p (a c) -> p a c", a=2),
                                  f32(mwh[:, j, :, 0:KVLR]), ALU.subtract).then_inc(mwl_set, 1)

            def wo_low(pair, j):
                dve.wait_ge(woh_set, pair + 1)
                dve.tensor_tensor(wol[:, j, :], bank(WO_BANK)[:, 0:D], f32(woh[:, j, :]), ALU.subtract
                                  ).then_inc(wol_set, 1)

            def take_query(job, m):
                par = m // HG % 2
                dve.wait_ge(qs_set, job + 1)
                now(dve, s_done, HG * (m // HG) - HG + job - m)
                dve.tensor_tensor(by_b(qa[:, par, m % HG, :]), by_b(bank(Q_BANK)), over_b(rope[:, 0, :]), ALU.mult
                                  ).then_inc(qcos_set, 1)

            def add_sine(job, m):
                part = qa[KVLR:, m // HG % 2, m % HG, :]
                dve.wait_ge(qu_set, job + 1)
                dve.wait_ge(qcos_set, job + 1)
                dve.tensor_tensor(part, part, qu[KVLR:, :], ALU.add).then_inc(q_set, 1)

            def negative_max(n, m):
                dve.wait_ge(s_done, n + 1)
                now(dve, p_done, n - 1)
                dve.tensor_reduce(nmax[:, m % 2, :],
                                  bank(S_BANK + m % 2).rearrange("p (h k) -> p h k", h=HG),
                                  AX.X, ALU.max, negate=True).then_inc(max_done, 1)

            def normalise(n):
                pv = bank(PV_BANK)[:, 0:HG * (KVLR + 1)].rearrange("p (h c) -> p h c", h=HG)
                dve.wait_ge(pv_done, n + 1)
                dve.reciprocal(rsum[:, :], pv[:, :, KVLR]).then_inc(rsum_set, 1)
                dve.wait_ge(rsum_set, n + 1)
                now(dve, oT_done, n)
                dve.tensor_tensor(o[:, :, :], pv[:, :, 0:KVLR],
                                  rsum[:, :].unsqueeze(2).to_broadcast([128, HG, KVLR]), ALU.mult
                                  ).then_inc(o_done, 1)

            def outputs_low(n, m):
                par, b = m // BC % 2, m % BC
                dve.wait_ge(oTh_set, n + 1)
                dve.tensor_tensor(oTl[:, par, :, b * S:b * S + S],
                                  bank(OT_BANK)[:, 0:NP * S].rearrange("p (a s) -> p a s", a=NP),
                                  f32(oTh[:, par, :, b * S:b * S + S]), ALU.subtract).then_inc(oTl_set, 1)

            def add_outputs(it, c):
                for m in range(KT):
                    dve.wait_ge(y_done, KT * it + m + 1)
                    dve.tensor_tensor(x[:, m, toks(c)], x[:, m, toks(c)], bank(Y_BANK + m), ALU.add
                                      ).then_inc(y_added, 1)

            for j in range(HG):
                mw_low(j, j)
            for job in range(LEAD - 1):
                take_query(job, job)
                add_sine(job, job)
            negative_max(0, 0)

            def dve_group(gi, first, last):
                for k in range(QUADS):
                    n = QUADS * gi + k
                    if k or not first:
                        normalise(n - 1)
                    more = k + LEAD - 1 < QUADS or not last
                    if more:
                        take_query(n + LEAD - 1, k + LEAD - 1)
                    if k + 1 < QUADS or not last:
                        negative_max(n + 1, k + 1)
                    if more:
                        add_sine(n + LEAD - 1, k + LEAD - 1)
                    if k or not first:
                        outputs_low(n - 1, k - 1 + QUADS)
                    if k % BC == 1 and (k > 1 or not first):
                        add_outputs(NCH * gi + k // BC - 1, (k // BC - 1) % NCH)
                    if k in WO_SLOTS:
                        j = WO_SLOTS.index(k)
                        wo_low(NP * gi + j, j)
                    if k in MW_SLOTS and not last:
                        j = MW_SLOTS.index(k)
                        mw_low(HG * gi + HG + j, j)

            over_groups(dve, dve_group)
            normalise(NG * QUADS - 1)
            outputs_low(NG * QUADS - 1, QUADS - 1)
            add_outputs(NG * NCH - 1, NCH - 1)

            wave = Linked(dve, wave_chain)

            def flat(a):
                return a[:, :, :].rearrange("p a b -> p (a b)")

            def ktile(a, k):
                return a[:, WB * k:WB * (k + 1), :]

            def over_e(ap):
                return ap.unsqueeze(2).to_broadcast([128, WB, E])

            def center(w, i):
                dve.wait_ge(mean_done, 2 * w + i + 1)
                dve.tensor_tensor(xw[:, :, :], x[:, :, wtoks(w)], over_k(bank(W_BANK)[:, 0:WT]), ALU.subtract
                                  ).then_inc(xc_done, 1)

            def variance(w, i):
                dve.wait_ge(var_done, 2 * w + i + 1)
                dve.tensor_scalar(stat[:, :], bank(W_BANK)[:, 0:WB], LN_EPS, None, ALU.add).then_inc(stat_set, 1)

            def running_maximum(w):
                dve.wait_ge(r_done, 2 * w + 1)
                for k in range(KT):
                    last = dve.tensor_tensor(ktile(kp, k)[:, :, 1:], by_b(xw[:, k, :]), by_b(bank(W_BANK)[:, 0:WT]),
                                             ALU.mult)
                wave.link(last)
                wave.link(dve.tensor_tensor_scan(flat(pp), flat(wdec), flat(kp), NEG, ALU.add, ALU.max))

            def state_exponents():
                before, after = pp[:, :, 0:S], pp[:, :, 1:]
                dve.tensor_tensor(e1b[:, :, 1:], before, after, ALU.subtract).then_inc(d1_set, 1)
                dve.tensor_tensor(e2b[:, :, 1:], kp[:, :, 1:], after, ALU.subtract).then_inc(d2_set, 1)

            def output_maximum():
                for k in range(KT):
                    last = dve.scalar_tensor_tensor(ktile(qq, k), ktile(kp, k)[:, :, 1:], tf[:, k:k + 1],
                                                    ktile(pp, k)[:, :, 0:S], ALU.add, ALU.max)
                wave.link(last)
                dve.tensor_tensor(e1[:, :, :], pp[:, :, 0:S], qq[:, :, :], ALU.subtract).then_inc(d3_set, 1)

            def new_key_exponent():
                for k in range(KT):
                    last = dve.scalar_tensor_tensor(ktile(e2, k), ktile(kp, k)[:, :, 1:], tf[:, k:k + 1],
                                                    ktile(qq, k), ALU.add, ALU.subtract)
                last.then_inc(d4_set, 1)

            def states(w):
                dve.wait_ge(e1b_set, w + 1)
                dve.wait_ge(e2b_set, w + 1)
                dve.tensor_tensor_scan(flat(bb), flat(e1b), flat(e2b), 0.0, ALU.mult, ALU.add)
                dve.wait_ge(g_set, w + 1)
                wave.link(dve.tensor_tensor_scan(flat(aa), flat(e1b), flat(g), 0.0, ALU.mult, ALU.add))

            def denominator(w):
                dve.wait_ge(e1_set, w + 1)
                wave.link(dve.tensor_tensor(qq[:, :, :], e1[:, :, :], bb[:, :, 0:S], ALU.mult))
                dve.wait_ge(e2_set, w + 1)
                wave.link(dve.tensor_tensor(qq[:, :, :], qq[:, :, :], e2[:, :, :], ALU.add))

            def quotient(w):
                wave.link(dve.tensor_tensor(e1[:, :, :], e1[:, :, :], aa[:, :, 0:S], ALU.mult))
                dve.wait_ge(e2v_set, w + 1)
                wave.link(dve.tensor_tensor(e1[:, :, :], e1[:, :, :], v[:, :, :], ALU.add))
                wave.link(dve.tensor_tensor(e1[:, :, :], e1[:, :, :], qq[:, :, :], ALU.mult))

            def add_wkv(w):
                for k in range(KT):
                    xs = by_b(x[:, k, wtoks(w)])
                    last = dve.tensor_tensor(xs, xs, ktile(e1, k), ALU.add)
                last.then_inc(wkv_done, 1)

            def logits(w):
                dve.wait_ge(hh_set, w + 1)
                dve.tensor_tensor(hl[:, :, held(w)], xw[:, :, :], f32(hh[:, :, held(w)]), ALU.subtract
                                  ).then_inc(hl_set, 1)
                dve.wait_ge(logit_done, w + 1)
                wave.link(dve.tensor_copy(lg[:, :, :],
                                          bank(W_BANK)[:, 0:WB * NR].rearrange("p (b e) -> p b e", e=NR)))
                wave.link(dve.tensor_reduce(rt[:, 0, :], lg[:, :, 0:E], AX.X, ALU.max))
                dve.tensor_tensor(pr[:, :, :], lg[:, :, 0:E], over_e(rt[:, 0, :]), ALU.subtract).then_inc(lmax_set, 1)

            def choose(w):
                dve.wait_ge(lexp_set, w + 1)
                wave.link(dve.tensor_reduce(rt[:, 1, :], pr[:, :, :], AX.X, ALU.add))
                wave.link(dve.reciprocal(rt[:, 1, :], rt[:, 1, :]))
                wave.link(dve.tensor_tensor(pr[:, :, :], pr[:, :, :], over_e(rt[:, 1, :]), ALU.mult))
                other = pr[:, :, :].unsqueeze(2).to_broadcast([128, WB, E, E])
                own = pr[:, :, :].unsqueeze(3).to_broadcast([128, WB, E, E])
                dve.tensor_tensor(gt[:, :, :, :], other, own, ALU.is_gt)
                wave.link(dve.tensor_tensor(eq[:, :, :, :], other, own, ALU.is_equal))
                wave.link(dve.tensor_tensor(eq[:, :, :, :], eq[:, :, :, :],
                                            low[:, :, :].unsqueeze(1).to_broadcast([128, WB, E, E]), ALU.mult))
                wave.link(dve.tensor_tensor(gt[:, :, :, :], gt[:, :, :, :], eq[:, :, :, :], ALU.add))
                dve.tensor_scalar(cw[:, :, E], lg[:, :, E], 1.0, None, ALU.add)
                wave.link(dve.tensor_reduce(rank[:, :, :], gt[:, :, :, :], AX.X, ALU.add))
                dve.scalar_tensor_tensor(cw[:, :, 0:E], rank[:, :, :], TOPK - 0.5, pr[:, :, :], ALU.is_lt, ALU.mult)
                wave.link(dve.reciprocal(cw[:, :, E], cw[:, :, E]))
                wave.link(dve.tensor_copy(cwp[:, :, 0:NR], cw[:, :, :]))
                dve.tensor_tensor(cwp[:, :, NR:], cw[:, :, :], f32(cwp[:, :, 0:NR]), ALU.subtract).then_inc(cw_set, 1)

            def dve_part(w, part):
                if part == 0:
                    wave.start(LINKS * w)
                if part in (0, 11):
                    center(w, part // 11)
                elif part in (1, 12):
                    variance(w, part // 12)
                elif part == 2:
                    running_maximum(w)
                elif part == 3:
                    state_exponents()
                elif part == 4:
                    output_maximum()
                elif part == 5:
                    new_key_exponent()
                elif part == 6:
                    states(w)
                elif part == 7:
                    denominator(w)
                elif part == 8:
                    wave.link(dve.reciprocal(qq[:, :, :], qq[:, :, :]))
                elif part == 9:
                    quotient(w)
                elif part == 10:
                    add_wkv(w)
                elif part == 13:
                    dve.wait_ge(r_done, 2 * w + 2)
                    dve.tensor_tensor(xw[:, :, :], xw[:, :, :], over_k(bank(W_BANK)[:, 0:WT]), ALU.mult
                                      ).then_inc(xn_done, 1)
                elif part == 14:
                    logits(w)
                elif part == 15:
                    choose(w)
                    assert wave.made == LINKS, wave.made

            for w in range(WAVES):
                for part in range(PARTS):
                    dve_part(w, part)
            dve.wait_ge(sel_in, 16)
            dve.tensor_copy(sel[:, :], selraw[:, :]).then_inc(sel_set, 1)

            def dve_chunk(c, waves):
                for f in range(FT):
                    w, n, free = fw(f), FT * c + f + 1, FT * c + max(f - 1, 0) + 1
                    hidden = act_t[0:w, f % 2, :]
                    if waves:
                        dve_part(*wave_part(c, 2 * f))
                    dve.wait_ge(up_done, n + 1)
                    dve.wait_ge(silu_done, n + 1)
                    dve.wait_ge(actl_set, free)
                    dve.tensor_tensor(hidden, act_s[0:w, f % 2, :], bank(U_BANK + f % 2)[0:w, :], ALU.mult
                                      ).then_inc(mix_done, 1)
                    dve.wait_ge(mix_done, n + 1)
                    dve.tensor_tensor(hidden, hidden, bank(C_BANK)[0:w, :], ALU.mult).then_inc(prod_done, 1)
                    if waves:
                        dve_part(*wave_part(c, 2 * f + 1))
                dve.wait_ge(down_done, FT * (c + 1) + 1)
                for m in range(KT):
                    dve.tensor_tensor(x[:, m, toks(c)], x[:, m, toks(c)], bank(Z_BANK + m), ALU.add
                                      ).then_inc(z_added, 1)

            over_chunks(dve, dve_chunk)

        @block.scalar
        def _(act):
            act.wait_ge(const_in, 16 * 6)
            act.activation(maskb[:, :], maskf[:, :], ACT.Copy)
            act.activation(identb[:, :], ident[:, :], ACT.Copy).then_inc(cast_set, 1)
            act.activation(td[:, :], td[:, :], ACT.Exp).then_inc(decay_exp, 1)
            act.wait_ge(const_set, 1)

            for t in range(NCH):
                act.wait_ge(pxc_done, t + 1)
                act.activation(sq[:, :, toks(t)], xc[:, :, toks(t)], ACT.Square).then_inc(psq_done, 1)
            for t in range(NCH):
                act.wait_ge(pvar_done, t + 1)
                act.activation(sd[:, toks(t)], bank(4 + t), ACT.Sqrt, bias=eps[:, 0:1]).then_inc(psd_done, 1)
            for t in range(NCH):
                b0 = 4 * (t % 2)
                act.wait_ge(qproj_done, t + 1)
                act.activation(sq[:, 0, toks(t)], bank(b0), ACT.Square)
                act.activation(sq[0:QR2, 1, toks(t)], bank(b0 + 1)[0:QR2, :], ACT.Square).then_inc(qsq_done, 1)
                act.wait_ge(qsum_done, t + 1)
                act.wait_ge(pxn_done, t + 1)
                act.activation(sd[:, toks(t)], bank(b0 + 2), ACT.Sqrt, bias=eps[:, 1:2]).then_inc(qsd_done, 1)
            for t in range(NCH):
                b0 = 4 * (t % 2)
                act.wait_ge(kvproj_done, t + 1)
                act.activation(sq[0:KVLR, 0, toks(t)], bank(b0)[0:KVLR, :], ACT.Square).then_inc(kvsq_done, 1)
                act.wait_ge(kvsum_done, t + 1)
                act.wait_ge(qn_done, t + 1)
                act.activation(sd[0:KVLR, toks(t)], bank(b0 + 2)[0:KVLR, :], ACT.Sqrt, bias=eps[0:KVLR, 1:2]
                               ).then_inc(kvsd_done, 1)

            def mw_high(head, j, freed):
                act.wait_ge(mw_done, head + 1)
                now(act, qp_done, freed)
                act.activation(mwh[:, j, :, 0:KVLR],
                               bank(MW_BANK)[:, 0:2 * KVLR].rearrange("p (a c) -> p a c", a=2), ACT.Copy)
                act.activation(mwh[:, j, :, KVLR:], rotated(j), ACT.Copy).then_inc(mwh_set, 1)

            def wo_high(pair, j, freed):
                act.wait_ge(wo_done, pair + 1)
                now(act, y_done, freed)
                act.activation(woh[:, j, :], bank(WO_BANK)[:, 0:D], ACT.Copy).then_inc(woh_set, 1)

            def exponentials(n, m):
                act.wait_ge(max_done, n + 1)
                now(act, pT_done, n - 1)
                for hd in range(HG):
                    last = act.activation(p[:, m % 2, hd, :], bank(S_BANK + m % 2)[:, hd * S:hd * S + S], ACT.Exp,
                                          bias=nmax[:, m % 2, hd:hd + 1])
                last.then_inc(p_done, 1)

            def probs_out(n):
                act.wait_ge(pT_done, n + 1)
                now(act, pv_done, n)
                act.activation(pT[:, :, :].rearrange("p h q -> p (h q)"), bank(PT_BANK), ACT.Copy
                               ).then_inc(pT_set, 1)

            def outputs_high(n, m, it):
                par, b = m // BC % 2, m % BC
                act.wait_ge(oT_done, n + 1)
                now(act, y_done, KT * (it - 1))
                act.activation(oTh[:, par, :, b * S:b * S + S],
                               bank(OT_BANK)[:, 0:NP * S].rearrange("p (a s) -> p a s", a=NP), ACT.Copy
                               ).then_inc(oTh_set, 1)

            def swap_halves(job):
                half = DR // 2
                act.wait_ge(qp_done, job + 1)
                now(act, qu_set, job)
                act.activation(qs[KVLR:KVLR + half, :], bank(Q_BANK)[KVLR + half:, :], ACT.Copy)
                act.activation(qs[KVLR + half:, :], bank(Q_BANK)[KVLR:KVLR + half, :], ACT.Copy).then_inc(qs_set, 1)

            for j in range(HG):
                mw_high(j, j, 0)
            for job in range(LEAD):
                swap_halves(job)
            exponentials(0, 0)

            def act_group(gi, first, last):
                for k in range(QUADS):
                    n = QUADS * gi + k
                    probs_out(n)
                    if k + 1 < QUADS or not last:
                        exponentials(n + 1, k + 1)
                    if k or not first:
                        outputs_high(n - 1, k - 1 + QUADS, NCH * gi + (k - 1) // BC)
                    if k + LEAD < QUADS or not last:
                        swap_halves(n + LEAD)
                    if k in WO_SLOTS:
                        j = WO_SLOTS.index(k)
                        wo_high(NP * gi + j, j, KT * NCH * gi)
                    if k in MW_SLOTS and not last:
                        j = MW_SLOTS.index(k)
                        mw_high(HG * gi + HG + j, j, QUADS * gi + QUADS - HG + j + 1)

            over_groups(act, act_group)
            outputs_high(NG * QUADS - 1, QUADS - 1, NG * NCH - 1)

            def square(w, i):
                act.wait_ge(xc_done, 2 * w + i + 1)
                act.activation(sqw[:, :, :], xw[:, :, :], ACT.Square).then_inc(sq_done, 1)

            def exp_of(a, ready, done, w):
                act.wait_ge(ready, w + 1)
                act.activation(a, a, ACT.Exp).then_inc(done, 1)

            def act_part(w, part):
                if part in (0, 11):
                    square(w, part // 11)
                elif part == 3:
                    act.wait_ge(d1_set, w + 1)
                    for k in range(KT):
                        a = e1b[:, WB * k:WB * (k + 1), 1:]
                        last = act.activation(a, a, ACT.Exp, bias=td[:, k:k + 1])
                    last.then_inc(e1b_set, 1)
                    exp_of(e2b[:, :, 1:], d2_set, e2b_set, w)
                elif part == 4:
                    exp_of(e1[:, :, :], d3_set, e1_set, w)
                elif part == 5:
                    exp_of(e2[:, :, :], d4_set, e2_set, w)
                elif part == 13:
                    act.wait_ge(xn_done, w + 1)
                    act.activation(hh[:, :, held(w)], xw[:, :, :], ACT.Copy).then_inc(hh_set, 1)
                elif part == 14:
                    act.wait_ge(lmax_set, w + 1)
                    act.activation(pr[:, :, :], pr[:, :, :], ACT.Exp)
                    act.activation(lg[:, :, E], lg[:, :, E], ACT.Exp, scale=-1.0).then_inc(lexp_set, 1)
                elif part == 16:
                    act.wait_ge(cT_done, w + 1)
                    act.activation(cT[:, held(w)], bank(W_BANK)[0:2 * NR, 0:WT], ACT.Copy).then_inc(cT_set, 1)

            def high_piece(n):
                raw, hi, _ = piece(n)
                act.wait_ge(stage_in[n % 2], 16 * (n // 2 + 1))
                act.activation(hi, raw, ACT.Copy).then_inc(piece_h, 1)

            act.wait_ge(wkv_ready, 1)
            for w in range(WAVES):
                for part in range(PARTS):
                    act_part(w, part)
                    if w * PARTS + part < len(PIECES):
                        high_piece(w * PARTS + part)

            def act_chunk(c, waves):
                for f in range(FT):
                    w, n, free = fw(f), FT * c + f + 1, FT * c + max(f - 1, 0) + 1
                    act.wait_ge(gate_done, n + 1)
                    act.wait_ge(mix_done, free)
                    act.activation(act_s[0:w, f % 2, :], bank(G_BANK + f % 2)[0:w, :], ACT.Silu).then_inc(silu_done, 1)
                    if waves:
                        act_part(*wave_part(c, 2 * f))
                    act.wait_ge(down_done, FT * c + max(f - 2, 0) + 1)
                    act.wait_ge(prod_done, n + 1)
                    act.activation(acth[0:w, f % 3, :], act_t[0:w, f % 2, :], ACT.Copy).then_inc(acth_set, 1)
                    if waves:
                        act_part(*wave_part(c, 2 * f + 1))

            over_chunks(act, act_chunk)

        @block.tensor
        def _(pe):
            def mm(out, lhsT, rhs, start, stop, **kw):
                return pe.matmul(out, lhsT, rhs, start=start, stop=stop, **kw)

            def mm3(out, wh, wl, rh, rl, start=True, stop=True):
                mm(out, wh, rh, start, False)
                mm(out, wh, rl, False, False)
                return mm(out, wl, rh, False, stop)

            def mean_of(out, src):
                for k in range(KT):
                    last = mm(out, mean_w[:, :], src(k), k == 0, k == KT - 1)
                return last

            pe.wait_ge(const_set, 1)
            for t in range(NCH):
                pe.wait_ge(x_in[t], 16)
                mean_of(bank(t), lambda k: x[:, k, toks(t)]).then_inc(pmean_done, 1)
            for t in range(NCH):
                pe.wait_ge(psq_done, t + 1)
                mean_of(bank(4 + t), lambda k: sq[:, k, toks(t)]).then_inc(pvar_done, 1)

            pe.wait_ge(w_in, 16 * 5)
            pe.wait_ge(const_in, 16 * 6)

            def project(t, weights, b0):
                for i, w in enumerate(weights):
                    for k in range(KT):
                        last = mm(bank(b0 + i), w(k), xc[:, k, toks(t)], k == 0, k == KT - 1)
                return last

            def query_latent(t):
                pe.wait_ge(pxn_done, t + 1)
                if t < 2:
                    pe.wait_ge(psd_done, NCH)
                else:
                    pe.wait_ge(qn_done, t - 1)
                project(t, (lambda k: qaw[:, k, 0:128], lambda k: qaw[:, k, 128:]), 4 * (t % 2)
                        ).then_inc(qproj_done, 1)

            def query_squares(t):
                pe.wait_ge(qsq_done, t + 1)
                out = bank(4 * (t % 2) + 2)
                mm(out, meanq_w[:, :], sq[:, 0, toks(t)], True, False)
                mm(out, meanq_w[0:QR2, :], sq[0:QR2, 1, toks(t)], False, True).then_inc(qsum_done, 1)

            def key_latent(t):
                if t < 2:
                    pe.wait_ge(qn_done, t + NCH - 1)
                else:
                    pe.wait_ge(ckv_set, t - 1)
                    pe.wait_ge(keys_done, t - 1)
                project(t, (lambda k: kvw[:, k, 0:128], lambda k: kvw[:, k, 128:]), 4 * (t % 2)
                        ).then_inc(kvproj_done, 1)

            def key_squares(t):
                pe.wait_ge(kvsq_done, t + 1)
                mm(bank(4 * (t % 2) + 2)[0:KVLR, :], meankv_w[:, :], sq[0:KVLR, 0, toks(t)], True, True
                   ).then_inc(kvsum_done, 1)

            def values_by_token(t):
                pe.wait_ge(ckn_done, t + 1)
                for b in range(BC):
                    last = pe.transpose(bank(4 * (t % 2) + 3)[:, b * KVLR:(b + 1) * KVLR],
                                        xc[0:KVLR, 0, bass.ds(t * CH + b * S, S)], ident[0:KVLR, 0:KVLR])
                last.then_inc(ckvT_done, 1)

            for t in range(NCH + 1):
                if t < NCH:
                    query_latent(t)
                if t:
                    query_squares(t - 1)
            for t in range(NCH + 1):
                if t < NCH:
                    key_latent(t)
                if t:
                    key_squares(t - 1)
                    values_by_token(t - 1)

            def absorb_queries(head, j, gi, projected):
                pe.wait_ge(raw_m_in, 16 * (gi + 1))
                now(pe, mwl_set, head)
                now(pe, y_added, KT * projected)
                keys = raw_m[:, j, 128 + 2 * QR2:128 + 2 * QR2 + KVLR]
                for a in range(2):
                    last = mm(bank(MW_BANK)[:, a * KVLR:(a + 1) * KVLR],
                              raw_m[:, j, 128 * a:128 * (a + 1)], keys, True, True)
                last.then_inc(mw_done, 1)

            def absorb_outputs(pair, j, gi, projected):
                pe.wait_ge(raw_v_in, 16 * (gi + 1))
                now(pe, wol_set, pair)
                now(pe, y_added, KT * projected)
                for a in range(2):
                    last = mm(bank(WO_BANK)[a * KVLR:(a + 1) * KVLR, 0:D], raw_v[:, 2 * j + a, 0:KVLR],
                              raw_v[:, 2 * j + a, KVLR:], True, True)
                last.then_inc(wo_done, 1)

            def queries(job, m, gi):
                c, j = m // HG % NCH, m % HG
                pe.wait_ge(mwl_set, HG * gi + j + 1)
                pe.wait_ge(rot_set, HG * gi + j + 1)
                now(pe, qcos_set, job)
                out = bank(Q_BANK)
                mm3(out, mwh[:, j, 0, :], mwl[:, j, 0, :], qn1h[:, toks(c)], qn1l[:, toks(c)], True, False)
                mm(out, mwh[:, j, 1, :], qn2[:, toks(c)], False, False)
                mm(out, mwl[0:QR2, j, 1, :], qn2[0:QR2, toks(c)], False, True).then_inc(qp_done, 1)

            def scores(n, m, jobs):
                par, b = m // BC % 2, m % BC
                key = bass.ds((m % QUADS) * S, S)
                now(pe, p_done, n - 1)
                pe.wait_ge(q_set, jobs)
                out = bank(S_BANK + m % 2)
                mm(out, identb[:, :], maskb[:, :].unsqueeze(1).to_broadcast([128, HG, S]), True, True)
                for j in range(HG):
                    part = out[:, j * S:(j + 1) * S]
                    last = mm(part, qa[:, par, j, b * S:(b + 1) * S], ka[:, key], False, True,
                              skip_group_check=True)
                last.then_inc(s_done, 1)

            def transpose_probs(n, m):
                pe.wait_ge(p_done, n + 1)
                now(pe, pT_set, n)
                for j in range(HG):
                    last = pe.transpose(bank(PT_BANK)[:, j * S:(j + 1) * S], p[:, m % 2, j, :], ident[:, :])
                last.then_inc(pT_done, 1)

            def weigh_values(n, m):
                pe.wait_ge(pT_set, n + 1)
                now(pe, o_done, n)
                for j in range(HG):
                    last = mm(bank(PV_BANK)[:, j * (KVLR + 1):(j + 1) * (KVLR + 1)], pT[:, j, :],
                              ckv[:, m % QUADS, :], True, True)
                last.then_inc(pv_done, 1)

            def transpose_outputs(n):
                pe.wait_ge(o_done, n + 1)
                now(pe, oTl_set, n)
                for a in range(NP):
                    last = pe.transpose(bank(OT_BANK)[:, a * S:(a + 1) * S],
                                        o[:, 2 * a:2 * a + 2, :].rearrange("p h c -> p (h c)"), ident[:, :])
                last.then_inc(oT_done, 1)

            def project_outputs(it, par, gi, heads):
                pe.wait_ge(oTl_set, BC * (it + 1))
                pe.wait_ge(wol_set, NP * (gi + 1))
                pe.wait_ge(mwl_set, heads)
                for m in range(KT):
                    now(pe, y_added, KT * (it - 1) + m + 1)
                    cols = slice(128 * m, 128 * (m + 1))
                    for a in range(NP):
                        last = mm3(bank(Y_BANK + m), woh[:, a, cols], wol[:, a, cols], oTh[:, par, a, :],
                                   oTl[:, par, a, :], a == 0, a == NP - 1)
                    last.then_inc(y_done, 1)

            pe.wait_ge(ckv_set, NCH)
            pe.wait_ge(keys_done, NCH)
            pe.wait_ge(cast_set, 1)
            for j in range(HG):
                absorb_queries(j, j, 0, 0)
            for job in range(LEAD):
                queries(job, job, 0)
            scores(0, 0, HG)

            def pe_group(gi, first, last):
                for k in range(QUADS):
                    n = QUADS * gi + k
                    if k + 1 < QUADS or not last:
                        scores(n + 1, k + 1, n - k + (k + 1) // BC * HG + HG)
                    transpose_probs(n, k)
                    if k + LEAD < QUADS or not last:
                        queries(n + LEAD, k + LEAD, gi + (k + LEAD) // QUADS)
                    if k or not first:
                        transpose_outputs(n - 1)
                    if k % BC == 1 and (k > 1 or not first):
                        it = NCH * gi + k // BC - 1
                        absorbed = 0 if last else len([j for j in MW_SLOTS if j < k])
                        project_outputs(it, (k // BC + 1) % 2, gi if k > 1 else gi - 1, HG * (gi + 1) + absorbed)
                    weigh_values(n, k)
                    projected = NCH * gi + (k - 1) // BC
                    if k in WO_SLOTS:
                        j = WO_SLOTS.index(k)
                        absorb_outputs(NP * gi + j, j, gi, projected)
                    if k in MW_SLOTS and not last:
                        j = MW_SLOTS.index(k)
                        absorb_queries(HG * gi + HG + j, j, gi + 1, projected)

            over_groups(pe, pe_group)
            transpose_outputs(NG * QUADS - 1)
            project_outputs(NG * NCH - 1, (NCH - 1) % 2, NG - 1, NH)

            def variances(w, i):
                pe.wait_ge(sq_done, 2 * w + i + 1)
                for b in range(WB):
                    for k in range(KT):
                        last = mm(bank(W_BANK)[:, b:b + 1], sqw[:, k, b * S:(b + 1) * S], mean_w[:, 0:1],
                                  k == 0, k == KT - 1)
                last.then_inc(var_done, 1)

            def spread(w, i):
                pe.wait_ge(rinv_set, 2 * w + i + 1)
                for b in range(WB):
                    last = mm(bank(W_BANK)[:, b * S:(b + 1) * S], rinv[:, b:b + 1].to_broadcast([128, 128]),
                              ident[:, :], True, True)
                last.then_inc(r_done, 1)

            def pe_part(w, part):
                if part in (0, 10):
                    if part == 0:
                        now(pe, cT_set, w)
                    else:
                        pe.wait_ge(wkv_done, w + 1)
                    mean_of(bank(W_BANK)[:, 0:WT], lambda k: x[:, k, wtoks(w)]).then_inc(mean_done, 1)
                elif part in (1, 12):
                    variances(w, part // 12)
                elif part in (2, 13):
                    spread(w, part // 13)
                elif part == 14:
                    pe.wait_ge(xn_done, w + 1)
                    for b in range(WB):
                        for k in range(KT):
                            last = mm(bank(W_BANK)[:, b * NR:(b + 1) * NR], xw[:, k, b * S:(b + 1) * S], wr[:, k, :],
                                      k == 0, k == KT - 1)
                    last.then_inc(logit_done, 1)
                elif part == 16:
                    pe.wait_ge(cw_set, w + 1)
                    for b in range(WB):
                        last = pe.transpose(bank(W_BANK)[0:2 * NR, b * S:(b + 1) * S], f32(cwp[:, b, :]),
                                            ident[:, :])
                    last.then_inc(cT_done, 1)

            pe.wait_ge(y_added, KT * NG * NCH)
            for w in range(WAVES):
                for part in range(PARTS):
                    pe_part(w, part)

            pe.wait_ge(piece_l, len(PIECES))
            pe.wait_ge(piece_h, len(PIECES))
            pe.wait_ge(sel_set, 1)

            def hidden(out, col, w, c, ks=range(KT)):
                now_c = bass.ds((c % 2) * CH, CH)
                for k in ks:
                    last = mm3(out, wguh[:, k, col:col + w], wgul[:, k, col:col + w], hh[:, k, now_c],
                               hl[:, k, now_c], k == 0, k == KT - 1)
                return last

            def weights_of(f, c):
                mm(bank(C_BANK), sel[:, 128 * f:128 * (f + 1)], cT[:, bass.ds((c % 2) * CH, CH)], True, True
                   ).then_inc(up_done, 1)

            def down(n, f):
                w = fw(f)
                pe.wait_ge(actl_set, n + 1)
                for m in range(KT):
                    cols = slice(128 * m, 128 * (m + 1))
                    last = mm3(bank(Z_BANK + m), wdh[0:w, f, cols], wdl[0:w, f, cols], acth[0:w, f % 3, :],
                               actl[0:w, f % 3, :], f == 0, f == FT - 1)
                last.then_inc(down_done, 1)

            def banks_free(n, f):
                pe.wait_ge(mix_done, n - f + max(f - 1, 0))
                pe.wait_ge(silu_done, n - f + max(f - 1, 0))

            def pe_chunk(c, waves):
                for f in range(FT):
                    w, n = fw(f), FT * c + f + 1
                    if f == 0:
                        pe.wait_ge(hl_set, WAVES * (c + 1))
                    if f < FT - 1:
                        banks_free(n, f)
                    hidden(bank(G_BANK + f % 2)[0:w, :], 128 * f, w, c).then_inc(gate_done, 1)
                    if f < FT - 1:
                        pe.wait_ge(prod_done, n)
                    hidden(bank(U_BANK + f % 2)[0:w, :], FF + 128 * f, w, c, range(1))
                    if waves:
                        pe_part(*wave_part(c, 2 * f))
                    hidden(bank(U_BANK + f % 2)[0:w, :], FF + 128 * f, w, c, range(1, KT))
                    if f == 0:
                        pe.wait_ge(cT_set, WAVES * (c + 1))
                    if f < FT - 1:
                        weights_of(f, c)
                    if f == FT - 2:
                        banks_free(n + 1, f + 1)
                    if f == 2:
                        pe.wait_ge(z_added, KT * c + 1)
                    if f == FT - 1:
                        pe.wait_ge(prod_done, n)
                    if f >= 2:
                        down(n - 2, f - 2)
                    if f == FT - 1:
                        weights_of(f, c)
                    if waves:
                        pe_part(*wave_part(c, 2 * f + 1))
                for f in (FT - 2, FT - 1):
                    down(FT * c + f + 1, f)

            over_chunks(pe, pe_chunk)


def _tables():
    inv = (1.0 / np.float32(10000.0) ** (np.arange(0, DR, 2, dtype=np.float32) / np.float32(DR))).astype(np.float32)
    ang = np.arange(S, dtype=np.float32)[None, :] * inv[:, None]
    cos, sin, one = np.cos(ang), np.sin(ang), np.ones((DR, S), np.float32)
    sc = np.float32(SCALE)
    rope = np.stack([np.concatenate([one, cos, cos]), np.concatenate([one, -sin, sin]),
                     np.concatenate([one, cos * sc, cos * sc]), np.concatenate([one, -sin * sc, sin * sc])], 1)
    expert = np.concatenate([np.repeat(np.arange(E), FE), np.full(FS, E), np.full(FT * 128 - FF, -1)])
    sel = (np.arange(2 * NR)[:, None] % NR == expert[None, :]).astype(np.float32)
    pos = np.arange(S)
    mask = np.where(pos[None, :] > pos[:, None], np.float32(NEG), np.float32(0)).astype(np.float32)
    order = np.arange(E)
    low = np.broadcast_to((order[None, :] < order[:, None]).astype(np.float32), (128, E, E))
    return (rope.astype(np.float32), mask, np.eye(128, dtype=np.float32), low, sel)


def kernel(x, ctx_2048, L0_attn_q_a_w, L0_attn_q_a_ln_w, L0_attn_q_b_w, L0_attn_kv_a_w, L0_attn_kv_a_ln_w,
           L0_attn_kv_b_w, L0_attn_o_w, L0_xattn_time_decay, L0_xattn_time_first, L0_ffn_Wr, L0_ffn_Wg,
           L0_ffn_Wu, L0_ffn_Wd, L0_ffn_Sg, L0_ffn_Su, L0_ffn_Sd, L0_ffn_Wsg):
    import concourse.bacc as bacc
    from concourse.bass_utils import run_bass_kernel_spmd

    def feature_major(a):
        return np.asarray(a).reshape(TOK, KT, 128).transpose(2, 1, 0)

    def columns(a):
        return np.asarray(a).reshape(KT, 128, -1).transpose(1, 0, 2)

    qa, qln, qb = (np.asarray(a) for a in (L0_attn_q_a_w, L0_attn_q_a_ln_w, L0_attn_q_b_w))
    kva, kvb, ow = (np.asarray(a) for a in (L0_attn_kv_a_w, L0_attn_kv_b_w, L0_attn_o_w))
    rot = kva[:, KVLR:]
    swapped = np.concatenate([rot[:, DR // 2:], rot[:, :DR // 2]], 1)
    qb = qb.reshape(QLR, NH, DN + DR)
    kvb = kvb.reshape(KVLR, NH, DN + DV)
    twice = np.concatenate([np.arange(128), np.arange(128, QLR), np.arange(128, QLR)])
    m = np.concatenate([qb[twice, :, :DN].transpose(2, 1, 0), kvb[:, :, :DN].transpose(2, 1, 0),
                        qb[:128, :, DN:], qb[twice[128:], :, DN:]], 2)
    vo = np.concatenate([kvb[:, :, DN:].transpose(2, 1, 0), ow.reshape(NH, DV, D).transpose(1, 0, 2)], 2)

    def by_group(a):
        return a.reshape(128, NG, -1).transpose(1, 0, 2)

    def experts(w, shared):
        return np.concatenate([np.asarray(w).transpose(1, 0, 2).reshape(D, E * FE), np.asarray(shared)], 1)

    rope, mask, ident, low, sel = _tables()
    given = [
        ("xT", feature_major(x)), ("ctx", feature_major(ctx_2048)),
        ("td", np.asarray(L0_xattn_time_decay).reshape(KT, 128).T),
        ("tf", np.asarray(L0_xattn_time_first).reshape(KT, 128).T),
        ("qaw", columns(qa[:, twice])), ("qaln", qln[twice].reshape(2, 128).T),
        ("kvw", columns(np.concatenate([kva, swapped, swapped], 1))),
        ("kvln", np.asarray(L0_attn_kv_a_ln_w).reshape(KVLR, 1)),
        ("head", np.concatenate([by_group(m), by_group(vo)], 2)),
        ("wr", columns(np.concatenate([np.asarray(L0_ffn_Wr), np.asarray(L0_ffn_Wsg)], 1))),
        ("wgu", np.concatenate([experts(L0_ffn_Wg, L0_ffn_Sg), experts(L0_ffn_Wu, L0_ffn_Su)], 1)),
        ("wd", np.concatenate([np.asarray(L0_ffn_Wd).reshape(E * FE, D), np.asarray(L0_ffn_Sd)], 0)),
        ("rope", rope), ("mask", mask), ("ident", ident), ("low", low), ("sel", sel),
    ]
    nc = bacc.Bacc("TRN2", target_bir_lowering=False, num_devices=1)
    arrays, args = {}, []
    for name, a in given:
        a = np.ascontiguousarray(a)
        arrays["in_" + name] = a
        args.append(nc.dram_tensor("in_" + name, a.shape, mybir.dt.from_np(a.dtype), kind="ExternalInput").ap())
    args.append(nc.dram_tensor("out", (128, KT, TOK), F32, kind="ExternalOutput").ap())
    decoder_program(nc, *args)
    r = run_bass_kernel_spmd(nc, [arrays], core_ids=[0])
    return np.ascontiguousarray(r.results[0]["out"].transpose(2, 1, 0)).reshape(B, S, D)
```

```python
import concourse.bass as bass
from concourse import mybir
from contextlib import ExitStack, contextmanager
import numpy as np

F32 = mybir.dt.float32
F32R = mybir.dt.float32r
BF16 = mybir.dt.bfloat16
ALU = mybir.AluOpType
ACT = mybir.ActivationFunctionType
AX = mybir.AxisListType

B, S, D = 16, 128, 256
TOK = B * S
KT = D // 128
CH = 512
NCH = TOK // CH
BC = CH // S
NH, QLR, KVLR, DR, DN, DV = 32, 192, 64, 64, 128, 128
QR2 = QLR - 128
HG = 4
NG = NH // HG
NP = HG // 2
QUADS = NCH * BC
SCALE = float(DN + DR) ** -0.5
E, TOPK, FE, FS = 8, 2, 176, 704
FF = E * FE + FS
FT = -(-FF // 128)
NR = E + 1
NEG = -1e38
SEG = S + 1
LN_EPS, RMS_EPS = 1e-5, 1e-6
WT = 256
WB = WT // S
NW = TOK // WT
WAVES = CH // WT
SEGS = KT * WB
PARTS = 17
LINKS = 17
MCOL = 128 + 2 * QR2 + KVLR + 2 * DR
VCOL = KVLR + D
LEAD = 6
MW_SLOTS = (6, 7, 8, 10)
WO_SLOTS = (2, 3)
PIECE = 2 * FF // 4
PIECES = ([("gu", k, a, PIECE, 128) for k in range(KT) for a in range(0, 2 * FF, PIECE)]
          + [("d", 0, a, 4, 128) for a in range(0, FT - 1, 4)] + [("d", 0, FT - 1, 1, FF - 128 * (FT - 1))])


def fw(f):
    return min(128, FF - 128 * f)


class Linked:

    def __init__(self, eng, sem):
        self.eng, self.sem, self.base, self.made = eng, sem, 0, 0

    def start(self, base):
        self.base, self.made = base, 0

    def link(self, result):
        result.then_inc(self.sem, 1)
        self.made += 1
        self.eng.wait_ge(self.sem, self.base + self.made)


def decoder_program(nc, xT_d, ctx_d, td_d, tf_d, qaw_d, qaln_d, kvw_d, kvln_d, head_d, wr_d,
                    wgu_d, wd_d, rope_d, mask_d, ident_d, low_d, sel_d, out_d):
    stack = ExitStack()
    with stack:
        def sem(name):
            return stack.enter_context(nc.semaphore(name))

        def sb(ctx, name, shape, dt=F32):
            return ctx.enter_context(nc.sbuf_tensor(name, shape, dt))

        x = sb(stack, "x", [128, KT, TOK])
        ident = sb(stack, "ident", [128, 128])
        mean_w = sb(stack, "mean_w", [128, 128])
        power = sb(stack, "power", [128, 3 * BC])
        td = sb(stack, "td", [128, KT])
        tf = sb(stack, "tf", [128, KT])
        wr = sb(stack, "wr", [128, KT, NR])
        low = sb(stack, "low", [128, E, E])
        ps = stack.enter_context(nc.psum_tensor("ps", [128, 8, CH], F32))
        xw = sb(stack, "xw", [128, KT, WT])
        sqw = sb(stack, "sqw", [128, KT, WT])
        stat = sb(stack, "stat", [128, WB])
        rinv = sb(stack, "rinv", [128, WB])
        v = sb(stack, "v", [128, SEGS, S])
        wdec = sb(stack, "wdec", [128, SEGS, SEG])
        kp, pp, e1b, e2b, g, aa, bb = (sb(stack, n, [128, SEGS, SEG]) for n in
                                       ("kp", "pp", "e1b", "e2b", "g", "aa", "bb"))
        qq, e1, e2 = (sb(stack, n, [128, SEGS, S]) for n in ("qq", "e1", "e2"))
        lg = sb(stack, "lg", [128, WB, NR])
        pr = sb(stack, "pr", [128, WB, E])
        rt = sb(stack, "rt", [128, 2, WB])
        gt, eq = (sb(stack, n, [128, WB, E, E]) for n in ("gt", "eq"))
        rank = sb(stack, "rank", [128, WB, E])
        cw = sb(stack, "cw", [128, WB, NR])
        cwp = sb(stack, "cwp", [128, WB, 2 * NR], F32R)

        att = ExitStack()
        maskf = sb(att, "maskf", [128, S])
        maskb = sb(att, "maskb", [128, S], BF16)
        identb = sb(att, "identb", [128, 128], BF16)
        meanl_w = sb(att, "meanl_w", [128, 2])
        epsr = sb(att, "epsr", [128, 3 * BC])
        rope = sb(att, "rope", [128, 4, S])
        qaw = sb(att, "qaw", [128, KT, 128 + 2 * QR2])
        kvw = sb(att, "kvw", [128, KT, 256])
        lnw = sb(att, "lnw", [128, 3])
        qn1h = sb(att, "qn1h", [128, TOK], F32R)
        qn1l = sb(att, "qn1l", [128, TOK], F32R)
        qn2 = sb(att, "qn2", [128, TOK], F32R)
        ka = sb(att, "ka", [128, TOK])
        ckv = sb(att, "ckv", [128, B, KVLR + 1])
        xc = sb(att, "xc", [128, 2, KT, CH])
        sq = sb(att, "sq", [128, KT, CH])
        sqp = sb(att, "sqp", [128, 3, CH])
        raw = sb(att, "raw", [128, 2, 4, CH])
        pstat = sb(att, "pstat", [128, 3 * BC])
        prinv = sb(att, "prinv", [128, 3 * BC])
        pt1, pt2 = sb(att, "pt1", [128, CH]), sb(att, "pt2", [128, CH])
        ckn = sb(att, "ckn", [KVLR, CH])
        raw_m = sb(att, "raw_m", [128, HG, MCOL])
        raw_v = sb(att, "raw_v", [128, HG, VCOL])
        mwh = sb(att, "mwh", [128, HG, 2, 128], F32R)
        mwl = sb(att, "mwl", [128, HG, 2, 128], F32R)
        woh = sb(att, "woh", [128, NP, D], F32R)
        wol = sb(att, "wol", [128, NP, D], F32R)
        qa = sb(att, "qa", [128, 2, HG, CH])
        qs = sb(att, "qs", [128, CH])
        qu = sb(att, "qu", [128, CH])
        nmax = sb(att, "nmax", [128, 2, HG])
        p = sb(att, "p", [128, 2, HG, S])
        pT = sb(att, "pT", [128, HG, S])
        rsum = sb(att, "rsum", [128, HG])
        o = sb(att, "o", [128, HG, KVLR])
        oTh = sb(att, "oTh", [128, 2, NP, CH], F32R)
        oTl = sb(att, "oTl", [128, 2, NP, CH], F32R)
        att.close()

        ffn = ExitStack()
        wguh = sb(ffn, "wguh", [128, KT, 2 * FF], F32R)
        wgul = sb(ffn, "wgul", [128, KT, 2 * FF], F32R)
        wdh = sb(ffn, "wdh", [128, FT, D], F32R)
        wdl = sb(ffn, "wdl", [128, FT, D], F32R)
        sel = sb(ffn, "sel", [2 * NR, FT * 128], F32R)
        hh = sb(ffn, "hh", [128, KT, 2 * CH], F32R)
        hl = sb(ffn, "hl", [128, KT, 2 * CH], F32R)
        cT = sb(ffn, "cT", [2 * NR, 2 * CH], F32R)
        staging = ExitStack()
        stage = sb(staging, "stage", [128, 2, PIECE])
        selraw = sb(staging, "selraw", [2 * NR, FT * 128])
        staging.close()
        act_s = sb(ffn, "act_s", [128, 2, CH])
        act_t = sb(ffn, "act_t", [128, 2, CH])
        acth = sb(ffn, "acth", [128, 3, CH], F32R)
        actl = sb(ffn, "actl", [128, 3, CH], F32R)
        ffn.close()

        x_in = [sem(f"x_in{t}") for t in range(NCH)]
        w_in, const_in, raw_m_in, raw_v_in, v_in, sel_in, out_done = (sem(n) for n in (
            "w_in", "const_in", "raw_m_in", "raw_v_in", "v_in", "sel_in", "out_done"))
        stage_in = [sem("stage_in0"), sem("stage_in1")]
        const_set = sem("const_set")
        cast_set = sem("cast_set")
        (pmean_done, pxc_done, psq_done, pstat_done, pstat_set, prinv_set, pr_done, pxn_done, qproj_done, kproj_done,
         qsquares_set, ksquares_set, raw_set, qr_done, qn_set, kr_done, ckn_set, keys_set, ckvT_done, ckv_set) = (
            sem(n) for n in ("pmean_done", "pxc_done", "psq_done", "pstat_done", "pstat_set", "prinv_set", "pr_done",
                             "pxn_done", "qproj_done", "kproj_done", "qsquares_set", "ksquares_set", "raw_set",
                             "qr_done", "qn_set", "kr_done", "ckn_set", "keys_set", "ckvT_done", "ckv_set"))
        prep_chain = sem("prep_chain")
        mw_done, mwh_set, mwl_set, rot_set, wo_done, woh_set, wol_set = (sem(n) for n in (
            "mw_done", "mwh_set", "mwl_set", "rot_set", "wo_done", "woh_set", "wol_set"))
        qp_done, qs_set, qu_set, qcos_set, q_set = (sem(n) for n in (
            "qp_done", "qs_set", "qu_set", "qcos_set", "q_set"))
        s_done, max_done, p_done, pT_done, pT_set, pv_done, o_done, oT_done, oTh_set, oTl_set = (
            sem(n) for n in ("s_done", "max_done", "p_done", "pT_done", "pT_set", "pv_done",
                             "o_done", "oT_done", "oTh_set", "oTl_set"))
        rsum_set, y_done, y_added = sem("rsum_set"), sem("y_done"), sem("y_added")
        piece_h, piece_l, sel_set = sem("piece_h"), sem("piece_l"), sem("sel_set")
        decay_exp, wkv_ready = sem("decay_exp"), sem("wkv_ready")
        mean_done, xc_done, sq_done, var_done, stat_set, rinv_set, r_done, xn_done = (sem(n) for n in (
            "mean_done", "xc_done", "sq_done", "var_done", "stat_set", "rinv_set", "r_done", "xn_done"))
        (kp_set, ww_set, pp_set, qmax_set, d1_set, d2_set, d3_set, d4_set, e1b_set, e2b_set, e1_set, e2_set, g_set, states_set, e2v_set,
         e1a_set, n_set, wkv_done) = (
            sem(n) for n in ("kp_set", "ww_set", "pp_set", "qmax_set", "d1_set", "d2_set", "d3_set", "d4_set", "e1b_set", "e2b_set", "e1_set",
                             "e2_set", "g_set", "states_set", "e2v_set", "e1a_set", "n_set", "wkv_done"))
        hh_set, hl_set, logit_done, lmax_set, lexp_set, cw_set, cT_done, cT_set = (sem(n) for n in (
            "hh_set", "hl_set", "logit_done", "lmax_set", "lexp_set", "cw_set", "cT_done", "cT_set"))
        primed = (gate_done, up_done, share_done, tanh_done, gated_done, mix_done, prod_done, acth_set, actl_set,
                  down_done, z_added) = [
            sem(n) for n in ("gate_done", "up_done", "share_done", "tanh_done", "gated_done", "mix_done",
                             "prod_done", "acth_set", "actl_set", "down_done", "z_added")]
        primed_set = sem("primed_set")
        wave_chain = sem("wave_chain")

        MEAN_BANK, STAT_BANK, R_BANK, RQ_BANK, P_BANK = 0, 1, 2, 3, 4
        S_BANK, PT_BANK, PV_BANK, OT_BANK, Q_BANK, Y_BANK = 0, 2, 3, 4, 5, 6
        WO_BANK, MW_BANK = Y_BANK, Y_BANK + 1
        G_BANK, U_BANK, C_BANK, Z_BANK, W_BANK = 0, 2, 4, 5, 7

        def bank(i):
            return ps[:, i, :]

        def toks(t):
            return bass.ds(t * CH, CH)

        def f32(ap):
            return ap.bitcast(F32)

        def over_b(ap):
            return ap.unsqueeze(1).to_broadcast([ap.shape[0], BC, S])

        def by_b(ap):
            return ap.rearrange("p (b s) -> p b s", s=S)

        def wtoks(w):
            return bass.ds(w * WT, WT)

        def held(w):
            return bass.ds((w % (2 * WAVES)) * WT, WT)

        def over_k(ap):
            return ap.unsqueeze(1).to_broadcast([ap.shape[0], KT, ap.shape[-1]])

        def now(eng, s, value):
            if not (isinstance(value, int) and value <= 0):
                eng.wait_ge(s, value)

        def over_groups(eng, body):
            body(0, True, False)
            with eng.Fori(1, NG - 1) as gi:
                body(gi, False, False)
            body(NG - 1, False, True)

        def stats_of(u):
            return slice(0 if u < NCH else BC, 3 * BC if u else BC)

        def wave_part(c, step):
            return WAVES * (c + 1) + step // PARTS, step % PARTS

        def over_chunks(eng, body):
            with eng.Fori(0, NCH - 1) as c:
                body(c, True)
            body(NCH - 1, False)

        def rotated(j):
            return raw_m[:, j, MCOL - 2 * DR:].rearrange("p (a c) -> p a c", a=2)

        def piece(n):
            kind, k, a, w, rows = PIECES[n]
            if kind == "gu":
                return stage[:, n % 2, 0:w], wguh[:, k, a:a + w], wgul[:, k, a:a + w]
            return (stage[0:rows, n % 2, 0:w * D], *(t[0:rows, a:a + w, :].rearrange("p f n -> p (f n)")
                                                     for t in (wdh, wdl)))

        block = stack.enter_context(nc.Block())

        @block.sync
        def _(sp):
            for t in range(NCH):
                sp.dma_start(x[:, :, toks(t)], xT_d[:, :, toks(t)]).then_inc(x_in[t], 16)
            for dst, src in ((qaw[:, :, :], qaw_d), (kvw[:, :, :], kvw_d), (lnw[:, 0:2], qaln_d),
                             (lnw[0:KVLR, 2:3], kvln_d), (rope[:, :, :], rope_d)):
                sp.dma_start(dst, src).then_inc(w_in, 16)
            for dst, src in ((ident[:, :], ident_d), (maskf[:, :], mask_d), (td[:, :], td_d),
                             (tf[:, :], tf_d), (wr[:, :, :], wr_d),
                             (low[:, :, :], low_d)):
                sp.dma_start(dst, src).then_inc(const_in, 16)

            def load_m(gi):
                sp.dma_start(raw_m[:, :, :].rearrange("p a b -> p (a b)"),
                             head_d[bass.ds(gi, 1), :, 0:HG * MCOL].rearrange("a p n -> (a p) n")
                             ).then_inc(raw_m_in, 16)

            def load_v(gi):
                sp.dma_start(raw_v[:, :, :].rearrange("p a b -> p (a b)"),
                             head_d[bass.ds(gi, 1), :, HG * MCOL:].rearrange("a p n -> (a p) n")
                             ).then_inc(raw_v_in, 16)

            load_m(0)
            load_v(0)
            with sp.Fori(1, NG) as gi:
                sp.wait_ge(mw_done, gi * HG)
                sp.wait_ge(rot_set, gi * HG)
                load_m(gi)
                sp.wait_ge(wo_done, gi * NP)
                load_v(gi)

            def load_v_wave(w):
                sp.dma_start(v[:, :, :].rearrange("p (k b) s -> p k (b s)", k=KT), ctx_d[:, :, wtoks(w)]
                             ).then_inc(v_in, 16)

            load_v_wave(0)
            sp.wait_ge(y_added, KT * NG * NCH)
            sp.dma_start(selraw[:, :], sel_d).then_inc(sel_in, 16)
            for n in range(len(PIECES)):
                if n >= 2:
                    sp.wait_ge(piece_l, n - 1)
                kind, k, a, w, rows = PIECES[n]
                if kind == "gu":
                    src, dst = wgu_d[128 * k:128 * k + 128, a:a + w], stage[:, n % 2, 0:w]
                else:
                    src = wd_d[128 * a:128 * a + rows * w, :].rearrange("(f p) n -> p f n", p=rows)
                    dst = stage[0:rows, n % 2, 0:w * D].rearrange("p (f n) -> p f n", n=D)
                sp.dma_start(dst, src).then_inc(stage_in[n % 2], 16)
            for w in range(1, WAVES):
                sp.wait_ge(wkv_done, w)
                load_v_wave(w)
            with sp.Fori(0, NCH - 1) as c:
                for i in range(WAVES):
                    w = WAVES * (c + 1) + i
                    sp.wait_ge(wkv_done, w)
                    load_v_wave(w)
                sp.wait_ge(z_added, KT * (c + 1) + 1)
                sp.dma_start(out_d[:, :, toks(c)], x[:, :, toks(c)]).then_inc(out_done, 16)
            sp.wait_ge(z_added, KT * NCH + 1)
            sp.dma_start(out_d[:, :, toks(NCH - 1)], x[:, :, toks(NCH - 1)]).then_inc(out_done, 16)
            sp.wait_ge(out_done, 16 * NCH)

        @block.gpsimd
        def _(pool):
            for s in primed:
                pool.sem_inc(s, 1)
            pool.memset(mean_w[:, :], 1.0 / D)
            pool.memset(power[:, :], -0.5)
            pool.memset(meanl_w[:, 0:1], 1.0 / QLR)
            pool.memset(meanl_w[:, 1:2], 1.0 / KVLR)
            pool.memset(epsr[:, 0:BC], LN_EPS)
            pool.memset(epsr[:, BC:], RMS_EPS)
            pool.memset(qs[:, :], 0.0)
            pool.memset(ckv[:, :, :], 1.0).then_inc(const_set, 1)

            for u in range(NCH + 1):
                cols = stats_of(u)
                pool.wait_ge(pstat_set, u + 1)
                pool.tensor_tensor(prinv[:, cols], pstat[:, cols], power[:, cols], ALU.pow).then_inc(prinv_set, 1)

            def rot_parts(head, j):
                pool.wait_ge(mwh_set, head + 1)
                pool.tensor_tensor(mwl[:, j, :, KVLR:], rotated(j), f32(mwh[:, j, :, KVLR:]), ALU.subtract
                                   ).then_inc(rot_set, 1)

            def times_sine(job):
                pool.wait_ge(qs_set, job + 1)
                now(pool, q_set, job)
                pool.tensor_tensor(by_b(qu[:, :]), by_b(qs[:, :]), over_b(rope[:, 1, :]), ALU.mult
                                   ).then_inc(qu_set, 1)

            for j in range(HG):
                rot_parts(j, j)
            for job in range(LEAD):
                times_sine(job)

            def pool_group(gi, first, last):
                for k in range(QUADS):
                    if k + LEAD < QUADS or not last:
                        times_sine(QUADS * gi + k + LEAD)
                    if k in MW_SLOTS and not last:
                        j = MW_SLOTS.index(k)
                        rot_parts(HG * gi + HG + j, j)

            over_groups(pool, pool_group)

            def inverse_deviation(w, i):
                pool.wait_ge(stat_set, 2 * w + i + 1)
                pool.tensor_tensor(rinv[:, :], stat[:, :], power[:, 0:WB], ALU.pow).then_inc(rinv_set, 1)

            def pool_part(w, part):
                if part in (1, 12):
                    inverse_deviation(w, part // 12)
                elif part == 3:
                    before, after = pp[:, :, 0:S], pp[:, :, 1:]
                    pool.wait_ge(pp_set, w + 1)
                    pool.tensor_tensor(e1b[:, :, 1:], before, after, ALU.subtract).then_inc(d1_set, 1)
                    pool.tensor_tensor(e2b[:, :, 1:], kp[:, :, 1:], after, ALU.subtract).then_inc(d2_set, 1)
                elif part == 5:
                    pool.wait_ge(v_in, 16 * (w + 1))
                    pool.wait_ge(e2b_set, w + 1)
                    pool.tensor_tensor(g[:, :, 1:], e2b[:, :, 1:], v[:, :, :], ALU.mult).then_inc(g_set, 1)
                elif part == 6:
                    pool.wait_ge(e2_set, w + 1)
                    pool.wait_ge(g_set, w + 1)
                    pool.tensor_tensor(v[:, :, :], e2[:, :, :], v[:, :, :], ALU.mult).then_inc(e2v_set, 1)
                elif part == 7:
                    pool.wait_ge(e1_set, w + 1)
                    pool.wait_ge(states_set, w + 1)
                    pool.tensor_tensor(g[:, :, 1:], e1[:, :, :], aa[:, :, 0:S], ALU.mult).then_inc(e1a_set, 1)
                elif part == 8:
                    pool.wait_ge(e1a_set, w + 1)
                    pool.tensor_tensor(g[:, :, 1:], g[:, :, 1:], v[:, :, :], ALU.add).then_inc(n_set, 1)
                elif part == 14:
                    pool.wait_ge(hh_set, w + 1)
                    pool.tensor_tensor(hl[:, :, held(w)], xw[:, :, :], f32(hh[:, :, held(w)]), ALU.subtract
                                       ).then_inc(hl_set, 1)

            def low_piece(n):
                raw, hi, lo = piece(n)
                pool.wait_ge(piece_h, n + 1)
                pool.tensor_tensor(lo, raw, f32(hi), ALU.subtract).then_inc(piece_l, 1)

            for w in range(WAVES):
                for part in range(PARTS):
                    pool_part(w, part)
                    if w * PARTS + part < len(PIECES):
                        low_piece(w * PARTS + part)

            def pool_chunk(c, waves):
                for f in range(FT):
                    w, n = fw(f), FT * c + f + 1
                    if waves:
                        pool_part(*wave_part(c, 2 * f))
                    pool.wait_ge(acth_set, n + 1)
                    pool.tensor_tensor(actl[0:w, f % 3, :], act_t[0:w, f % 2, :], f32(acth[0:w, f % 3, :]),
                                       ALU.subtract).then_inc(actl_set, 1)
                    if waves:
                        pool_part(*wave_part(c, 2 * f + 1))

            over_chunks(pool, pool_chunk)

        @block.vector
        def _(dve):
            linked = Linked(dve, prep_chain)
            link = linked.link

            dve.wait_ge(decay_exp, 1)
            link(dve.tensor_scalar(td[:, :], td[:, :], -1.0, None, ALU.mult))
            link(dve.memset(wdec[:, :, :], 0.0))
            for k in range(KT):
                real = wdec[:, WB * k:WB * (k + 1), 1:]
                dve.tensor_scalar(real, real, td[:, k:k + 1], None, ALU.add)
            dve.memset(wdec[:, :, 0:1], NEG)
            dve.memset(kp[:, :, 0:1], NEG)
            dve.memset(e1b[:, :, 0:1], 0.0)
            dve.memset(e2b[:, :, 0:1], 0.0)
            link(dve.memset(g[:, :, 0:1], 0.0))
            dve.sem_inc(wkv_ready, 1)

            def center_chunk(t):
                dve.wait_ge(pmean_done, t + 1)
                now(dve, kproj_done, t - 1)
                dve.tensor_tensor(xc[:, t % 2, :, :], x[:, :, toks(t)], over_k(bank(MEAN_BANK)), ALU.subtract
                                  ).then_inc(pxc_done, 1)

            def query_latent(t):
                dve.wait_ge(raw_set, t + 1)
                dve.wait_ge(qr_done, t + 1)
                r = bank(RQ_BANK)
                dve.scalar_tensor_tensor(pt1[:, :], raw[:, t % 2, 0, :], lnw[:, 0:1], r, ALU.mult, ALU.mult)
                link(dve.scalar_tensor_tensor(pt2[:, :], raw[:, t % 2, 1, :], lnw[:, 1:2], r, ALU.mult, ALU.mult))
                dve.tensor_copy(qn1h[:, toks(t)], pt1[:, :])
                link(dve.tensor_copy(qn2[:, toks(t)], pt2[:, :]))
                dve.tensor_tensor(qn1l[:, toks(t)], pt1[:, :], f32(qn1h[:, toks(t)]), ALU.subtract)
                low_rows = qn2[QR2:, toks(t)]
                link(dve.tensor_tensor(low_rows, pt2[QR2:, :], f32(low_rows), ALU.subtract))
                dve.sem_inc(qn_set, 1)

            def key_latent(t):
                dve.wait_ge(kr_done, t + 1)
                now(dve, ckvT_done, t)
                dve.scalar_tensor_tensor(ckn[:, :], raw[0:KVLR, t % 2, 2, :], lnw[0:KVLR, 2:3],
                                         bank(R_BANK)[0:KVLR, :], ALU.mult, ALU.mult).then_inc(ckn_set, 1)
                dve.tensor_tensor(by_b(pt1[KVLR:, :]), by_b(raw[KVLR:, t % 2, 2, :]), over_b(rope[KVLR:, 2, :]),
                                  ALU.mult)
                link(dve.tensor_tensor(by_b(pt2[KVLR:, :]), by_b(raw[KVLR:, t % 2, 3, :]), over_b(rope[KVLR:, 3, :]),
                                       ALU.mult))
                dve.tensor_scalar(ka[0:KVLR, toks(t)], ckn[:, :], SCALE, None, ALU.mult)
                link(dve.tensor_tensor(ka[KVLR:, toks(t)], pt1[KVLR:, :], pt2[KVLR:, :], ALU.add))
                dve.sem_inc(keys_set, 1)

            center_chunk(0)
            dve.wait_ge(w_in, 16 * 5)
            for u in range(NCH + 1):
                cols = stats_of(u)
                dve.wait_ge(pstat_done, u + 1)
                dve.tensor_tensor(pstat[:, cols], bank(STAT_BANK)[:, cols], epsr[:, cols], ALU.add
                                  ).then_inc(pstat_set, 1)
                if u < NCH:
                    dve.wait_ge(pr_done, u + 1)
                    dve.tensor_tensor(xc[:, u % 2, :, :], xc[:, u % 2, :, :], over_k(bank(R_BANK)), ALU.mult
                                      ).then_inc(pxn_done, 1)
                if u + 1 < NCH:
                    center_chunk(u + 1)
                if u:
                    query_latent(u - 1)
                    key_latent(u - 1)

            def mw_low(head, j):
                dve.wait_ge(mwh_set, head + 1)
                dve.tensor_tensor(mwl[:, j, :, 0:KVLR],
                                  bank(MW_BANK)[:, 0:2 * KVLR].rearrange("p (a c) -> p a c", a=2),
                                  f32(mwh[:, j, :, 0:KVLR]), ALU.subtract).then_inc(mwl_set, 1)

            def wo_low(pair, j):
                dve.wait_ge(woh_set, pair + 1)
                dve.tensor_tensor(wol[:, j, :], bank(WO_BANK)[:, 0:D], f32(woh[:, j, :]), ALU.subtract
                                  ).then_inc(wol_set, 1)

            def take_query(job, m):
                par = m // HG % 2
                dve.wait_ge(qs_set, job + 1)
                now(dve, s_done, HG * (m // HG) - HG + job - m)
                dve.tensor_tensor(by_b(qa[:, par, m % HG, :]), by_b(bank(Q_BANK)), over_b(rope[:, 0, :]), ALU.mult
                                  ).then_inc(qcos_set, 1)

            def add_sine(job, m):
                part = qa[KVLR:, m // HG % 2, m % HG, :]
                dve.wait_ge(qu_set, job + 1)
                dve.wait_ge(qcos_set, job + 1)
                dve.tensor_tensor(part, part, qu[KVLR:, :], ALU.add).then_inc(q_set, 1)

            def negative_max(n, m):
                dve.wait_ge(s_done, n + 1)
                now(dve, p_done, n - 1)
                dve.tensor_reduce(nmax[:, m % 2, :],
                                  bank(S_BANK + m % 2).rearrange("p (h k) -> p h k", h=HG),
                                  AX.X, ALU.max, negate=True).then_inc(max_done, 1)

            def normalise(n):
                pv = bank(PV_BANK)[:, 0:HG * (KVLR + 1)].rearrange("p (h c) -> p h c", h=HG)
                dve.wait_ge(pv_done, n + 1)
                dve.reciprocal(rsum[:, :], pv[:, :, KVLR]).then_inc(rsum_set, 1)
                dve.wait_ge(rsum_set, n + 1)
                now(dve, oT_done, n)
                dve.tensor_tensor(o[:, :, :], pv[:, :, 0:KVLR],
                                  rsum[:, :].unsqueeze(2).to_broadcast([128, HG, KVLR]), ALU.mult
                                  ).then_inc(o_done, 1)

            def outputs_low(n, m):
                par, b = m // BC % 2, m % BC
                dve.wait_ge(oTh_set, n + 1)
                dve.tensor_tensor(oTl[:, par, :, b * S:b * S + S],
                                  bank(OT_BANK)[:, 0:NP * S].rearrange("p (a s) -> p a s", a=NP),
                                  f32(oTh[:, par, :, b * S:b * S + S]), ALU.subtract).then_inc(oTl_set, 1)

            def add_outputs(it, c):
                for m in range(KT):
                    dve.wait_ge(y_done, KT * it + m + 1)
                    dve.tensor_tensor(x[:, m, toks(c)], x[:, m, toks(c)], bank(Y_BANK + m), ALU.add
                                      ).then_inc(y_added, 1)

            for j in range(HG):
                mw_low(j, j)
            for job in range(LEAD - 1):
                take_query(job, job)
                add_sine(job, job)
            negative_max(0, 0)

            def dve_group(gi, first, last):
                for k in range(QUADS):
                    n = QUADS * gi + k
                    if k or not first:
                        normalise(n - 1)
                    more = k + LEAD - 1 < QUADS or not last
                    if more:
                        take_query(n + LEAD - 1, k + LEAD - 1)
                    if k + 1 < QUADS or not last:
                        negative_max(n + 1, k + 1)
                    if more:
                        add_sine(n + LEAD - 1, k + LEAD - 1)
                    if k or not first:
                        outputs_low(n - 1, k - 1 + QUADS)
                    if k % BC == 1 and (k > 1 or not first):
                        add_outputs(NCH * gi + k // BC - 1, (k // BC - 1) % NCH)
                    if k in WO_SLOTS:
                        j = WO_SLOTS.index(k)
                        wo_low(NP * gi + j, j)
                    if k in MW_SLOTS and not last:
                        j = MW_SLOTS.index(k)
                        mw_low(HG * gi + HG + j, j)

            over_groups(dve, dve_group)
            normalise(NG * QUADS - 1)
            outputs_low(NG * QUADS - 1, QUADS - 1)
            add_outputs(NG * NCH - 1, NCH - 1)

            wave = Linked(dve, wave_chain)

            def flat(a):
                return a[:, :, :].rearrange("p a b -> p (a b)")

            def ktile(a, k):
                return a[:, WB * k:WB * (k + 1), :]

            def over_e(ap):
                return ap.unsqueeze(2).to_broadcast([128, WB, E])

            def center(w, i):
                now(dve, hl_set, w)
                dve.wait_ge(mean_done, 2 * w + i + 1)
                dve.tensor_tensor(xw[:, :, :], x[:, :, wtoks(w)], over_k(bank(W_BANK)[:, 0:WT]), ALU.subtract
                                  ).then_inc(xc_done, 1)

            def variance(w, i):
                dve.wait_ge(var_done, 2 * w + i + 1)
                dve.tensor_scalar(stat[:, :], bank(W_BANK)[:, 0:WB], LN_EPS, None, ALU.add).then_inc(stat_set, 1)

            def running_maximum(w):
                dve.wait_ge(r_done, 2 * w + 1)
                for k in range(KT):
                    last = dve.tensor_tensor(ktile(kp, k)[:, :, 1:], by_b(xw[:, k, :]), by_b(bank(W_BANK)[:, 0:WT]),
                                             ALU.mult)
                last.then_inc(kp_set, 1)
                dve.wait_ge(kp_set, w + 1)
                dve.tensor_tensor_scan(flat(pp), flat(wdec), flat(kp), NEG, ALU.add, ALU.max).then_inc(pp_set, 1)

            def output_maximum(w):
                dve.wait_ge(ww_set, w + 1)
                dve.wait_ge(pp_set, w + 1)
                dve.tensor_tensor(qq[:, :, :], e2[:, :, :], pp[:, :, 0:S], ALU.max).then_inc(qmax_set, 1)
                dve.wait_ge(qmax_set, w + 1)
                dve.tensor_tensor(e1[:, :, :], pp[:, :, 0:S], qq[:, :, :], ALU.subtract).then_inc(d3_set, 1)

            def denominator_state(w):
                dve.tensor_tensor(e2[:, :, :], e2[:, :, :], qq[:, :, :], ALU.subtract).then_inc(d4_set, 1)
                dve.wait_ge(e1b_set, w + 1)
                dve.wait_ge(e2b_set, w + 1)
                wave.link(dve.tensor_tensor_scan(flat(bb), flat(e1b), flat(e2b), 0.0, ALU.mult, ALU.add))

            def numerator_state(w):
                dve.wait_ge(g_set, w + 1)
                dve.tensor_tensor_scan(flat(aa), flat(e1b), flat(g), 0.0, ALU.mult, ALU.add).then_inc(states_set, 1)

            def denominator(w):
                dve.wait_ge(e1_set, w + 1)
                dve.wait_ge(e2_set, w + 1)
                wave.link(dve.tensor_tensor(qq[:, :, :], e1[:, :, :], bb[:, :, 0:S], ALU.mult))
                wave.link(dve.tensor_tensor(qq[:, :, :], qq[:, :, :], e2[:, :, :], ALU.add))

            def add_wkv(w):
                dve.wait_ge(n_set, w + 1)
                wave.link(dve.tensor_tensor(e1[:, :, :], g[:, :, 1:], qq[:, :, :], ALU.mult))
                for k in range(KT):
                    xs = by_b(x[:, k, wtoks(w)])
                    last = dve.tensor_tensor(xs, xs, ktile(e1, k), ALU.add)
                last.then_inc(wkv_done, 1)

            def logits(w):
                dve.wait_ge(logit_done, w + 1)
                wave.link(dve.tensor_copy(lg[:, :, :],
                                          bank(W_BANK)[:, 0:WB * NR].rearrange("p (b e) -> p b e", e=NR)))
                wave.link(dve.tensor_reduce(rt[:, 0, :], lg[:, :, 0:E], AX.X, ALU.max))
                dve.tensor_tensor(pr[:, :, :], lg[:, :, 0:E], over_e(rt[:, 0, :]), ALU.subtract).then_inc(lmax_set, 1)

            def choose(w):
                dve.wait_ge(lexp_set, w + 1)
                wave.link(dve.tensor_reduce(rt[:, 1, :], pr[:, :, :], AX.X, ALU.add))
                wave.link(dve.reciprocal(rt[:, 1, :], rt[:, 1, :]))
                wave.link(dve.tensor_tensor(pr[:, :, :], pr[:, :, :], over_e(rt[:, 1, :]), ALU.mult))
                other = pr[:, :, :].unsqueeze(2).to_broadcast([128, WB, E, E])
                own = pr[:, :, :].unsqueeze(3).to_broadcast([128, WB, E, E])
                dve.tensor_tensor(gt[:, :, :, :], other, own, ALU.is_gt)
                wave.link(dve.tensor_tensor(eq[:, :, :, :], other, own, ALU.is_equal))
                wave.link(dve.tensor_tensor(eq[:, :, :, :], eq[:, :, :, :],
                                            low[:, :, :].unsqueeze(1).to_broadcast([128, WB, E, E]), ALU.mult))
                wave.link(dve.tensor_tensor(gt[:, :, :, :], gt[:, :, :, :], eq[:, :, :, :], ALU.add))
                dve.tensor_scalar(cw[:, :, E], lg[:, :, E], 1.0, None, ALU.add)
                wave.link(dve.tensor_reduce(rank[:, :, :], gt[:, :, :, :], AX.X, ALU.add))
                dve.scalar_tensor_tensor(cw[:, :, 0:E], rank[:, :, :], TOPK - 0.5, pr[:, :, :], ALU.is_lt, ALU.mult)
                wave.link(dve.reciprocal(cw[:, :, E], cw[:, :, E]))
                wave.link(dve.tensor_copy(cwp[:, :, 0:NR], cw[:, :, :]))
                dve.tensor_tensor(cwp[:, :, NR:], cw[:, :, :], f32(cwp[:, :, 0:NR]), ALU.subtract).then_inc(cw_set, 1)

            def dve_part(w, part):
                if part == 0:
                    wave.start(LINKS * w)
                if part in (0, 11):
                    center(w, part // 11)
                elif part in (1, 12):
                    variance(w, part // 12)
                elif part == 2:
                    running_maximum(w)
                elif part == 4:
                    output_maximum(w)
                elif part == 5:
                    denominator_state(w)
                elif part == 6:
                    denominator(w)
                    numerator_state(w)
                elif part in (7, 9):
                    half = ktile(qq, part // 9)
                    wave.link(dve.reciprocal(half, half))
                elif part == 10:
                    add_wkv(w)
                elif part == 13:
                    dve.wait_ge(r_done, 2 * w + 2)
                    dve.tensor_tensor(xw[:, :, :], xw[:, :, :], over_k(bank(W_BANK)[:, 0:WT]), ALU.mult
                                      ).then_inc(xn_done, 1)
                elif part == 14:
                    logits(w)
                elif part == 15:
                    choose(w)
                    assert wave.made == LINKS, wave.made

            for w in range(WAVES):
                for part in range(PARTS):
                    dve_part(w, part)
            dve.wait_ge(sel_in, 16)
            dve.tensor_copy(sel[:, :], selraw[:, :]).then_inc(sel_set, 1)

            def dve_chunk(c, waves):
                for f in range(FT):
                    w, n, free = fw(f), FT * c + f + 1, FT * c + max(f - 1, 0) + 1
                    part = act_t[0:w, f % 2, :]
                    dve.wait_ge(tanh_done, n + 1)
                    dve.wait_ge(actl_set, free)
                    dve.scalar_tensor_tensor(part, act_s[0:w, f % 2, :], 1.0, bank(G_BANK + f % 2)[0:w, :],
                                             ALU.add, ALU.mult).then_inc(gated_done, 1)
                    if waves:
                        dve_part(*wave_part(c, 2 * f))
                    dve.wait_ge(up_done, n + 1)
                    dve.wait_ge(gated_done, n + 1)
                    dve.tensor_tensor(part, part, bank(U_BANK + f % 2)[0:w, :], ALU.mult).then_inc(mix_done, 1)
                    dve.wait_ge(share_done, n + 1)
                    dve.wait_ge(mix_done, n + 1)
                    dve.scalar_tensor_tensor(part, part, 0.5, bank(C_BANK)[0:w, :], ALU.mult, ALU.mult
                                             ).then_inc(prod_done, 1)
                    if waves:
                        dve_part(*wave_part(c, 2 * f + 1))
                dve.wait_ge(down_done, FT * (c + 1) + 1)
                for m in range(KT):
                    dve.tensor_tensor(x[:, m, toks(c)], x[:, m, toks(c)], bank(Z_BANK + m), ALU.add
                                      ).then_inc(z_added, 1)

            over_chunks(dve, dve_chunk)

        @block.scalar
        def _(act):
            act.wait_ge(const_in, 16 * 6)
            act.activation(maskb[:, :], maskf[:, :], ACT.Copy)
            act.activation(identb[:, :], ident[:, :], ACT.Copy).then_inc(cast_set, 1)
            act.activation(td[:, :], td[:, :], ACT.Exp).then_inc(decay_exp, 1)
            act.wait_ge(const_set, 1)

            def square_chunk(t):
                act.wait_ge(pxc_done, t + 1)
                now(act, pstat_done, t)
                act.activation(sq[:, :, :], xc[:, t % 2, :, :], ACT.Square).then_inc(psq_done, 1)

            square_chunk(0)
            for u in range(NCH + 2):
                if u >= 2:
                    t = u - 2
                    act.wait_ge(ckvT_done, t + 1)
                    act.activation(ckv[:, BC * t:BC * (t + 1), 0:KVLR],
                                   bank(RQ_BANK)[:, 0:BC * KVLR].rearrange("p (b c) -> p b c", c=KVLR), ACT.Copy
                                   ).then_inc(ckv_set, 1)
                if u + 1 < NCH:
                    square_chunk(u + 1)
                if u < NCH:
                    now(act, keys_set, u - 1)
                    now(act, qn_set, u - 1)
                    act.wait_ge(qproj_done, u + 1)
                    act.wait_ge(pstat_done, u + 1)
                    act.activation(sqp[:, 0:2, :], ps[:, P_BANK:P_BANK + 2, :], ACT.Square).then_inc(qsquares_set, 1)
                    act.activation(raw[:, u % 2, 0:2, :], ps[:, P_BANK:P_BANK + 2, :], ACT.Copy)
                    act.wait_ge(kproj_done, u + 1)
                    act.activation(sqp[:, 2, :], bank(P_BANK + 2), ACT.Square).then_inc(ksquares_set, 1)
                    act.activation(raw[:, u % 2, 2:4, :], ps[:, P_BANK + 2:P_BANK + 4, :], ACT.Copy
                                   ).then_inc(raw_set, 1)

            def mw_high(head, j, freed):
                act.wait_ge(mw_done, head + 1)
                now(act, qp_done, freed)
                act.activation(mwh[:, j, :, 0:KVLR],
                               bank(MW_BANK)[:, 0:2 * KVLR].rearrange("p (a c) -> p a c", a=2), ACT.Copy)
                act.activation(mwh[:, j, :, KVLR:], rotated(j), ACT.Copy).then_inc(mwh_set, 1)

            def wo_high(pair, j, freed):
                act.wait_ge(wo_done, pair + 1)
                now(act, y_done, freed)
                act.activation(woh[:, j, :], bank(WO_BANK)[:, 0:D], ACT.Copy).then_inc(woh_set, 1)

            def exponentials(n, m):
                act.wait_ge(max_done, n + 1)
                now(act, pT_done, n - 1)
                for hd in range(HG):
                    last = act.activation(p[:, m % 2, hd, :], bank(S_BANK + m % 2)[:, hd * S:hd * S + S], ACT.Exp,
                                          bias=nmax[:, m % 2, hd:hd + 1])
                last.then_inc(p_done, 1)

            def probs_out(n):
                act.wait_ge(pT_done, n + 1)
                now(act, pv_done, n)
                act.activation(pT[:, :, :].rearrange("p h q -> p (h q)"), bank(PT_BANK), ACT.Copy
                               ).then_inc(pT_set, 1)

            def outputs_high(n, m, it):
                par, b = m // BC % 2, m % BC
                act.wait_ge(oT_done, n + 1)
                now(act, y_done, KT * (it - 1))
                act.activation(oTh[:, par, :, b * S:b * S + S],
                               bank(OT_BANK)[:, 0:NP * S].rearrange("p (a s) -> p a s", a=NP), ACT.Copy
                               ).then_inc(oTh_set, 1)

            def swap_halves(job):
                half = DR // 2
                act.wait_ge(qp_done, job + 1)
                now(act, qu_set, job)
                act.activation(qs[KVLR:KVLR + half, :], bank(Q_BANK)[KVLR + half:, :], ACT.Copy)
                act.activation(qs[KVLR + half:, :], bank(Q_BANK)[KVLR:KVLR + half, :], ACT.Copy).then_inc(qs_set, 1)

            for j in range(HG):
                mw_high(j, j, 0)
            for job in range(LEAD):
                swap_halves(job)
            exponentials(0, 0)

            def act_group(gi, first, last):
                for k in range(QUADS):
                    n = QUADS * gi + k
                    probs_out(n)
                    if k + 1 < QUADS or not last:
                        exponentials(n + 1, k + 1)
                    if k or not first:
                        outputs_high(n - 1, k - 1 + QUADS, NCH * gi + (k - 1) // BC)
                    if k + LEAD < QUADS or not last:
                        swap_halves(n + LEAD)
                    if k in WO_SLOTS:
                        j = WO_SLOTS.index(k)
                        wo_high(NP * gi + j, j, KT * NCH * gi)
                    if k in MW_SLOTS and not last:
                        j = MW_SLOTS.index(k)
                        mw_high(HG * gi + HG + j, j, QUADS * gi + QUADS - HG + j + 1)

            over_groups(act, act_group)
            outputs_high(NG * QUADS - 1, QUADS - 1, NG * NCH - 1)

            def square(w, i):
                act.wait_ge(xc_done, 2 * w + i + 1)
                act.activation(sqw[:, :, :], xw[:, :, :], ACT.Square).then_inc(sq_done, 1)

            def exp_of(a, ready, done, w):
                act.wait_ge(ready, w + 1)
                act.activation(a, a, ACT.Exp).then_inc(done, 1)

            def act_part(w, part):
                if part in (0, 11):
                    square(w, part // 11)
                elif part == 3:
                    act.wait_ge(kp_set, w + 1)
                    for k in range(KT):
                        rows = slice(WB * k, WB * (k + 1))
                        last = act.activation(e2[:, rows, :], kp[:, rows, 1:], ACT.Identity, bias=tf[:, k:k + 1])
                    last.then_inc(ww_set, 1)
                elif part == 4:
                    act.wait_ge(d1_set, w + 1)
                    for k in range(KT):
                        a = e1b[:, WB * k:WB * (k + 1), 1:]
                        last = act.activation(a, a, ACT.Exp, bias=td[:, k:k + 1])
                    last.then_inc(e1b_set, 1)
                    exp_of(e2b[:, :, 1:], d2_set, e2b_set, w)
                elif part == 5:
                    exp_of(e1[:, :, :], d3_set, e1_set, w)
                    exp_of(e2[:, :, :], d4_set, e2_set, w)
                elif part == 13:
                    act.wait_ge(xn_done, w + 1)
                    act.activation(hh[:, :, held(w)], xw[:, :, :], ACT.Copy).then_inc(hh_set, 1)
                elif part == 14:
                    act.wait_ge(lmax_set, w + 1)
                    act.activation(pr[:, :, :], pr[:, :, :], ACT.Exp)
                    act.activation(lg[:, :, E], lg[:, :, E], ACT.Exp, scale=-1.0).then_inc(lexp_set, 1)
                elif part == 16:
                    act.wait_ge(cT_done, w + 1)
                    act.activation(cT[:, held(w)], bank(W_BANK)[0:2 * NR, 0:WT], ACT.Copy).then_inc(cT_set, 1)

            def high_piece(n):
                raw, hi, _ = piece(n)
                act.wait_ge(stage_in[n % 2], 16 * (n // 2 + 1))
                act.activation(hi, raw, ACT.Copy).then_inc(piece_h, 1)

            act.wait_ge(wkv_ready, 1)
            for w in range(WAVES):
                for part in range(PARTS):
                    act_part(w, part)
                    if w * PARTS + part < len(PIECES):
                        high_piece(w * PARTS + part)

            def act_chunk(c, waves):
                for f in range(FT):
                    w, n, free = fw(f), FT * c + f + 1, FT * c + max(f - 1, 0) + 1
                    act.wait_ge(gate_done, n + 1)
                    act.wait_ge(gated_done, free)
                    act.activation(act_s[0:w, f % 2, :], bank(G_BANK + f % 2)[0:w, :], ACT.Tanh, scale=0.5
                                   ).then_inc(tanh_done, 1)
                    if waves:
                        act_part(*wave_part(c, 2 * f))
                    act.wait_ge(down_done, FT * c + max(f - 2, 0) + 1)
                    act.wait_ge(prod_done, n + 1)
                    act.activation(acth[0:w, f % 3, :], act_t[0:w, f % 2, :], ACT.Copy).then_inc(acth_set, 1)
                    if waves:
                        act_part(*wave_part(c, 2 * f + 1))

            over_chunks(act, act_chunk)

        @block.tensor
        def _(pe):
            def mm(out, lhsT, rhs, start, stop, **kw):
                return pe.matmul(out, lhsT, rhs, start=start, stop=stop, **kw)

            def mm3(out, wh, wl, rh, rl, start=True, stop=True):
                mm(out, wh, rh, start, False)
                mm(out, wh, rl, False, False)
                return mm(out, wl, rh, False, stop)

            def mean_of(out, src):
                for k in range(KT):
                    last = mm(out, mean_w[:, :], src(k), k == 0, k == KT - 1)
                return last

            def means(t):
                pe.wait_ge(x_in[t], 16)
                now(pe, pxc_done, t)
                mean_of(bank(MEAN_BANK), lambda k: x[:, k, toks(t)]).then_inc(pmean_done, 1)

            def mean_squares(b, col, parts):
                for i, (src, w) in enumerate(parts):
                    last = mm(bank(STAT_BANK)[:, col + b:col + b + 1], src[:, b * S:(b + 1) * S], w,
                              i == 0, i == len(parts) - 1)
                return last

            def statistics(u):
                now(pe, pstat_set, u)
                for b in range(BC):
                    if u < NCH:
                        pe.wait_ge(psq_done, u + 1)
                        last = mean_squares(b, 0, [(sq[:, k, :], mean_w[:, 0:1]) for k in range(KT)])
                for b in range(BC):
                    if u:
                        pe.wait_ge(ksquares_set, u)
                        pe.wait_ge(qsquares_set, u)
                        mean_squares(b, BC, [(sqp[:, 0, :], meanl_w[:, 0:1]), (sqp[0:QR2, 1, :], meanl_w[0:QR2, 0:1])])
                        last = mean_squares(b, 2 * BC, [(sqp[0:KVLR, 2, :], meanl_w[0:KVLR, 1:2])])
                last.then_inc(pstat_done, 1)

            def spread_chunk(out, col):
                for b in range(BC):
                    last = mm(out[:, b * S:(b + 1) * S], prinv[:, col + b:col + b + 1].to_broadcast([128, 128]),
                              ident[:, :], True, True)
                return last

            def project(u, weights, i):
                for j in range(2):
                    for k in range(KT):
                        last = mm(bank(P_BANK + i + j), weights[:, k, 128 * j:128 * (j + 1)], xc[:, u % 2, k, :],
                                  k == 0, k == KT - 1)
                return last

            pe.wait_ge(const_set, 1)
            means(0)
            for u in range(NCH + 2):
                if u <= NCH:
                    statistics(u)
                if u >= 2:
                    t = u - 2
                    pe.wait_ge(ckn_set, t + 1)
                    pe.wait_ge(qn_set, t + 1)
                    for b in range(BC):
                        last = pe.transpose(bank(RQ_BANK)[:, b * KVLR:(b + 1) * KVLR], ckn[:, b * S:(b + 1) * S],
                                            ident[0:KVLR, 0:KVLR])
                    last.then_inc(ckvT_done, 1)
                if u + 1 < NCH:
                    means(u + 1)
                if u == 0:
                    pe.wait_ge(const_in, 16 * 6)
                    pe.wait_ge(w_in, 16 * 5)
                if u <= NCH:
                    pe.wait_ge(prinv_set, u + 1)
                if u < NCH:
                    now(pe, ckn_set, u - 1)
                    spread_chunk(bank(R_BANK), 0).then_inc(pr_done, 1)
                if 0 < u <= NCH:
                    now(pe, ckv_set, u - 1)
                    spread_chunk(bank(RQ_BANK), BC).then_inc(qr_done, 1)
                if u < NCH:
                    pe.wait_ge(pxn_done, u + 1)
                    now(pe, raw_set, u)
                    project(u, qaw, 0).then_inc(qproj_done, 1)
                    project(u, kvw, 2).then_inc(kproj_done, 1)
                if 0 < u <= NCH:
                    spread_chunk(bank(R_BANK), 2 * BC).then_inc(kr_done, 1)

            def absorb_queries(head, j, gi, projected):
                pe.wait_ge(raw_m_in, 16 * (gi + 1))
                now(pe, mwl_set, head)
                now(pe, y_added, KT * projected)
                keys = raw_m[:, j, 128 + 2 * QR2:128 + 2 * QR2 + KVLR]
                for a in range(2):
                    last = mm(bank(MW_BANK)[:, a * KVLR:(a + 1) * KVLR],
                              raw_m[:, j, 128 * a:128 * (a + 1)], keys, True, True)
                last.then_inc(mw_done, 1)

            def absorb_outputs(pair, j, gi, projected):
                pe.wait_ge(raw_v_in, 16 * (gi + 1))
                now(pe, wol_set, pair)
                now(pe, y_added, KT * projected)
                for a in range(2):
                    last = mm(bank(WO_BANK)[a * KVLR:(a + 1) * KVLR, 0:D], raw_v[:, 2 * j + a, 0:KVLR],
                              raw_v[:, 2 * j + a, KVLR:], True, True)
                last.then_inc(wo_done, 1)

            def queries(job, m, gi):
                c, j = m // HG % NCH, m % HG
                pe.wait_ge(mwl_set, HG * gi + j + 1)
                pe.wait_ge(rot_set, HG * gi + j + 1)
                now(pe, qcos_set, job)
                out = bank(Q_BANK)
                mm3(out, mwh[:, j, 0, :], mwl[:, j, 0, :], qn1h[:, toks(c)], qn1l[:, toks(c)], True, False)
                mm(out, mwh[:, j, 1, :], qn2[:, toks(c)], False, False)
                mm(out, mwl[0:QR2, j, 1, :], qn2[0:QR2, toks(c)], False, True).then_inc(qp_done, 1)

            def scores(n, m, jobs):
                par, b = m // BC % 2, m % BC
                key = bass.ds((m % QUADS) * S, S)
                now(pe, p_done, n - 1)
                pe.wait_ge(q_set, jobs)
                out = bank(S_BANK + m % 2)
                mm(out, identb[:, :], maskb[:, :].unsqueeze(1).to_broadcast([128, HG, S]), True, True)
                for j in range(HG):
                    part = out[:, j * S:(j + 1) * S]
                    last = mm(part, qa[:, par, j, b * S:(b + 1) * S], ka[:, key], False, True,
                              skip_group_check=True)
                last.then_inc(s_done, 1)

            def transpose_probs(n, m):
                pe.wait_ge(p_done, n + 1)
                now(pe, pT_set, n)
                for j in range(HG):
                    last = pe.transpose(bank(PT_BANK)[:, j * S:(j + 1) * S], p[:, m % 2, j, :], ident[:, :])
                last.then_inc(pT_done, 1)

            def weigh_values(n, m):
                pe.wait_ge(pT_set, n + 1)
                now(pe, o_done, n)
                for j in range(HG):
                    last = mm(bank(PV_BANK)[:, j * (KVLR + 1):(j + 1) * (KVLR + 1)], pT[:, j, :],
                              ckv[:, m % QUADS, :], True, True)
                last.then_inc(pv_done, 1)

            def transpose_outputs(n):
                pe.wait_ge(o_done, n + 1)
                now(pe, oTl_set, n)
                for a in range(NP):
                    last = pe.transpose(bank(OT_BANK)[:, a * S:(a + 1) * S],
                                        o[:, 2 * a:2 * a + 2, :].rearrange("p h c -> p (h c)"), ident[:, :])
                last.then_inc(oT_done, 1)

            def project_outputs(it, par, gi, heads):
                pe.wait_ge(oTl_set, BC * (it + 1))
                pe.wait_ge(wol_set, NP * (gi + 1))
                pe.wait_ge(mwl_set, heads)
                for m in range(KT):
                    now(pe, y_added, KT * (it - 1) + m + 1)
                    cols = slice(128 * m, 128 * (m + 1))
                    for a in range(NP):
                        last = mm3(bank(Y_BANK + m), woh[:, a, cols], wol[:, a, cols], oTh[:, par, a, :],
                                   oTl[:, par, a, :], a == 0, a == NP - 1)
                    last.then_inc(y_done, 1)

            pe.wait_ge(ckv_set, NCH)
            pe.wait_ge(keys_set, NCH)
            pe.wait_ge(raw_set, NCH)
            pe.wait_ge(cast_set, 1)
            for j in range(HG):
                absorb_queries(j, j, 0, 0)
            for job in range(LEAD):
                queries(job, job, 0)
            scores(0, 0, HG)

            def pe_group(gi, first, last):
                for k in range(QUADS):
                    n = QUADS * gi + k
                    if k + 1 < QUADS or not last:
                        scores(n + 1, k + 1, n - k + (k + 1) // BC * HG + HG)
                    transpose_probs(n, k)
                    if k or not first:
                        transpose_outputs(n - 1)
                    if k % BC == 1 and (k > 1 or not first):
                        it = NCH * gi + k // BC - 1
                        absorbed = 0 if last else len([j for j in MW_SLOTS if j < k])
                        project_outputs(it, (k // BC + 1) % 2, gi if k > 1 else gi - 1, HG * (gi + 1) + absorbed)
                    if k + LEAD < QUADS or not last:
                        queries(n + LEAD, k + LEAD, gi + (k + LEAD) // QUADS)
                    weigh_values(n, k)
                    projected = NCH * gi + (k - 1) // BC
                    if k in WO_SLOTS:
                        j = WO_SLOTS.index(k)
                        absorb_outputs(NP * gi + j, j, gi, projected)
                    if k in MW_SLOTS and not last:
                        j = MW_SLOTS.index(k)
                        absorb_queries(HG * gi + HG + j, j, gi + 1, projected)

            over_groups(pe, pe_group)
            transpose_outputs(NG * QUADS - 1)
            project_outputs(NG * NCH - 1, (NCH - 1) % 2, NG - 1, NH)

            def variances(w, i):
                pe.wait_ge(sq_done, 2 * w + i + 1)
                for b in range(WB):
                    for k in range(KT):
                        last = mm(bank(W_BANK)[:, b:b + 1], sqw[:, k, b * S:(b + 1) * S], mean_w[:, 0:1],
                                  k == 0, k == KT - 1)
                last.then_inc(var_done, 1)

            def spread(w, i):
                pe.wait_ge(rinv_set, 2 * w + i + 1)
                for b in range(WB):
                    last = mm(bank(W_BANK)[:, b * S:(b + 1) * S], rinv[:, b:b + 1].to_broadcast([128, 128]),
                              ident[:, :], True, True)
                last.then_inc(r_done, 1)

            def pe_part(w, part):
                if part in (0, 11):
                    if part == 0:
                        now(pe, cT_set, w)
                    else:
                        pe.wait_ge(wkv_done, w + 1)
                    mean_of(bank(W_BANK)[:, 0:WT], lambda k: x[:, k, wtoks(w)]).then_inc(mean_done, 1)
                elif part in (1, 12):
                    variances(w, part // 12)
                elif part in (2, 13):
                    spread(w, part // 13)
                elif part == 14:
                    pe.wait_ge(xn_done, w + 1)
                    for b in range(WB):
                        for k in range(KT):
                            last = mm(bank(W_BANK)[:, b * NR:(b + 1) * NR], xw[:, k, b * S:(b + 1) * S], wr[:, k, :],
                                      k == 0, k == KT - 1)
                    last.then_inc(logit_done, 1)
                elif part == 16:
                    pe.wait_ge(cw_set, w + 1)
                    for b in range(WB):
                        last = pe.transpose(bank(W_BANK)[0:2 * NR, b * S:(b + 1) * S], f32(cwp[:, b, :]),
                                            ident[:, :])
                    last.then_inc(cT_done, 1)

            pe.wait_ge(y_added, KT * NG * NCH)
            for w in range(WAVES):
                for part in range(PARTS):
                    pe_part(w, part)

            pe.wait_ge(piece_l, len(PIECES))
            pe.wait_ge(piece_h, len(PIECES))
            pe.wait_ge(sel_set, 1)

            def hidden(out, col, w, c, ks=range(KT)):
                now_c = bass.ds((c % 2) * CH, CH)
                for k in ks:
                    last = mm3(out, wguh[:, k, col:col + w], wgul[:, k, col:col + w], hh[:, k, now_c],
                               hl[:, k, now_c], k == 0, k == KT - 1)
                return last

            def share(f, c):
                mm(bank(C_BANK), sel[:, 128 * f:128 * (f + 1)], cT[:, bass.ds((c % 2) * CH, CH)], True, True
                   ).then_inc(share_done, 1)

            def down(n, f, share_free=None):
                w = fw(f)
                pe.wait_ge(actl_set, n + 1)
                for m in range(KT):
                    if m == KT - 1 and share_free is not None:
                        pe.wait_ge(prod_done, share_free)
                    cols = slice(128 * m, 128 * (m + 1))
                    last = mm3(bank(Z_BANK + m), wdh[0:w, f, cols], wdl[0:w, f, cols], acth[0:w, f % 3, :],
                               actl[0:w, f % 3, :], f == 0, f == FT - 1)
                last.then_inc(down_done, 1)

            def banks_free(n, f):
                pe.wait_ge(mix_done, n - f + max(f - 1, 0))

            def pe_chunk(c, waves):
                for f in range(FT):
                    w, n = fw(f), FT * c + f + 1
                    if f == 0:
                        pe.wait_ge(hl_set, WAVES * (c + 1))
                    if f < FT - 1:
                        banks_free(n, f)
                    up = bank(U_BANK + f % 2)[0:w, :]
                    hidden(bank(G_BANK + f % 2)[0:w, :], 128 * f, w, c).then_inc(gate_done, 1)
                    hidden(up, FF + 128 * f, w, c, range(1))
                    if waves:
                        pe_part(*wave_part(c, 2 * f))
                    if f < 2:
                        pe.wait_ge(prod_done, n)
                    hidden(up, FF + 128 * f, w, c, range(1, KT)).then_inc(up_done, 1)
                    if f == FT - 2:
                        banks_free(n + 1, f + 1)
                    if f == 2:
                        pe.wait_ge(z_added, KT * c + 1)
                    if f == 0:
                        pe.wait_ge(cT_set, WAVES * (c + 1))
                    if f >= 2:
                        down(n - 2, f - 2, n)
                    share(f, c)
                    if waves:
                        pe_part(*wave_part(c, 2 * f + 1))
                for f in (FT - 2, FT - 1):
                    down(FT * c + f + 1, f)

            over_chunks(pe, pe_chunk)


def _tables():
    inv = (1.0 / np.float32(10000.0) ** (np.arange(0, DR, 2, dtype=np.float32) / np.float32(DR))).astype(np.float32)
    ang = np.arange(S, dtype=np.float32)[None, :] * inv[:, None]
    cos, sin, one = np.cos(ang), np.sin(ang), np.ones((DR, S), np.float32)
    sc = np.float32(SCALE)
    rope = np.stack([np.concatenate([one, cos, cos]), np.concatenate([one, -sin, sin]),
                     np.concatenate([one, cos * sc, cos * sc]), np.concatenate([one, -sin * sc, sin * sc])], 1)
    expert = np.concatenate([np.repeat(np.arange(E), FE), np.full(FS, E), np.full(FT * 128 - FF, -1)])
    sel = (np.arange(2 * NR)[:, None] % NR == expert[None, :]).astype(np.float32)
    pos = np.arange(S)
    mask = np.where(pos[None, :] > pos[:, None], np.float32(NEG), np.float32(0)).astype(np.float32)
    order = np.arange(E)
    low = np.broadcast_to((order[None, :] < order[:, None]).astype(np.float32), (128, E, E))
    return (rope.astype(np.float32), mask, np.eye(128, dtype=np.float32), low, sel)


def kernel(x, ctx_2048, L0_attn_q_a_w, L0_attn_q_a_ln_w, L0_attn_q_b_w, L0_attn_kv_a_w, L0_attn_kv_a_ln_w,
           L0_attn_kv_b_w, L0_attn_o_w, L0_xattn_time_decay, L0_xattn_time_first, L0_ffn_Wr, L0_ffn_Wg,
           L0_ffn_Wu, L0_ffn_Wd, L0_ffn_Sg, L0_ffn_Su, L0_ffn_Sd, L0_ffn_Wsg):
    import concourse.bacc as bacc
    from concourse.bass_utils import run_bass_kernel_spmd

    def feature_major(a):
        return np.asarray(a).reshape(TOK, KT, 128).transpose(2, 1, 0)

    def columns(a):
        return np.asarray(a).reshape(KT, 128, -1).transpose(1, 0, 2)

    qa, qln, qb = (np.asarray(a) for a in (L0_attn_q_a_w, L0_attn_q_a_ln_w, L0_attn_q_b_w))
    kva, kvb, ow = (np.asarray(a) for a in (L0_attn_kv_a_w, L0_attn_kv_b_w, L0_attn_o_w))
    rot = kva[:, KVLR:]
    swapped = np.concatenate([rot[:, DR // 2:], rot[:, :DR // 2]], 1)
    qb = qb.reshape(QLR, NH, DN + DR)
    kvb = kvb.reshape(KVLR, NH, DN + DV)
    twice = np.concatenate([np.arange(128), np.arange(128, QLR), np.arange(128, QLR)])
    m = np.concatenate([qb[twice, :, :DN].transpose(2, 1, 0), kvb[:, :, :DN].transpose(2, 1, 0),
                        qb[:128, :, DN:], qb[twice[128:], :, DN:]], 2)
    vo = np.concatenate([kvb[:, :, DN:].transpose(2, 1, 0), ow.reshape(NH, DV, D).transpose(1, 0, 2)], 2)

    def by_group(a):
        return a.reshape(128, NG, -1).transpose(1, 0, 2)

    def experts(w, shared):
        return np.concatenate([np.asarray(w).transpose(1, 0, 2).reshape(D, E * FE), np.asarray(shared)], 1)

    rope, mask, ident, low, sel = _tables()
    given = [
        ("xT", feature_major(x)), ("ctx", feature_major(ctx_2048)),
        ("td", np.asarray(L0_xattn_time_decay).reshape(KT, 128).T),
        ("tf", np.asarray(L0_xattn_time_first).reshape(KT, 128).T),
        ("qaw", columns(qa[:, twice])), ("qaln", qln[twice].reshape(2, 128).T),
        ("kvw", columns(np.concatenate([kva, swapped, swapped], 1))),
        ("kvln", np.asarray(L0_attn_kv_a_ln_w).reshape(KVLR, 1)),
        ("head", np.concatenate([by_group(m), by_group(vo)], 2)),
        ("wr", columns(np.concatenate([np.asarray(L0_ffn_Wr), np.asarray(L0_ffn_Wsg)], 1))),
        ("wgu", np.concatenate([experts(L0_ffn_Wg, L0_ffn_Sg), experts(L0_ffn_Wu, L0_ffn_Su)], 1)),
        ("wd", np.concatenate([np.asarray(L0_ffn_Wd).reshape(E * FE, D), np.asarray(L0_ffn_Sd)], 0)),
        ("rope", rope), ("mask", mask), ("ident", ident), ("low", low), ("sel", sel),
    ]
    nc = bacc.Bacc("TRN2", target_bir_lowering=False, num_devices=1)
    arrays, args = {}, []
    for name, a in given:
        a = np.ascontiguousarray(a)
        arrays["in_" + name] = a
        args.append(nc.dram_tensor("in_" + name, a.shape, mybir.dt.from_np(a.dtype), kind="ExternalInput").ap())
    args.append(nc.dram_tensor("out", (128, KT, TOK), F32, kind="ExternalOutput").ap())
    decoder_program(nc, *args)
    r = run_bass_kernel_spmd(nc, [arrays], core_ids=[0])
    return np.ascontiguousarray(r.results[0]["out"].transpose(2, 1, 0)).reshape(B, S, D)
```

```python
import concourse.bass as bass
from concourse import mybir
from contextlib import ExitStack
import numpy as np

F32 = mybir.dt.float32
F32R = mybir.dt.float32r
BF16 = mybir.dt.bfloat16
ALU = mybir.AluOpType
ACT = mybir.ActivationFunctionType
AX = mybir.AxisListType

B, S, D = 16, 128, 256
TOK = B * S
KT = D // 128
CH = 512
NCH = TOK // CH
BC = CH // S
NH, QLR, KVLR, DR, DN, DV = 32, 192, 64, 64, 128, 128
QR2 = QLR - 128
HG = 4
NG = NH // HG
NP = HG // 2
QUADS = NCH * BC
SCALE = float(DN + DR) ** -0.5
E, TOPK, FE, FS = 8, 2, 176, 704
FF = E * FE + FS
FT = -(-FF // 128)
NR = E + 1
NEG = -1e38
SEG = S + 1
LN_EPS, RMS_EPS = 1e-5, 1e-6
WT = 256
WB = WT // S
WAVES = CH // WT
SEGS = KT * WB
PARTS = 17
LINKS = 17
QUAD_PARTS = {6: (0,), 7: (1,), 8: (2,), 9: (3, 4), 10: (5,), 11: (6,), 12: (7, 8), 13: (9, 10), 14: (11,), 15: (12,)}
BETWEEN = [(0, part) for part in range(13, PARTS)] + [(w, part) for w in range(1, WAVES) for part in range(PARTS)]
MCOL = 128 + 2 * QR2 + KVLR + 2 * DR
VCOL = KVLR + D
LEAD = 6
MW_SLOTS = (6, 7, 8, 10)
WO_SLOTS = (2, 3)
PIECE = 2 * FF // 4
PIECES = ([("d", 0, a, 4, 128) for a in range(0, FT - 1, 4)] + [("d", 0, FT - 1, 1, FF - 128 * (FT - 1))]
          + [("gu", k, a, PIECE, 128) for k in range(KT) for a in range(0, 2 * FF, PIECE)])
EARLY = len([q for q in PIECES if q[0] == "d"])
STAGES = 3


def fw(f):
    return min(128, FF - 128 * f)


class Linked:

    def __init__(self, eng, sem):
        self.eng, self.sem, self.base, self.made = eng, sem, 0, 0

    def start(self, base):
        self.base, self.made = base, 0

    def link(self, result):
        result.then_inc(self.sem, 1)
        self.made += 1
        self.eng.wait_ge(self.sem, self.base + self.made)


def decoder_program(nc, xT_d, ctx_d, td_d, tf_d, qaw_d, qaln_d, kvw_d, kvln_d, head_d, wr_d,
                    wgu_d, wd_d, rope_d, mask_d, ident_d, low_d, sel_d, out_d):
    stack = ExitStack()
    with stack:
        def sem(name):
            return stack.enter_context(nc.semaphore(name))

        def sb(ctx, name, shape, dt=F32):
            return ctx.enter_context(nc.sbuf_tensor(name, shape, dt))

        x = sb(stack, "x", [128, KT, TOK])
        ident = sb(stack, "ident", [128, 128])
        mean_w = sb(stack, "mean_w", [128, 128])
        power = sb(stack, "power", [128, 3 * BC])
        td = sb(stack, "td", [128, KT])
        tf = sb(stack, "tf", [128, KT])
        wr = sb(stack, "wr", [128, KT, NR])
        low = sb(stack, "low", [128, E, E])
        ps = stack.enter_context(nc.psum_tensor("ps", [128, 8, CH], F32))
        xw = sb(stack, "xw", [128, KT, WT])
        sqw = sb(stack, "sqw", [128, KT, WT])
        stat = sb(stack, "stat", [128, WB])
        rinv = sb(stack, "rinv", [128, WB])
        v = sb(stack, "v", [128, SEGS, S])
        wdec = sb(stack, "wdec", [128, SEGS, SEG])
        kp, pp, e1b, e2b, g, aa, bb = (sb(stack, n, [128, SEGS, SEG]) for n in
                                       ("kp", "pp", "e1b", "e2b", "g", "aa", "bb"))
        qq, e1, e2 = (sb(stack, n, [128, SEGS, S]) for n in ("qq", "e1", "e2"))
        lg = sb(stack, "lg", [128, WB, NR])
        pr = sb(stack, "pr", [128, WB, E])
        rt = sb(stack, "rt", [128, 2, WB])
        gt, eq = (sqw[:, k, 0:WB * E * E].rearrange("p (b i j) -> p b i j", b=WB, i=E) for k in range(2))
        rank = sb(stack, "rank", [128, WB, E])
        cw = sb(stack, "cw", [128, WB, NR])
        cwp = sb(stack, "cwp", [128, WB, 2 * NR], F32R)

        att = ExitStack()
        maskf = sb(att, "maskf", [128, S])
        maskb = sb(att, "maskb", [128, S], BF16)
        identb = sb(att, "identb", [128, 128], BF16)
        meanl_w = sb(att, "meanl_w", [128, 2])
        epsr = sb(att, "epsr", [128, 3 * BC])
        rope = sb(att, "rope", [128, 4, S])
        qn1h = sb(att, "qn1h", [128, TOK], F32R)
        qn1l = sb(att, "qn1l", [128, TOK], F32R)
        qn2 = sb(att, "qn2", [128, TOK], F32R)
        ka = sb(att, "ka", [128, TOK])
        ckv = sb(att, "ckv", [128, B, KVLR + 1])
        raw_m = sb(att, "raw_m", [128, HG, MCOL])
        raw_v = sb(att, "raw_v", [128, HG, VCOL])
        mwh = sb(att, "mwh", [128, HG, 2, 128], F32R)
        mwl = sb(att, "mwl", [128, HG, 2, 128], F32R)
        woh = sb(att, "woh", [128, NP, D], F32R)
        wol = sb(att, "wol", [128, NP, D], F32R)
        qa = sb(att, "qa", [128, 2, HG, CH])
        qs = sb(att, "qs", [128, CH])
        qu = sb(att, "qu", [128, CH])
        nmax = sb(att, "nmax", [128, 2, HG])
        p = sb(att, "p", [128, 2, HG, S])
        pT = sb(att, "pT", [128, HG, S])
        rsum = sb(att, "rsum", [128, HG])
        o = sb(att, "o", [128, HG, KVLR])
        oTh = sb(att, "oTh", [128, 2, NP, CH], F32R)
        oTl = sb(att, "oTl", [128, 2, NP, CH], F32R)
        qaw = sb(att, "qaw", [128, KT, 128 + 2 * QR2])
        kvw = sb(att, "kvw", [128, KT, 256])
        lnw = sb(att, "lnw", [128, 3])
        xc = sb(att, "xc", [128, 2, KT, CH])
        sq = sb(att, "sq", [128, KT, CH])
        sqp = sb(att, "sqp", [128, 3, CH])
        raw = sb(att, "raw", [128, 2, 4, CH])
        pstat = sb(att, "pstat", [128, 3 * BC])
        prinv = sb(att, "prinv", [128, 3 * BC])
        pt1, pt2 = sb(att, "pt1", [128, CH]), sb(att, "pt2", [128, CH])
        ckn = sb(att, "ckn", [KVLR, CH])
        att.close()

        ffn = ExitStack()
        wguh = sb(ffn, "wguh", [128, KT, 2 * FF], F32R)
        wgul = sb(ffn, "wgul", [128, KT, 2 * FF], F32R)
        sel = sb(ffn, "sel", [2 * NR, FT * 128], F32R)
        hh = sb(ffn, "hh", [128, KT, 2 * CH], F32R)
        hl = sb(ffn, "hl", [128, KT, 2 * CH], F32R)
        cT = sb(ffn, "cT", [2 * NR, 2 * CH], F32R)
        staging = ExitStack()
        selraw = sb(staging, "selraw", [2 * NR, FT * 128])
        staging.close()
        act_s = sb(ffn, "act_s", [128, 2, CH])
        act_t = sb(ffn, "act_t", [128, 2, CH])
        acth = sb(ffn, "acth", [128, 3, CH], F32R)
        actl = sb(ffn, "actl", [128, 3, CH], F32R)
        wdh = sb(ffn, "wdh", [128, FT, D], F32R)
        wdl = sb(ffn, "wdl", [128, FT, D], F32R)
        stage = sb(ffn, "stage", [128, STAGES, PIECE])
        ffn.close()

        x_in = [sem(f"x_in{t}") for t in range(NCH)]
        ident_in, w_in, const_in, raw_m_in, raw_v_in, v_in, sel_in, out_done = (sem(n) for n in (
            "ident_in", "w_in", "const_in", "raw_m_in", "raw_v_in", "v_in", "sel_in", "out_done"))
        stage_in = [sem(f"stage_in{i}") for i in range(STAGES)]
        const_set = sem("const_set")
        cast_set = sem("cast_set")
        (pmean_done, pxc_done, psq_done, pvar_done, pstat_set, prinv_set, lvar_done, lstat_set, lrinv_set, pr_done, pxn_done, qproj_done, kproj_done,
         qsquares_set, ksquares_set, raw_set, qr_done, qn_set, kr_done, ckn_set, keys_set, ckvT_done, ckv_set) = (
            sem(n) for n in ("pmean_done", "pxc_done", "psq_done", "pvar_done", "pstat_set", "prinv_set",
                             "lvar_done", "lstat_set", "lrinv_set", "pr_done",
                             "pxn_done", "qproj_done", "kproj_done", "qsquares_set", "ksquares_set", "raw_set",
                             "qr_done", "qn_set", "kr_done", "ckn_set", "keys_set", "ckvT_done", "ckv_set"))
        prep_chain = sem("prep_chain")
        mw_done, mwh_set, mwl_set, rot_set, wo_done, woh_set, wol_set = (sem(n) for n in (
            "mw_done", "mwh_set", "mwl_set", "rot_set", "wo_done", "woh_set", "wol_set"))
        qp_done, qs_set, qu_set, qcos_set, q_set = (sem(n) for n in (
            "qp_done", "qs_set", "qu_set", "qcos_set", "q_set"))
        s_done, max_done, p_done, pT_done, pT_set, pv_done, o_done, oT_done, oTh_set, oTl_set = (
            sem(n) for n in ("s_done", "max_done", "p_done", "pT_done", "pT_set", "pv_done",
                             "o_done", "oT_done", "oTh_set", "oTl_set"))
        rsum_set, y_done, y_added = sem("rsum_set"), sem("y_done"), sem("y_added")
        piece_h, sel_set = sem("piece_h"), sem("sel_set")
        piece_l = [sem("piece_l0"), sem("piece_l1")]
        decay_exp, wkv_ready = sem("decay_exp"), sem("wkv_ready")
        mean_done, xc_done, sq_done, var_done, stat_set, rinv_set, r_done, xn_done = (sem(n) for n in (
            "mean_done", "xc_done", "sq_done", "var_done", "stat_set", "rinv_set", "r_done", "xn_done"))
        (kp_set, ww_set, pp_set, qmax_set, d1_set, d2_set, d3_set, d4_set, e1b_set, e2b_set, e1_set, e2_set, g_set, states_set, e2v_set,
         e1a_set, n_set, wkv_done) = (
            sem(n) for n in ("kp_set", "ww_set", "pp_set", "qmax_set", "d1_set", "d2_set", "d3_set", "d4_set", "e1b_set", "e2b_set", "e1_set",
                             "e2_set", "g_set", "states_set", "e2v_set", "e1a_set", "n_set", "wkv_done"))
        hh_set, hl_set, logit_done, lmax_set, lexp_set, cw_set, cT_done, cT_set = (sem(n) for n in (
            "hh_set", "hl_set", "logit_done", "lmax_set", "lexp_set", "cw_set", "cT_done", "cT_set"))
        primed = (gate_done, up_done, share_done, silu_done, mix_done, prod_done, acth_set, actl_set,
                  down_done, z_added) = [
            sem(n) for n in ("gate_done", "up_done", "share_done", "silu_done", "mix_done",
                             "prod_done", "acth_set", "actl_set", "down_done", "z_added")]
        wave_chain = sem("wave_chain")

        NORM_BANK, LSTAT_BANK, RK_BANK, RQ_BANK, P_BANK = 0, 1, 2, 3, 4
        S_BANK, PT_BANK, PV_BANK, OT_BANK, Q_BANK, Y_BANK = 0, 2, 3, 4, 5, 6
        WO_BANK, MW_BANK = Y_BANK, Y_BANK + 1
        G_BANK, U_BANK, C_BANK, Z_BANK, W_BANK = 0, 2, 4, 5, 7

        def bank(i):
            return ps[:, i, :]

        def toks(t):
            return bass.ds(t * CH, CH)

        def f32(ap):
            return ap.bitcast(F32)

        def over_b(ap):
            return ap.unsqueeze(1).to_broadcast([ap.shape[0], BC, S])

        def by_b(ap):
            return ap.rearrange("p (b s) -> p b s", s=S)

        def wtoks(w):
            return bass.ds(w * WT, WT)

        def held(w):
            return bass.ds((w % (2 * WAVES)) * WT, WT)

        def over_k(ap):
            return ap.unsqueeze(1).to_broadcast([ap.shape[0], KT, ap.shape[-1]])

        def now(eng, s, value):
            if not (isinstance(value, int) and value <= 0):
                eng.wait_ge(s, value)

        def over_groups(eng, body):
            body(0, True, False)
            with eng.Fori(1, NG - 1) as gi:
                body(gi, False, False)
            body(NG - 1, False, True)

        NORM_COLS, LATENT_COLS = slice(0, BC), slice(BC, 3 * BC)

        def wave_part(c, step):
            return WAVES * (c + 1) + step // PARTS, step % PARTS

        def over_chunks(eng, body):
            with eng.Fori(0, NCH - 1) as c:
                body(c, True)
            body(NCH - 1, False)

        def rotated(j):
            return raw_m[:, j, MCOL - 2 * DR:].rearrange("p (a c) -> p a c", a=2)

        def by_dve(n):
            return int(n >= EARLY and n % 2)

        def lows(n, engine):
            return len([i for i in range(n) if by_dve(i) == engine])

        def piece(n):
            kind, k, a, w, rows = PIECES[n]
            if kind == "gu":
                return stage[:, n % STAGES, 0:w], wguh[:, k, a:a + w], wgul[:, k, a:a + w]
            return (stage[0:rows, n % STAGES, 0:w * D], *(t[0:rows, a:a + w, :].rearrange("p f n -> p (f n)")
                                                     for t in (wdh, wdl)))

        block = stack.enter_context(nc.Block())

        @block.sync
        def _(sp):
            sp.dma_start(x[:, :, toks(0)], xT_d[:, :, toks(0)]).then_inc(x_in[0], 16)
            sp.dma_start(ident[:, :], ident_d).then_inc(ident_in, 16)
            for dst, src in ((qaw[:, :, :], qaw_d), (kvw[:, :, :], kvw_d), (lnw[:, 0:2], qaln_d),
                             (lnw[0:KVLR, 2:3], kvln_d), (rope[:, :, :], rope_d)):
                sp.dma_start(dst, src).then_inc(w_in, 16)
            for t in range(1, NCH):
                sp.dma_start(x[:, :, toks(t)], xT_d[:, :, toks(t)]).then_inc(x_in[t], 16)
            for dst, src in ((maskf[:, :], mask_d), (td[:, :], td_d),
                             (tf[:, :], tf_d), (wr[:, :, :], wr_d),
                             (low[:, :, :], low_d)):
                sp.dma_start(dst, src).then_inc(const_in, 16)

            def load_m(gi):
                sp.dma_start(raw_m[:, :, :].rearrange("p a b -> p (a b)"),
                             head_d[bass.ds(gi, 1), :, 0:HG * MCOL].rearrange("a p n -> (a p) n")
                             ).then_inc(raw_m_in, 16)

            def load_v(gi):
                sp.dma_start(raw_v[:, :, :].rearrange("p a b -> p (a b)"),
                             head_d[bass.ds(gi, 1), :, HG * MCOL:].rearrange("a p n -> (a p) n")
                             ).then_inc(raw_v_in, 16)

            load_m(0)
            load_v(0)
            with sp.Fori(1, NG) as gi:
                sp.wait_ge(mw_done, gi * HG)
                sp.wait_ge(rot_set, gi * HG)
                load_m(gi)
                sp.wait_ge(wo_done, gi * NP)
                load_v(gi)

            def load_v_wave(w):
                sp.dma_start(v[:, :, :].rearrange("p (k b) s -> p k (b s)", k=KT), ctx_d[:, :, wtoks(w)]
                             ).then_inc(v_in, 16)

            load_v_wave(0)
            def load_piece(n):
                if n >= STAGES:
                    e = by_dve(n - STAGES)
                    sp.wait_ge(piece_l[e], lows(n - STAGES + 1, e))
                kind, k, a, w, rows = PIECES[n]
                if kind == "gu":
                    src, dst = wgu_d[128 * k:128 * k + 128, a:a + w], stage[:, n % STAGES, 0:w]
                else:
                    src = wd_d[128 * a:128 * a + rows * w, :].rearrange("(f p) n -> p f n", p=rows)
                    dst = stage[0:rows, n % STAGES, 0:w * D].rearrange("p (f n) -> p f n", n=D)
                sp.dma_start(dst, src).then_inc(stage_in[n % STAGES], 16)

            for n in range(EARLY + STAGES):
                load_piece(n)
            for w in range(1, WAVES):
                sp.wait_ge(wkv_done, w)
                load_v_wave(w)
            sp.wait_ge(y_added, KT * NG * NCH)
            sp.dma_start(selraw[:, :], sel_d).then_inc(sel_in, 16)
            for n in range(EARLY + STAGES, len(PIECES)):
                load_piece(n)
            with sp.Fori(0, NCH - 1) as c:
                for i in range(WAVES):
                    w = WAVES * (c + 1) + i
                    sp.wait_ge(wkv_done, w)
                    load_v_wave(w)
                sp.wait_ge(z_added, KT * (c + 1) + 1)
                sp.dma_start(out_d[:, :, toks(c)], x[:, :, toks(c)]).then_inc(out_done, 16)
            sp.wait_ge(z_added, KT * NCH + 1)
            sp.dma_start(out_d[:, :, toks(NCH - 1)], x[:, :, toks(NCH - 1)]).then_inc(out_done, 16)
            sp.wait_ge(out_done, 16 * NCH)

        @block.gpsimd
        def _(pool):
            for s in primed:
                pool.sem_inc(s, 1)
            pool.memset(mean_w[:, :], 1.0 / D)
            pool.memset(power[:, :], -0.5)
            pool.memset(meanl_w[:, 0:1], 1.0 / QLR)
            pool.memset(meanl_w[:, 1:2], 1.0 / KVLR)
            pool.memset(epsr[:, 0:BC], LN_EPS)
            pool.memset(epsr[:, BC:], RMS_EPS)
            pool.memset(qs[:, :], 0.0)
            pool.memset(ckv[:, :, :], 1.0).then_inc(const_set, 1)

            def raise_power(cols, ready, done, t):
                pool.wait_ge(ready, t + 1)
                pool.tensor_tensor(prinv[:, cols], pstat[:, cols], power[:, cols], ALU.pow).then_inc(done, 1)

            raise_power(NORM_COLS, pstat_set, prinv_set, 0)
            for u in range(NCH + 1):
                if u:
                    raise_power(LATENT_COLS, lstat_set, lrinv_set, u - 1)
                if u + 1 < NCH:
                    raise_power(NORM_COLS, pstat_set, prinv_set, u + 1)

            def rot_parts(head, j):
                pool.wait_ge(mwh_set, head + 1)
                pool.tensor_tensor(mwl[:, j, :, KVLR:], rotated(j), f32(mwh[:, j, :, KVLR:]), ALU.subtract
                                   ).then_inc(rot_set, 1)

            def times_sine(job):
                pool.wait_ge(qs_set, job + 1)
                now(pool, q_set, job)
                pool.tensor_tensor(by_b(qu[:, :]), by_b(qs[:, :]), over_b(rope[:, 1, :]), ALU.mult
                                   ).then_inc(qu_set, 1)

            for j in range(HG):
                rot_parts(j, j)
            for job in range(LEAD):
                times_sine(job)

            def inverse_deviation(w, i):
                pool.wait_ge(stat_set, 2 * w + i + 1)
                pool.tensor_tensor(rinv[:, :], stat[:, :], power[:, 0:WB], ALU.pow).then_inc(rinv_set, 1)

            def pool_part(w, part):
                if part in (1, 12):
                    inverse_deviation(w, part // 12)
                elif part == 3:
                    before, after = pp[:, :, 0:S], pp[:, :, 1:]
                    pool.wait_ge(pp_set, w + 1)
                    pool.tensor_tensor(e1b[:, :, 1:], before, after, ALU.subtract).then_inc(d1_set, 1)
                    pool.tensor_tensor(e2b[:, :, 1:], kp[:, :, 1:], after, ALU.subtract).then_inc(d2_set, 1)
                elif part == 6:
                    pool.wait_ge(v_in, 16 * (w + 1))
                    pool.wait_ge(e2b_set, w + 1)
                    pool.tensor_tensor(g[:, :, 1:], e2b[:, :, 1:], v[:, :, :], ALU.mult).then_inc(g_set, 1)
                    pool.wait_ge(e2_set, w + 1)
                    pool.wait_ge(g_set, w + 1)
                    pool.tensor_tensor(v[:, :, :], e2[:, :, :], v[:, :, :], ALU.mult).then_inc(e2v_set, 1)
                elif part == 8:
                    pool.wait_ge(e1_set, w + 1)
                    pool.wait_ge(states_set, w + 1)
                    pool.tensor_tensor(g[:, :, 1:], e1[:, :, :], aa[:, :, 0:S], ALU.mult).then_inc(e1a_set, 1)
                elif part == 9:
                    pool.wait_ge(e1a_set, w + 1)
                    pool.tensor_tensor(g[:, :, 1:], g[:, :, 1:], v[:, :, :], ALU.add).then_inc(n_set, 1)
                elif part == 14:
                    pool.wait_ge(hh_set, w + 1)
                    pool.tensor_tensor(hl[:, :, held(w)], xw[:, :, :], f32(hh[:, :, held(w)]), ALU.subtract
                                       ).then_inc(hl_set, 1)

            def low_piece(n):
                raw, hi, lo = piece(n)
                pool.wait_ge(piece_h, n + 1)
                pool.tensor_tensor(lo, raw, f32(hi), ALU.subtract).then_inc(piece_l[0], 1)

            def pool_group(gi, first, last):
                for k in range(QUADS):
                    if k + LEAD < QUADS or not last:
                        times_sine(QUADS * gi + k + LEAD)
                    if k in MW_SLOTS and not last:
                        j = MW_SLOTS.index(k)
                        rot_parts(HG * gi + HG + j, j)
                    if last:
                        if k < EARLY:
                            low_piece(k)
                        for part in QUAD_PARTS.get(k, ()):
                            pool_part(0, part)

            over_groups(pool, pool_group)

            for n, (w, part) in enumerate(BETWEEN):
                pool_part(w, part)
                if EARLY + n < len(PIECES) and not by_dve(EARLY + n):
                    low_piece(EARLY + n)

            def pool_chunk(c, waves):
                for f in range(FT):
                    w, n = fw(f), FT * c + f + 1
                    if waves:
                        pool_part(*wave_part(c, 2 * f))
                    if waves:
                        pool_part(*wave_part(c, 2 * f + 1))
                    pool.wait_ge(acth_set, n + 1)
                    pool.tensor_tensor(actl[0:w, f % 3, :], act_t[0:w, f % 2, :], f32(acth[0:w, f % 3, :]),
                                       ALU.subtract).then_inc(actl_set, 1)

            over_chunks(pool, pool_chunk)

        @block.vector
        def _(dve):
            linked = Linked(dve, prep_chain)
            link = linked.link

            def mw_low(head, j, src=bank(MW_BANK)):
                dve.wait_ge(mwh_set, head + 1)
                dve.tensor_tensor(mwl[:, j, :, 0:KVLR],
                                  src[:, 0:2 * KVLR].rearrange("p (a c) -> p a c", a=2),
                                  f32(mwh[:, j, :, 0:KVLR]), ALU.subtract).then_inc(mwl_set, 1)

            def center_chunk(t):
                dve.wait_ge(pmean_done, t + 1)
                now(dve, kproj_done, t - 1)
                dve.tensor_tensor(xc[:, t % 2, :, :], x[:, :, toks(t)], over_k(bank(NORM_BANK)), ALU.subtract
                                  ).then_inc(pxc_done, 1)

            def query_latent(t):
                dve.wait_ge(raw_set, t + 1)
                dve.wait_ge(qr_done, t + 1)
                r = bank(RQ_BANK)
                dve.scalar_tensor_tensor(pt1[:, :], raw[:, t % 2, 0, :], lnw[:, 0:1], r, ALU.mult, ALU.mult)
                link(dve.scalar_tensor_tensor(pt2[:, :], raw[:, t % 2, 1, :], lnw[:, 1:2], r, ALU.mult, ALU.mult))
                dve.tensor_copy(qn1h[:, toks(t)], pt1[:, :])
                link(dve.tensor_copy(qn2[:, toks(t)], pt2[:, :]))
                dve.tensor_tensor(qn1l[:, toks(t)], pt1[:, :], f32(qn1h[:, toks(t)]), ALU.subtract)
                low_rows = qn2[QR2:, toks(t)]
                link(dve.tensor_tensor(low_rows, pt2[QR2:, :], f32(low_rows), ALU.subtract))
                dve.sem_inc(qn_set, 1)

            def key_latent(t):
                dve.wait_ge(kr_done, t + 1)
                now(dve, ckvT_done, t)
                dve.scalar_tensor_tensor(ckn[:, :], raw[0:KVLR, t % 2, 2, :], lnw[0:KVLR, 2:3],
                                         bank(RK_BANK)[0:KVLR, :], ALU.mult, ALU.mult).then_inc(ckn_set, 1)
                dve.tensor_tensor(by_b(pt1[KVLR:, :]), by_b(raw[KVLR:, t % 2, 2, :]), over_b(rope[KVLR:, 2, :]),
                                  ALU.mult)
                link(dve.tensor_tensor(by_b(pt2[KVLR:, :]), by_b(raw[KVLR:, t % 2, 3, :]), over_b(rope[KVLR:, 3, :]),
                                       ALU.mult))
                dve.tensor_scalar(ka[0:KVLR, toks(t)], ckn[:, :], SCALE, None, ALU.mult)
                link(dve.tensor_tensor(ka[KVLR:, toks(t)], pt1[KVLR:, :], pt2[KVLR:, :], ALU.add))
                dve.sem_inc(keys_set, 1)

            def statistic(src, cols, ready, done, t):
                dve.wait_ge(ready, t + 1)
                dve.tensor_tensor(pstat[:, cols], src[:, cols], epsr[:, cols], ALU.add).then_inc(done, 1)

            def norm_chunk(t):
                statistic(bank(NORM_BANK), NORM_COLS, pvar_done, pstat_set, t)
                dve.wait_ge(pr_done, t + 1)
                dve.tensor_tensor(xc[:, t % 2, :, :], xc[:, t % 2, :, :], over_k(bank(NORM_BANK)), ALU.mult
                                  ).then_inc(pxn_done, 1)

            center_chunk(0)
            norm_chunk(0)
            for u in range(NCH + 1):
                if u:
                    statistic(bank(LSTAT_BANK), LATENT_COLS, lvar_done, lstat_set, u - 1)
                if u == NCH:
                    for j in range(HG):
                        mw_low(j, j, bank(P_BANK + j))
                if u:
                    dve.wait_ge(w_in, 16 * 5)
                if u + 1 < NCH:
                    center_chunk(u + 1)
                    norm_chunk(u + 1)
                if u:
                    query_latent(u - 1)
                    key_latent(u - 1)

            dve.wait_ge(decay_exp, 1)
            link(dve.tensor_scalar(td[:, :], td[:, :], -1.0, None, ALU.mult))
            link(dve.memset(wdec[:, :, :], 0.0))
            for k in range(KT):
                real = wdec[:, WB * k:WB * (k + 1), 1:]
                dve.tensor_scalar(real, real, td[:, k:k + 1], None, ALU.add)
            dve.memset(wdec[:, :, 0:1], NEG)
            dve.memset(kp[:, :, 0:1], NEG)
            dve.memset(e1b[:, :, 0:1], 0.0)
            dve.memset(e2b[:, :, 0:1], 0.0)
            link(dve.memset(g[:, :, 0:1], 0.0))
            dve.sem_inc(wkv_ready, 1)

            def wo_low(pair, j):
                dve.wait_ge(woh_set, pair + 1)
                dve.tensor_tensor(wol[:, j, :], bank(WO_BANK)[:, 0:D], f32(woh[:, j, :]), ALU.subtract
                                  ).then_inc(wol_set, 1)

            def take_query(job, m):
                par = m // HG % 2
                dve.wait_ge(qs_set, job + 1)
                now(dve, s_done, HG * (m // HG) - HG + job - m)
                dve.tensor_tensor(by_b(qa[:, par, m % HG, :]), by_b(bank(Q_BANK)), over_b(rope[:, 0, :]), ALU.mult
                                  ).then_inc(qcos_set, 1)

            def add_sine(job, m):
                part = qa[KVLR:, m // HG % 2, m % HG, :]
                dve.wait_ge(qu_set, job + 1)
                dve.wait_ge(qcos_set, job + 1)
                dve.tensor_tensor(part, part, qu[KVLR:, :], ALU.add).then_inc(q_set, 1)

            def negative_max(n, m):
                dve.wait_ge(s_done, n + 1)
                now(dve, p_done, n - 1)
                dve.tensor_reduce(nmax[:, m % 2, :],
                                  bank(S_BANK + m % 2).rearrange("p (h k) -> p h k", h=HG),
                                  AX.X, ALU.max, negate=True).then_inc(max_done, 1)

            def normalise(n):
                pv = bank(PV_BANK)[:, 0:HG * (KVLR + 1)].rearrange("p (h c) -> p h c", h=HG)
                dve.wait_ge(pv_done, n + 1)
                dve.reciprocal(rsum[:, :], pv[:, :, KVLR]).then_inc(rsum_set, 1)
                dve.wait_ge(rsum_set, n + 1)
                now(dve, oT_done, n)
                dve.tensor_tensor(o[:, :, :], pv[:, :, 0:KVLR],
                                  rsum[:, :].unsqueeze(2).to_broadcast([128, HG, KVLR]), ALU.mult
                                  ).then_inc(o_done, 1)

            def outputs_low(n, m):
                par, b = m // BC % 2, m % BC
                dve.wait_ge(oTh_set, n + 1)
                dve.tensor_tensor(oTl[:, par, :, b * S:b * S + S],
                                  bank(OT_BANK)[:, 0:NP * S].rearrange("p (a s) -> p a s", a=NP),
                                  f32(oTh[:, par, :, b * S:b * S + S]), ALU.subtract).then_inc(oTl_set, 1)

            def add_outputs(it, c):
                for m in range(KT):
                    dve.wait_ge(y_done, KT * it + m + 1)
                    dve.tensor_tensor(x[:, m, toks(c)], x[:, m, toks(c)], bank(Y_BANK + m), ALU.add
                                      ).then_inc(y_added, 1)

            for job in range(LEAD - 1):
                take_query(job, job)
                add_sine(job, job)
            negative_max(0, 0)

            wave = Linked(dve, wave_chain)

            def flat(a):
                return a[:, :, :].rearrange("p a b -> p (a b)")

            def ktile(a, k):
                return a[:, WB * k:WB * (k + 1), :]

            def over_e(ap):
                return ap.unsqueeze(2).to_broadcast([128, WB, E])

            def center(w, i):
                now(dve, hl_set, w)
                dve.wait_ge(mean_done, 2 * w + i + 1)
                dve.tensor_tensor(xw[:, :, :], x[:, :, wtoks(w)], over_k(bank(W_BANK)[:, 0:WT]), ALU.subtract
                                  ).then_inc(xc_done, 1)

            def variance(w, i):
                dve.wait_ge(var_done, 2 * w + i + 1)
                dve.tensor_scalar(stat[:, :], bank(W_BANK)[:, 0:WB], LN_EPS, None, ALU.add).then_inc(stat_set, 1)

            def running_maximum(w):
                dve.wait_ge(r_done, 2 * w + 1)
                for k in range(KT):
                    last = dve.tensor_tensor(ktile(kp, k)[:, :, 1:], by_b(xw[:, k, :]), by_b(bank(W_BANK)[:, 0:WT]),
                                             ALU.mult)
                last.then_inc(kp_set, 1)
                dve.wait_ge(kp_set, w + 1)
                dve.tensor_tensor_scan(flat(pp), flat(wdec), flat(kp), NEG, ALU.add, ALU.max).then_inc(pp_set, 1)

            def output_maximum(w):
                dve.wait_ge(ww_set, w + 1)
                dve.wait_ge(pp_set, w + 1)
                dve.tensor_tensor(qq[:, :, :], e2[:, :, :], pp[:, :, 0:S], ALU.max).then_inc(qmax_set, 1)
                dve.wait_ge(qmax_set, w + 1)
                dve.tensor_tensor(e1[:, :, :], pp[:, :, 0:S], qq[:, :, :], ALU.subtract).then_inc(d3_set, 1)

            def denominator_state(w):
                dve.wait_ge(e1b_set, w + 1)
                dve.wait_ge(e2b_set, w + 1)
                wave.link(dve.tensor_tensor_scan(flat(bb), flat(e1b), flat(e2b), 0.0, ALU.mult, ALU.add))

            def numerator_state(w):
                dve.wait_ge(g_set, w + 1)
                dve.tensor_tensor_scan(flat(aa), flat(e1b), flat(g), 0.0, ALU.mult, ALU.add).then_inc(states_set, 1)

            def denominator(w):
                dve.wait_ge(e1_set, w + 1)
                dve.wait_ge(e2_set, w + 1)
                wave.link(dve.tensor_tensor(qq[:, :, :], e1[:, :, :], bb[:, :, 0:S], ALU.mult))
                wave.link(dve.tensor_tensor(qq[:, :, :], qq[:, :, :], e2[:, :, :], ALU.add))

            def add_wkv(w):
                dve.wait_ge(n_set, w + 1)
                wave.link(dve.tensor_tensor(e1[:, :, :], g[:, :, 1:], qq[:, :, :], ALU.mult))
                for k in range(KT):
                    xs = by_b(x[:, k, wtoks(w)])
                    last = dve.tensor_tensor(xs, xs, ktile(e1, k), ALU.add)
                last.then_inc(wkv_done, 1)

            def logits(w):
                dve.wait_ge(logit_done, w + 1)
                wave.link(dve.tensor_copy(lg[:, :, :],
                                          bank(W_BANK)[:, 0:WB * NR].rearrange("p (b e) -> p b e", e=NR)))
                wave.link(dve.tensor_reduce(rt[:, 0, :], lg[:, :, 0:E], AX.X, ALU.max))
                dve.tensor_tensor(pr[:, :, :], lg[:, :, 0:E], over_e(rt[:, 0, :]), ALU.subtract).then_inc(lmax_set, 1)

            def choose(w):
                dve.wait_ge(lexp_set, w + 1)
                wave.link(dve.tensor_reduce(rt[:, 1, :], pr[:, :, :], AX.X, ALU.add))
                wave.link(dve.reciprocal(rt[:, 1, :], rt[:, 1, :]))
                wave.link(dve.tensor_tensor(pr[:, :, :], pr[:, :, :], over_e(rt[:, 1, :]), ALU.mult))
                other = pr[:, :, :].unsqueeze(2).to_broadcast([128, WB, E, E])
                own = pr[:, :, :].unsqueeze(3).to_broadcast([128, WB, E, E])
                dve.tensor_tensor(gt[:, :, :, :], other, own, ALU.is_gt)
                wave.link(dve.tensor_tensor(eq[:, :, :, :], other, own, ALU.is_equal))
                wave.link(dve.tensor_tensor(eq[:, :, :, :], eq[:, :, :, :],
                                            low[:, :, :].unsqueeze(1).to_broadcast([128, WB, E, E]), ALU.mult))
                wave.link(dve.tensor_tensor(gt[:, :, :, :], gt[:, :, :, :], eq[:, :, :, :], ALU.add))
                dve.tensor_scalar(cw[:, :, E], lg[:, :, E], 1.0, None, ALU.add)
                wave.link(dve.tensor_reduce(rank[:, :, :], gt[:, :, :, :], AX.X, ALU.add))
                dve.scalar_tensor_tensor(cw[:, :, 0:E], rank[:, :, :], TOPK - 0.5, pr[:, :, :], ALU.is_lt, ALU.mult)
                wave.link(dve.reciprocal(cw[:, :, E], cw[:, :, E]))
                wave.link(dve.tensor_copy(cwp[:, :, 0:NR], cw[:, :, :]))
                dve.tensor_tensor(cwp[:, :, NR:], cw[:, :, :], f32(cwp[:, :, 0:NR]), ALU.subtract).then_inc(cw_set, 1)

            def dve_part(w, part):
                if part == 0:
                    wave.start(LINKS * w)
                if part in (0, 11):
                    center(w, part // 11)
                elif part in (1, 12):
                    variance(w, part // 12)
                elif part == 2:
                    running_maximum(w)
                elif part == 3:
                    output_maximum(w)
                elif part == 4:
                    dve.tensor_tensor(e2[:, :, :], e2[:, :, :], qq[:, :, :], ALU.subtract).then_inc(d4_set, 1)
                elif part == 6:
                    denominator_state(w)
                    denominator(w)
                elif part == 8:
                    numerator_state(w)
                elif part in (7, 9):
                    half = ktile(qq, part // 9)
                    wave.link(dve.reciprocal(half, half))
                elif part == 10:
                    add_wkv(w)
                elif part == 13:
                    dve.wait_ge(r_done, 2 * w + 2)
                    dve.tensor_tensor(xw[:, :, :], xw[:, :, :], over_k(bank(W_BANK)[:, 0:WT]), ALU.mult
                                      ).then_inc(xn_done, 1)
                elif part == 14:
                    logits(w)
                elif part == 15:
                    choose(w)
                    assert wave.made == LINKS, wave.made

            def dve_group(gi, first, last):
                for k in range(QUADS):
                    n = QUADS * gi + k
                    if k or not first:
                        normalise(n - 1)
                    more = k + LEAD - 1 < QUADS or not last
                    if more:
                        take_query(n + LEAD - 1, k + LEAD - 1)
                    if k + 1 < QUADS or not last:
                        negative_max(n + 1, k + 1)
                    if more:
                        add_sine(n + LEAD - 1, k + LEAD - 1)
                    if k or not first:
                        outputs_low(n - 1, k - 1 + QUADS)
                    if k % BC == 1 and (k > 1 or not first):
                        add_outputs(NCH * gi + k // BC - 1, (k // BC - 1) % NCH)
                    if k in WO_SLOTS:
                        j = WO_SLOTS.index(k)
                        wo_low(NP * gi + j, j)
                    if k in MW_SLOTS and not last:
                        j = MW_SLOTS.index(k)
                        mw_low(HG * gi + HG + j, j)
                    if last:
                        for part in QUAD_PARTS.get(k, ()):
                            dve_part(0, part)

            over_groups(dve, dve_group)
            normalise(NG * QUADS - 1)
            outputs_low(NG * QUADS - 1, QUADS - 1)
            add_outputs(NG * NCH - 1, NCH - 1)

            def low_piece(n):
                raw, hi, lo = piece(n)
                dve.wait_ge(piece_h, n + 1)
                dve.tensor_tensor(lo, raw, f32(hi), ALU.subtract).then_inc(piece_l[1], 1)

            for n, (w, part) in enumerate(BETWEEN):
                dve_part(w, part)
                if EARLY + n < len(PIECES) and by_dve(EARLY + n):
                    low_piece(EARLY + n)
            dve.wait_ge(sel_in, 16)
            dve.tensor_copy(sel[:, :], selraw[:, :]).then_inc(sel_set, 1)

            def dve_chunk(c, waves):
                for f in range(FT):
                    w, n, free = fw(f), FT * c + f + 1, FT * c + max(f - 1, 0) + 1
                    part = act_t[0:w, f % 2, :]
                    if waves:
                        dve_part(*wave_part(c, 2 * f))
                    dve.wait_ge(up_done, n + 1)
                    dve.wait_ge(silu_done, n + 1)
                    dve.wait_ge(actl_set, free)
                    dve.tensor_tensor(part, act_s[0:w, f % 2, :], bank(U_BANK + f % 2)[0:w, :], ALU.mult
                                      ).then_inc(mix_done, 1)
                    if waves:
                        dve_part(*wave_part(c, 2 * f + 1))
                    dve.wait_ge(share_done, n + 1)
                    dve.wait_ge(mix_done, n + 1)
                    dve.tensor_tensor(part, part, bank(C_BANK)[0:w, :], ALU.mult).then_inc(prod_done, 1)
                dve.wait_ge(down_done, FT * (c + 1) + 1)
                for m in range(KT):
                    dve.tensor_tensor(x[:, m, toks(c)], x[:, m, toks(c)], bank(Z_BANK + m), ALU.add
                                      ).then_inc(z_added, 1)

            over_chunks(dve, dve_chunk)

        @block.scalar
        def _(act):
            def mw_high(head, j, freed, src=bank(MW_BANK)):
                act.wait_ge(mw_done, head + 1)
                now(act, qp_done, freed)
                act.activation(mwh[:, j, :, 0:KVLR],
                               src[:, 0:2 * KVLR].rearrange("p (a c) -> p a c", a=2), ACT.Copy)
                act.activation(mwh[:, j, :, KVLR:], rotated(j), ACT.Copy).then_inc(mwh_set, 1)

            def square_chunk(t):
                act.wait_ge(pxc_done, t + 1)
                now(act, pvar_done, t)
                act.activation(sq[:, :, :], xc[:, t % 2, :, :], ACT.Square).then_inc(psq_done, 1)

            square_chunk(0)
            for u in range(NCH + 2):
                if u + 1 < NCH:
                    square_chunk(u + 1)
                if u == NCH:
                    for j in range(HG):
                        mw_high(j, j, 0, bank(P_BANK + j))
                if u < NCH:
                    now(act, keys_set, u - 1)
                    now(act, qn_set, u - 1)
                    now(act, lvar_done, u)
                    act.wait_ge(qproj_done, u + 1)
                    act.activation(sqp[:, 0:2, :], ps[:, P_BANK:P_BANK + 2, :], ACT.Square).then_inc(qsquares_set, 1)
                    act.activation(raw[:, u % 2, 0:2, :], ps[:, P_BANK:P_BANK + 2, :], ACT.Copy)
                if u >= 2:
                    t = u - 2
                    act.wait_ge(ckvT_done, t + 1)
                    act.activation(ckv[:, BC * t:BC * (t + 1), 0:KVLR],
                                   bank(RQ_BANK)[:, 0:BC * KVLR].rearrange("p (b c) -> p b c", c=KVLR), ACT.Copy
                                   ).then_inc(ckv_set, 1)
                if u < NCH:
                    act.wait_ge(kproj_done, u + 1)
                    act.activation(sqp[:, 2, :], bank(P_BANK + 2), ACT.Square).then_inc(ksquares_set, 1)
                    act.activation(raw[:, u % 2, 2:4, :], ps[:, P_BANK + 2:P_BANK + 4, :], ACT.Copy
                                   ).then_inc(raw_set, 1)

            act.wait_ge(ident_in, 16)
            act.wait_ge(const_in, 16 * 5)
            act.activation(maskb[:, :], maskf[:, :], ACT.Copy)
            act.activation(identb[:, :], ident[:, :], ACT.Copy).then_inc(cast_set, 1)
            act.activation(td[:, :], td[:, :], ACT.Exp).then_inc(decay_exp, 1)

            def wo_high(pair, j, freed):
                act.wait_ge(wo_done, pair + 1)
                now(act, y_done, freed)
                act.activation(woh[:, j, :], bank(WO_BANK)[:, 0:D], ACT.Copy).then_inc(woh_set, 1)

            def exponentials(n, m):
                act.wait_ge(max_done, n + 1)
                now(act, pT_done, n - 1)
                for hd in range(HG):
                    last = act.activation(p[:, m % 2, hd, :], bank(S_BANK + m % 2)[:, hd * S:hd * S + S], ACT.Exp,
                                          bias=nmax[:, m % 2, hd:hd + 1])
                last.then_inc(p_done, 1)

            def probs_out(n):
                act.wait_ge(pT_done, n + 1)
                now(act, pv_done, n)
                act.activation(pT[:, :, :].rearrange("p h q -> p (h q)"), bank(PT_BANK), ACT.Copy
                               ).then_inc(pT_set, 1)

            def outputs_high(n, m, it):
                par, b = m // BC % 2, m % BC
                act.wait_ge(oT_done, n + 1)
                now(act, y_done, KT * (it - 1))
                act.activation(oTh[:, par, :, b * S:b * S + S],
                               bank(OT_BANK)[:, 0:NP * S].rearrange("p (a s) -> p a s", a=NP), ACT.Copy
                               ).then_inc(oTh_set, 1)

            def swap_halves(job):
                half = DR // 2
                act.wait_ge(qp_done, job + 1)
                now(act, qu_set, job)
                act.activation(qs[KVLR:KVLR + half, :], bank(Q_BANK)[KVLR + half:, :], ACT.Copy)
                act.activation(qs[KVLR + half:, :], bank(Q_BANK)[KVLR:KVLR + half, :], ACT.Copy).then_inc(qs_set, 1)

            for job in range(LEAD):
                swap_halves(job)
            exponentials(0, 0)

            def square(w, i):
                act.wait_ge(xc_done, 2 * w + i + 1)
                act.activation(sqw[:, :, :], xw[:, :, :], ACT.Square).then_inc(sq_done, 1)

            def exp_of(a, ready, done, w):
                act.wait_ge(ready, w + 1)
                act.activation(a, a, ACT.Exp).then_inc(done, 1)

            def act_part(w, part):
                if part in (0, 11):
                    square(w, part // 11)
                elif part == 3:
                    act.wait_ge(kp_set, w + 1)
                    for k in range(KT):
                        rows = slice(WB * k, WB * (k + 1))
                        last = act.activation(e2[:, rows, :], kp[:, rows, 1:], ACT.Identity, bias=tf[:, k:k + 1])
                    last.then_inc(ww_set, 1)
                elif part == 5:
                    act.wait_ge(d1_set, w + 1)
                    for k in range(KT):
                        a = e1b[:, WB * k:WB * (k + 1), 1:]
                        last = act.activation(a, a, ACT.Exp, bias=td[:, k:k + 1])
                    last.then_inc(e1b_set, 1)
                    exp_of(e2b[:, :, 1:], d2_set, e2b_set, w)
                    exp_of(e1[:, :, :], d3_set, e1_set, w)
                    exp_of(e2[:, :, :], d4_set, e2_set, w)
                elif part == 13:
                    act.wait_ge(xn_done, w + 1)
                    act.activation(hh[:, :, held(w)], xw[:, :, :], ACT.Copy).then_inc(hh_set, 1)
                elif part == 14:
                    act.wait_ge(lmax_set, w + 1)
                    act.activation(pr[:, :, :], pr[:, :, :], ACT.Exp)
                    act.activation(lg[:, :, E], lg[:, :, E], ACT.Exp, scale=-1.0).then_inc(lexp_set, 1)
                elif part == 16:
                    act.wait_ge(cT_done, w + 1)
                    act.activation(cT[:, held(w)], bank(W_BANK)[0:2 * NR, 0:WT], ACT.Copy).then_inc(cT_set, 1)

            def high_piece(n):
                raw, hi, _ = piece(n)
                act.wait_ge(stage_in[n % STAGES], 16 * (n // STAGES + 1))
                act.activation(hi, raw, ACT.Copy).then_inc(piece_h, 1)

            def act_group(gi, first, last):
                for k in range(QUADS):
                    n = QUADS * gi + k
                    probs_out(n)
                    if k + 1 < QUADS or not last:
                        exponentials(n + 1, k + 1)
                    if k or not first:
                        outputs_high(n - 1, k - 1 + QUADS, NCH * gi + (k - 1) // BC)
                    if k + LEAD < QUADS or not last:
                        swap_halves(n + LEAD)
                    if k in WO_SLOTS:
                        j = WO_SLOTS.index(k)
                        wo_high(NP * gi + j, j, KT * NCH * gi)
                    if k in MW_SLOTS and not last:
                        j = MW_SLOTS.index(k)
                        mw_high(HG * gi + HG + j, j, QUADS * gi + QUADS - HG + j + 1)
                    if last:
                        if k < EARLY:
                            high_piece(k)
                        for part in QUAD_PARTS.get(k, ()):
                            act_part(0, part)

            act.wait_ge(wkv_ready, 1)
            over_groups(act, act_group)
            outputs_high(NG * QUADS - 1, QUADS - 1, NG * NCH - 1)

            for n, (w, part) in enumerate(BETWEEN):
                act_part(w, part)
                if EARLY + n < len(PIECES):
                    if n == 0:
                        act.wait_ge(y_added, KT * NG * NCH)
                    high_piece(EARLY + n)

            def act_chunk(c, waves):
                for f in range(FT):
                    w, n, free = fw(f), FT * c + f + 1, FT * c + max(f - 1, 0) + 1
                    act.wait_ge(gate_done, n + 1)
                    act.wait_ge(mix_done, free)
                    act.activation(act_s[0:w, f % 2, :], bank(G_BANK + f % 2)[0:w, :], ACT.Silu).then_inc(silu_done, 1)
                    if waves:
                        act_part(*wave_part(c, 2 * f))
                    if waves:
                        act_part(*wave_part(c, 2 * f + 1))
                    act.wait_ge(down_done, FT * c + max(f - 2, 0) + 1)
                    act.wait_ge(prod_done, n + 1)
                    act.activation(acth[0:w, f % 3, :], act_t[0:w, f % 2, :], ACT.Copy).then_inc(acth_set, 1)

            over_chunks(act, act_chunk)

        @block.tensor
        def _(pe):
            def mm(out, lhsT, rhs, start, stop, **kw):
                return pe.matmul(out, lhsT, rhs, start=start, stop=stop, **kw)

            def mm3(out, wh, wl, rh, rl, start=True, stop=True):
                mm(out, wh, rh, start, False)
                mm(out, wh, rl, False, False)
                return mm(out, wl, rh, False, stop)

            def mean_of(out, src):
                for k in range(KT):
                    last = mm(out, mean_w[:, :], src(k), k == 0, k == KT - 1)
                return last

            def absorb_queries(head, j, gi, projected, out=bank(MW_BANK)):
                pe.wait_ge(raw_m_in, 16 * (gi + 1))
                if not isinstance(gi, int) or gi > 0:
                    pe.wait_ge(mwl_set, head)
                now(pe, y_added, KT * projected)
                keys = raw_m[:, j, 128 + 2 * QR2:128 + 2 * QR2 + KVLR]
                for a in range(2):
                    last = mm(out[:, a * KVLR:(a + 1) * KVLR],
                              raw_m[:, j, 128 * a:128 * (a + 1)], keys, True, True)
                last.then_inc(mw_done, 1)

            def means(t):
                pe.wait_ge(x_in[t], 16)
                now(pe, pxn_done, t)
                mean_of(bank(NORM_BANK), lambda k: x[:, k, toks(t)]).then_inc(pmean_done, 1)

            def mean_squares(out, b, parts):
                for i, (src, w) in enumerate(parts):
                    last = mm(out[:, b:b + 1], src[:, b * S:(b + 1) * S], w, i == 0, i == len(parts) - 1)
                return last

            def variances_chunk(t):
                pe.wait_ge(psq_done, t + 1)
                for b in range(BC):
                    last = mean_squares(bank(NORM_BANK), b, [(sq[:, k, :], mean_w[:, 0:1]) for k in range(KT)])
                last.then_inc(pvar_done, 1)

            def latent_squares(t):
                now(pe, lstat_set, t)
                pe.wait_ge(ksquares_set, t + 1)
                pe.wait_ge(qsquares_set, t + 1)
                out = bank(LSTAT_BANK)[:, BC:]
                for b in range(BC):
                    mean_squares(out, b, [(sqp[:, 0, :], meanl_w[:, 0:1]), (sqp[0:QR2, 1, :], meanl_w[0:QR2, 0:1])])
                    last = mean_squares(out[:, BC:], b, [(sqp[0:KVLR, 2, :], meanl_w[0:KVLR, 1:2])])
                last.then_inc(lvar_done, 1)

            def spread_chunk(out, col):
                for b in range(BC):
                    last = mm(out[:, b * S:(b + 1) * S], prinv[:, col + b:col + b + 1].to_broadcast([128, 128]),
                              ident[:, :], True, True)
                return last

            def project(u, weights, i):
                for j in range(2):
                    for k in range(KT):
                        last = mm(bank(P_BANK + i + j), weights[:, k, 128 * j:128 * (j + 1)], xc[:, u % 2, k, :],
                                  k == 0, k == KT - 1)
                return last

            def spread_norm(t):
                pe.wait_ge(prinv_set, t + 1)
                spread_chunk(bank(NORM_BANK), 0).then_inc(pr_done, 1)

            pe.wait_ge(const_set, 1)
            means(0)
            variances_chunk(0)
            pe.wait_ge(ident_in, 16)
            spread_norm(0)
            pe.wait_ge(w_in, 16 * 5)
            for u in range(NCH + 2):
                if u + 1 < NCH:
                    means(u + 1)
                if u == NCH:
                    pe.wait_ge(raw_set, NCH)
                    for j in range(HG):
                        absorb_queries(j, j, 0, 0, bank(P_BANK + j))
                if u < NCH:
                    pe.wait_ge(pxn_done, u + 1)
                    now(pe, raw_set, u)
                    project(u, qaw, 0).then_inc(qproj_done, 1)
                if u >= 2:
                    t = u - 2
                    pe.wait_ge(ckn_set, t + 1)
                    pe.wait_ge(qn_set, t + 1)
                    for b in range(BC):
                        last = pe.transpose(bank(RQ_BANK)[:, b * KVLR:(b + 1) * KVLR], ckn[:, b * S:(b + 1) * S],
                                            ident[0:KVLR, 0:KVLR])
                    last.then_inc(ckvT_done, 1)
                if u + 1 < NCH:
                    variances_chunk(u + 1)
                if u < NCH:
                    project(u, kvw, 2).then_inc(kproj_done, 1)
                if 0 < u <= NCH:
                    pe.wait_ge(lrinv_set, u)
                    now(pe, ckv_set, u - 1)
                    spread_chunk(bank(RQ_BANK), BC).then_inc(qr_done, 1)
                    now(pe, ckn_set, u - 1)
                    spread_chunk(bank(RK_BANK), 2 * BC).then_inc(kr_done, 1)
                if u + 1 < NCH:
                    spread_norm(u + 1)
                if u < NCH:
                    latent_squares(u)

            def absorb_outputs(pair, j, gi, projected):
                pe.wait_ge(raw_v_in, 16 * (gi + 1))
                now(pe, wol_set, pair)
                now(pe, y_added, KT * projected)
                for a in range(2):
                    last = mm(bank(WO_BANK)[a * KVLR:(a + 1) * KVLR, 0:D], raw_v[:, 2 * j + a, 0:KVLR],
                              raw_v[:, 2 * j + a, KVLR:], True, True)
                last.then_inc(wo_done, 1)

            def queries(job, m, gi):
                c, j = m // HG % NCH, m % HG
                pe.wait_ge(mwl_set, HG * gi + j + 1)
                pe.wait_ge(rot_set, HG * gi + j + 1)
                now(pe, qcos_set, job)
                out = bank(Q_BANK)
                mm3(out, mwh[:, j, 0, :], mwl[:, j, 0, :], qn1h[:, toks(c)], qn1l[:, toks(c)], True, False)
                mm(out, mwh[:, j, 1, :], qn2[:, toks(c)], False, False)
                mm(out, mwl[0:QR2, j, 1, :], qn2[0:QR2, toks(c)], False, True).then_inc(qp_done, 1)

            def scores(n, m, jobs):
                par, b = m // BC % 2, m % BC
                key = bass.ds((m % QUADS) * S, S)
                now(pe, p_done, n - 1)
                pe.wait_ge(q_set, jobs)
                out = bank(S_BANK + m % 2)
                mm(out, identb[:, :], maskb[:, :].unsqueeze(1).to_broadcast([128, HG, S]), True, True)
                for j in range(HG):
                    part = out[:, j * S:(j + 1) * S]
                    last = mm(part, qa[:, par, j, b * S:(b + 1) * S], ka[:, key], False, True,
                              skip_group_check=True)
                last.then_inc(s_done, 1)

            def transpose_probs(n, m):
                pe.wait_ge(p_done, n + 1)
                now(pe, pT_set, n)
                for j in range(HG):
                    last = pe.transpose(bank(PT_BANK)[:, j * S:(j + 1) * S], p[:, m % 2, j, :], ident[:, :])
                last.then_inc(pT_done, 1)

            def weigh_values(n, m):
                pe.wait_ge(pT_set, n + 1)
                now(pe, o_done, n)
                for j in range(HG):
                    last = mm(bank(PV_BANK)[:, j * (KVLR + 1):(j + 1) * (KVLR + 1)], pT[:, j, :],
                              ckv[:, m % QUADS, :], True, True)
                last.then_inc(pv_done, 1)

            def transpose_outputs(n):
                pe.wait_ge(o_done, n + 1)
                now(pe, oTl_set, n)
                for a in range(NP):
                    last = pe.transpose(bank(OT_BANK)[:, a * S:(a + 1) * S],
                                        o[:, 2 * a:2 * a + 2, :].rearrange("p h c -> p (h c)"), ident[:, :])
                last.then_inc(oT_done, 1)

            def project_outputs(it, par, gi, heads, wave_read=None, wave_count=0):
                pe.wait_ge(oTl_set, BC * (it + 1))
                pe.wait_ge(wol_set, NP * (gi + 1))
                pe.wait_ge(mwl_set, heads)
                for m in range(KT):
                    now(pe, y_added, KT * (it - 1) + m + 1)
                    if wave_read is not None and m == W_BANK - Y_BANK:
                        pe.wait_ge(wave_read, wave_count)
                    cols = slice(128 * m, 128 * (m + 1))
                    for a in range(NP):
                        last = mm3(bank(Y_BANK + m), woh[:, a, cols], wol[:, a, cols], oTh[:, par, a, :],
                                   oTl[:, par, a, :], a == 0, a == NP - 1)
                    last.then_inc(y_done, 1)

            pe.wait_ge(ckv_set, NCH)
            pe.wait_ge(keys_set, NCH)
            pe.wait_ge(raw_set, NCH)
            pe.wait_ge(cast_set, 1)
            pe.wait_ge(mwl_set, HG)
            for job in range(LEAD):
                queries(job, job, 0)
            scores(0, 0, HG)

            def variances(w, i):
                pe.wait_ge(sq_done, 2 * w + i + 1)
                for b in range(WB):
                    for k in range(KT):
                        last = mm(bank(W_BANK)[:, b:b + 1], sqw[:, k, b * S:(b + 1) * S], mean_w[:, 0:1],
                                  k == 0, k == KT - 1)
                last.then_inc(var_done, 1)

            def spread(w, i):
                pe.wait_ge(rinv_set, 2 * w + i + 1)
                for b in range(WB):
                    last = mm(bank(W_BANK)[:, b * S:(b + 1) * S], rinv[:, b:b + 1].to_broadcast([128, 128]),
                              ident[:, :], True, True)
                last.then_inc(r_done, 1)

            def pe_part(w, part):
                if part in (0, 11):
                    if part == 0:
                        now(pe, cT_set, w)
                        if isinstance(w, int) and w == 0:
                            pe.wait_ge(y_added, KT * (NG - 1) * NCH + KT)
                    else:
                        pe.wait_ge(wkv_done, w + 1)
                    mean_of(bank(W_BANK)[:, 0:WT], lambda k: x[:, k, wtoks(w)]).then_inc(mean_done, 1)
                elif part in (1, 12):
                    variances(w, part // 12)
                elif part in (2, 13):
                    spread(w, part // 13)
                elif part == 14:
                    pe.wait_ge(xn_done, w + 1)
                    for b in range(WB):
                        for k in range(KT):
                            last = mm(bank(W_BANK)[:, b * NR:(b + 1) * NR], xw[:, k, b * S:(b + 1) * S], wr[:, k, :],
                                      k == 0, k == KT - 1)
                    last.then_inc(logit_done, 1)
                elif part == 16:
                    pe.wait_ge(cw_set, w + 1)
                    for b in range(WB):
                        last = pe.transpose(bank(W_BANK)[0:2 * NR, b * S:(b + 1) * S], f32(cwp[:, b, :]),
                                            ident[:, :])
                    last.then_inc(cT_done, 1)

            def pe_group(gi, first, last):
                for k in range(QUADS):
                    n = QUADS * gi + k
                    if k + 1 < QUADS or not last:
                        scores(n + 1, k + 1, n - k + (k + 1) // BC * HG + HG)
                    transpose_probs(n, k)
                    if k or not first:
                        transpose_outputs(n - 1)
                    if k % BC == 1 and (k > 1 or not first):
                        it = NCH * gi + k // BC - 1
                        absorbed = 0 if last else len([j for j in MW_SLOTS if j < k])
                        in_use = (kp_set, 1) if last and k > 8 else ()
                        project_outputs(it, (k // BC + 1) % 2, gi if k > 1 else gi - 1, HG * (gi + 1) + absorbed, *in_use)
                    if k + LEAD < QUADS or not last:
                        queries(n + LEAD, k + LEAD, gi + (k + LEAD) // QUADS)
                    weigh_values(n, k)
                    projected = NCH * gi + (k - 1) // BC
                    if k in WO_SLOTS:
                        j = WO_SLOTS.index(k)
                        absorb_outputs(NP * gi + j, j, gi, projected)
                    if k in MW_SLOTS and not last:
                        j = MW_SLOTS.index(k)
                        absorb_queries(HG * gi + HG + j, j, gi + 1, projected)
                    if last:
                        for part in QUAD_PARTS.get(k, ()):
                            pe_part(0, part)

            over_groups(pe, pe_group)
            transpose_outputs(NG * QUADS - 1)
            project_outputs(NG * NCH - 1, (NCH - 1) % 2, NG - 1, NH, stat_set, 2)

            pe.wait_ge(y_added, KT * NG * NCH)
            for w, part in BETWEEN:
                pe_part(w, part)

            for engine in range(2):
                pe.wait_ge(piece_l[engine], lows(len(PIECES), engine))
            pe.wait_ge(piece_h, len(PIECES))
            pe.wait_ge(sel_set, 1)

            def hidden(out, col, w, c, ks=range(KT)):
                now_c = bass.ds((c % 2) * CH, CH)
                for k in ks:
                    last = mm3(out, wguh[:, k, col:col + w], wgul[:, k, col:col + w], hh[:, k, now_c],
                               hl[:, k, now_c], k == 0, k == KT - 1)
                return last

            def share(f, c):
                mm(bank(C_BANK), sel[:, 128 * f:128 * (f + 1)], cT[:, bass.ds((c % 2) * CH, CH)], True, True
                   ).then_inc(share_done, 1)

            def down(n, f, share_free=None):
                w = fw(f)
                pe.wait_ge(actl_set, n + 1)
                for m in range(KT):
                    if m == KT - 1 and share_free is not None:
                        pe.wait_ge(prod_done, share_free)
                    cols = slice(128 * m, 128 * (m + 1))
                    last = mm3(bank(Z_BANK + m), wdh[0:w, f, cols], wdl[0:w, f, cols], acth[0:w, f % 3, :],
                               actl[0:w, f % 3, :], f == 0, f == FT - 1)
                last.then_inc(down_done, 1)

            def banks_free(n, f):
                pe.wait_ge(mix_done, n - f + max(f - 1, 0))

            def pe_chunk(c, waves):
                for f in range(FT):
                    w, n = fw(f), FT * c + f + 1
                    if f == 0:
                        pe.wait_ge(hl_set, WAVES * (c + 1))
                    if f < FT - 1:
                        banks_free(n, f)
                    up = bank(U_BANK + f % 2)[0:w, :]
                    hidden(bank(G_BANK + f % 2)[0:w, :], 128 * f, w, c).then_inc(gate_done, 1)
                    hidden(up, FF + 128 * f, w, c, range(1))
                    if waves:
                        pe_part(*wave_part(c, 2 * f))
                    if f < 2:
                        pe.wait_ge(prod_done, n)
                    hidden(up, FF + 128 * f, w, c, range(1, KT)).then_inc(up_done, 1)
                    if f == FT - 2:
                        banks_free(n + 1, f + 1)
                    if f == 2:
                        pe.wait_ge(z_added, KT * c + 1)
                    if f == 0:
                        pe.wait_ge(cT_set, WAVES * (c + 1))
                    if f >= 2:
                        down(n - 2, f - 2, n)
                    if waves:
                        pe_part(*wave_part(c, 2 * f + 1))
                    share(f, c)
                    if f == FT - 1:
                        down(n - 1, f - 1)
                down(FT * (c + 1), FT - 1)

            over_chunks(pe, pe_chunk)


def _tables():
    inv = (1.0 / np.float32(10000.0) ** (np.arange(0, DR, 2, dtype=np.float32) / np.float32(DR))).astype(np.float32)
    ang = np.arange(S, dtype=np.float32)[None, :] * inv[:, None]
    cos, sin, one = np.cos(ang), np.sin(ang), np.ones((DR, S), np.float32)
    sc = np.float32(SCALE)
    rope = np.stack([np.concatenate([one, cos, cos]), np.concatenate([one, -sin, sin]),
                     np.concatenate([one, cos * sc, cos * sc]), np.concatenate([one, -sin * sc, sin * sc])], 1)
    expert = np.concatenate([np.repeat(np.arange(E), FE), np.full(FS, E), np.full(FT * 128 - FF, -1)])
    sel = (np.arange(2 * NR)[:, None] % NR == expert[None, :]).astype(np.float32)
    pos = np.arange(S)
    mask = np.where(pos[None, :] > pos[:, None], np.float32(NEG), np.float32(0)).astype(np.float32)
    order = np.arange(E)
    low = np.broadcast_to((order[None, :] < order[:, None]).astype(np.float32), (128, E, E))
    return (rope.astype(np.float32), mask, np.eye(128, dtype=np.float32), low, sel)


def kernel(x, ctx_2048, L0_attn_q_a_w, L0_attn_q_a_ln_w, L0_attn_q_b_w, L0_attn_kv_a_w, L0_attn_kv_a_ln_w,
           L0_attn_kv_b_w, L0_attn_o_w, L0_xattn_time_decay, L0_xattn_time_first, L0_ffn_Wr, L0_ffn_Wg,
           L0_ffn_Wu, L0_ffn_Wd, L0_ffn_Sg, L0_ffn_Su, L0_ffn_Sd, L0_ffn_Wsg):
    import concourse.bacc as bacc
    from concourse.bass_utils import run_bass_kernel_spmd

    def feature_major(a):
        return np.asarray(a).reshape(TOK, KT, 128).transpose(2, 1, 0)

    def columns(a):
        return np.asarray(a).reshape(KT, 128, -1).transpose(1, 0, 2)

    qa, qln, qb = (np.asarray(a) for a in (L0_attn_q_a_w, L0_attn_q_a_ln_w, L0_attn_q_b_w))
    kva, kvb, ow = (np.asarray(a) for a in (L0_attn_kv_a_w, L0_attn_kv_b_w, L0_attn_o_w))
    rot = kva[:, KVLR:]
    swapped = np.concatenate([rot[:, DR // 2:], rot[:, :DR // 2]], 1)
    qb = qb.reshape(QLR, NH, DN + DR)
    kvb = kvb.reshape(KVLR, NH, DN + DV)
    twice = np.concatenate([np.arange(128), np.arange(128, QLR), np.arange(128, QLR)])
    m = np.concatenate([qb[twice, :, :DN].transpose(2, 1, 0), kvb[:, :, :DN].transpose(2, 1, 0),
                        qb[:128, :, DN:], qb[twice[128:], :, DN:]], 2)
    vo = np.concatenate([kvb[:, :, DN:].transpose(2, 1, 0), ow.reshape(NH, DV, D).transpose(1, 0, 2)], 2)

    def by_group(a):
        return a.reshape(128, NG, -1).transpose(1, 0, 2)

    def experts(w, shared):
        return np.concatenate([np.asarray(w).transpose(1, 0, 2).reshape(D, E * FE), np.asarray(shared)], 1)

    rope, mask, ident, low, sel = _tables()
    given = [
        ("xT", feature_major(x)), ("ctx", feature_major(ctx_2048)),
        ("td", np.asarray(L0_xattn_time_decay).reshape(KT, 128).T),
        ("tf", np.asarray(L0_xattn_time_first).reshape(KT, 128).T),
        ("qaw", columns(qa[:, twice])), ("qaln", qln[twice].reshape(2, 128).T),
        ("kvw", columns(np.concatenate([kva, swapped, swapped], 1))),
        ("kvln", np.asarray(L0_attn_kv_a_ln_w).reshape(KVLR, 1)),
        ("head", np.concatenate([by_group(m), by_group(vo)], 2)),
        ("wr", columns(np.concatenate([np.asarray(L0_ffn_Wr), np.asarray(L0_ffn_Wsg)], 1))),
        ("wgu", np.concatenate([experts(L0_ffn_Wg, L0_ffn_Sg), experts(L0_ffn_Wu, L0_ffn_Su)], 1)),
        ("wd", np.concatenate([np.asarray(L0_ffn_Wd).reshape(E * FE, D), np.asarray(L0_ffn_Sd)], 0)),
        ("rope", rope), ("mask", mask), ("ident", ident), ("low", low), ("sel", sel),
    ]
    nc = bacc.Bacc("TRN2", target_bir_lowering=False, num_devices=1)
    arrays, args = {}, []
    for name, a in given:
        a = np.ascontiguousarray(a)
        arrays["in_" + name] = a
        args.append(nc.dram_tensor("in_" + name, a.shape, mybir.dt.from_np(a.dtype), kind="ExternalInput").ap())
    args.append(nc.dram_tensor("out", (128, KT, TOK), F32, kind="ExternalOutput").ap())
    decoder_program(nc, *args)
    r = run_bass_kernel_spmd(nc, [arrays], core_ids=[0])
    return np.ascontiguousarray(r.results[0]["out"].transpose(2, 1, 0)).reshape(B, S, D)
```
